# Optimizing a Trainium2 kernel written in Bass

```python
import numpy as np
import jax
import jax.numpy as jnp

def _softmax(x, axis=-1):
    return jax.nn.softmax(x, axis=axis)

def _gelu(x):
    return jax.nn.gelu(x, approximate=True)

def _silu(x):
    return jax.nn.silu(x)

def _sigmoid(x):
    return jax.nn.sigmoid(x)

def _layernorm(x, axis=-1, eps=1e-05):
    m = jnp.mean(x, axis=axis, keepdims=True)
    v = jnp.var(x, axis=axis, keepdims=True)
    return (x - m) / jnp.sqrt(v + eps)

def _scatter_add(tgt, idx, src, axis=0):
    return tgt.at[idx].add(src)

def _segment_sum(src, seg, n):
    return jax.ops.segment_sum(src, seg, n)
kernel_name = 'mk_xattn_ffn_d2_seqx_r8_18048e'

def setup_inputs(seed: int=0):
    np.random.seed(seed)
    _w = jnp.asarray

    def _rec_inputs():
        import jax
        import jax.numpy as jnp
        _rk = jax.random.key(seed)
        x = 0.0002417 + 0.9998 * jax.random.normal(jax.random.fold_in(_rk, 1), (64, 128, 128), jnp.float32)
        _lenS = 128 - jax.random.randint(jax.random.fold_in(_rk, 7), (64,), 0, max(1, 128 // 4) + 1, jnp.int32)
        _lenS2 = 77 - jax.random.randint(jax.random.fold_in(_rk, 8), (64,), 0, max(1, 77 // 4) + 1, jnp.int32)
        _ctx_1024P = jax.random.normal(jax.random.fold_in(_rk, 11), (64, 16, 128), jnp.float32)
        _ctx_1024c = jax.random.dirichlet(jax.random.fold_in(_rk, 511), 0.3 * jnp.ones((16,), jnp.float32), (64, 77))
        _ctx_1024t = jnp.einsum('bsk,bkd->bsd', _ctx_1024c, _ctx_1024P)
        _ctx_1024t = _ctx_1024t * jax.lax.rsqrt(jnp.mean(jnp.square(_ctx_1024t)) + 1e-12) * 0.953939
        ctx_1024 = 7.22013e-05 + 1.00017 * (_ctx_1024t + 0.3 * jax.random.normal(jax.random.fold_in(_rk, 611), (64, 77, 128), jnp.float32))
        _validS = jnp.arange(128)[None, :] < _lenS[:, None]
        _validS2 = jnp.arange(77)[None, :] < _lenS2[:, None]
        _causal = jnp.tril(jnp.ones((128, 128), dtype=bool))
        mask_Bx1xSxS2_ik1 = jnp.where(jnp.broadcast_to(_validS2[:, None, None, :], (64, 1, 128, 77)), 1, 0).astype(jnp.int32)
        return (x, ctx_1024, mask_Bx1xSxS2_ik1)
    x, ctx_1024, mask_Bx1xSxS2_ik1 = _rec_inputs()

    def _L0_xattn_setup():
        import jax, jax.numpy as jnp
        import numpy as np
        HEADS = 16
        EMBED = 128
        HEAD_DIM = EMBED // HEADS
        key = jax.random.key(seed)
        ks = jax.random.split(key, 6)
        N, S, E = (4, 256, EMBED)
        return {'value': jax.random.normal(ks[0], (N, S, E), dtype=jnp.float32), 'key': jax.random.normal(ks[1], (N, S, E), dtype=jnp.float32), 'query': jax.random.normal(ks[2], (N, S, E), dtype=jnp.float32), 'mask': jax.random.randint(ks[3], (N, 1, S, S), 0, 2, dtype=jnp.int32), 'w_out': jax.random.normal(ks[4], (E, E), dtype=jnp.float32) * E ** (-0.5), 'b_out': jax.random.normal(ks[5], (E,), dtype=jnp.float32) * 0.01}
    _L0_xattn_all = _L0_xattn_setup()
    _L0_xattn_in = {k: v for k, v in _L0_xattn_all.items() if k in ('w_out', 'b_out')}
    del _L0_xattn_all

    def _L0_ffn_setup():
        import jax, jax.numpy as jnp
        import numpy as np
        E = 16
        G = 4
        EPG = E // G
        K = 4
        TOPK_GROUP = 2
        PER_GROUP_K = K // TOPK_GROUP

        def _route(xf, router_w, correction_bias):
            S = xf.shape[0]
            logits = xf @ router_w.T
            scores = jax.nn.sigmoid(logits)
            sb = scores + correction_bias
            grp_top = jax.lax.top_k(sb.reshape(S, G, EPG), PER_GROUP_K)[0]
            group_scores = grp_top.sum(axis=-1)
            _, group_idx = jax.lax.top_k(group_scores, TOPK_GROUP)
            group_mask = jnp.zeros((S, G), sb.dtype).at[jnp.arange(S)[:, None], group_idx].set(1.0)
            score_mask = jnp.broadcast_to(group_mask[:, :, None], (S, G, EPG)).reshape(S, E)
            masked = jnp.where(score_mask > 0, sb, -jnp.inf)
            _, topk_idx = jax.lax.top_k(masked, K)
            w = jnp.take_along_axis(scores, topk_idx, axis=1)
            w = w / (w.sum(axis=-1, keepdims=True) + 1e-20)
            return (topk_idx, w, scores)
        key = jax.random.key(seed)
        ks = jax.random.split(key, 9)
        B, T, C, H, HS = (2, 128, 128, 32, 256)
        std = 0.02
        return {'x': jax.random.normal(ks[0], (B, T, C), jnp.float32), 'router_w': jax.random.normal(ks[1], (E, C), jnp.float32) * std, 'correction_bias': jnp.zeros((E,), jnp.float32), 'gate_w': jax.random.normal(ks[2], (E, C, H), jnp.float32) * std, 'up_w': jax.random.normal(ks[3], (E, C, H), jnp.float32) * std, 'down_w': jax.random.normal(ks[4], (E, H, C), jnp.float32) * std, 'shared_gate_w': jax.random.normal(ks[5], (HS, C), jnp.float32) * std, 'shared_up_w': jax.random.normal(ks[6], (HS, C), jnp.float32) * std, 'shared_down_w': jax.random.normal(ks[7], (C, HS), jnp.float32) * std}
    _L0_ffn_all = _L0_ffn_setup()
    _L0_ffn_in = {k: v for k, v in _L0_ffn_all.items() if k in ('router_w', 'correction_bias', 'gate_w', 'up_w', 'down_w', 'shared_gate_w', 'shared_up_w', 'shared_down_w')}
    del _L0_ffn_all

    def _L1_xattn_setup():
        import jax, jax.numpy as jnp
        import numpy as np
        EPS = 1e-05

        def layer_norm(x, g, b):
            mu = jnp.mean(x, axis=-1, keepdims=True)
            var = jnp.var(x, axis=-1, keepdims=True)
            return (x - mu) * jax.lax.rsqrt(var + EPS) * g + b
        key = jax.random.key(seed)
        ks = jax.random.split(key, 8)
        dim, heads, dim_head = (128, 16, 64)
        inner = heads * dim_head
        b, n, m = (8, 512, 64)
        s = dim ** (-0.5)
        return {'x': jax.random.normal(ks[0], (b, n, dim), jnp.float32), 'latents': jax.random.normal(ks[1], (b, m, dim), jnp.float32), 'ln_m_g': jnp.ones((dim,), jnp.float32), 'ln_m_b': jnp.zeros((dim,), jnp.float32), 'ln_l_g': jnp.ones((dim,), jnp.float32), 'ln_l_b': jnp.zeros((dim,), jnp.float32), 'Wq': jax.random.normal(ks[2], (dim, inner), jnp.float32) * s, 'Wkv': jax.random.normal(ks[3], (dim, 2 * inner), jnp.float32) * s, 'Wout': jax.random.normal(ks[4], (inner, dim), jnp.float32) * s}
    _L1_xattn_all = _L1_xattn_setup()
    _L1_xattn_in = {k: v for k, v in _L1_xattn_all.items() if k in ('ln_m_g', 'ln_m_b', 'ln_l_g', 'ln_l_b', 'Wq', 'Wkv', 'Wout')}
    del _L1_xattn_all

    def _L1_ffn_setup():
        import jax, jax.numpy as jnp
        import numpy as np
        BLOCK = 32
        W_BITS = 4
        ACT_BITS = 16

        def act_qdq(x):
            qmax = 2.0 ** (ACT_BITS - 1) - 1.0
            scale = jnp.maximum(jnp.max(jnp.abs(x)) / qmax, 1e-12)
            return jnp.clip(jnp.round(x / scale), -qmax - 1.0, qmax) * scale

        def fixed_qdq_u16(x):
            scale = 1.0 / 65536.0
            return jnp.clip(jnp.round(x / scale), 0.0, 65535.0) * scale

        def lpbq_dequant(w):
            O, I = w.shape
            qmax = 2.0 ** (W_BITS - 1) - 1.0
            wb = w.reshape(O, I // BLOCK, BLOCK)
            s = jnp.maximum(jnp.max(jnp.abs(wb), axis=-1, keepdims=True) / qmax, 1e-12)
            wq = jnp.clip(jnp.round(wb / s), -qmax - 1.0, qmax) * s
            return wq.reshape(O, I)
        key = jax.random.key(seed)
        k1, k2, k3, k4 = jax.random.split(key, 4)
        B, S, H, I = (2, 512, 128, 384)
        x = jax.random.normal(k1, (B, S, H), jnp.float32)
        w_gate = jax.random.normal(k2, (I, H), jnp.float32) * 0.02
        w_up = jax.random.normal(k3, (I, H), jnp.float32) * 0.02
        w_down = jax.random.normal(k4, (H, I), jnp.float32) * 0.02
        return {'x': x, 'w_gate': w_gate, 'w_up': w_up, 'w_down': w_down}
    _L1_ffn_all = _L1_ffn_setup()
    _L1_ffn_in = {k: v for k, v in _L1_ffn_all.items() if k in ('w_gate', 'w_up', 'w_down')}
    del _L1_ffn_all
    return {'x': x, 'ctx_1024': ctx_1024, 'mask_Bx1xSxS2_ik1': mask_Bx1xSxS2_ik1, 'L0_xattn_w_out': _L0_xattn_in['w_out'], 'L0_xattn_b_out': _L0_xattn_in['b_out'], 'L0_ffn_router_w': _L0_ffn_in['router_w'], 'L0_ffn_correction_bias': _L0_ffn_in['correction_bias'], 'L0_ffn_gate_w': _L0_ffn_in['gate_w'], 'L0_ffn_up_w': _L0_ffn_in['up_w'], 'L0_ffn_down_w': _L0_ffn_in['down_w'], 'L0_ffn_shared_gate_w': _L0_ffn_in['shared_gate_w'], 'L0_ffn_shared_up_w': _L0_ffn_in['shared_up_w'], 'L0_ffn_shared_down_w': _L0_ffn_in['shared_down_w'], 'L1_xattn_ln_m_g': _L1_xattn_in['ln_m_g'], 'L1_xattn_ln_m_b': _L1_xattn_in['ln_m_b'], 'L1_xattn_ln_l_g': _L1_xattn_in['ln_l_g'], 'L1_xattn_ln_l_b': _L1_xattn_in['ln_l_b'], 'L1_xattn_Wq': _L1_xattn_in['Wq'], 'L1_xattn_Wkv': _L1_xattn_in['Wkv'], 'L1_xattn_Wout': _L1_xattn_in['Wout'], 'L1_ffn_w_gate': _L1_ffn_in['w_gate'], 'L1_ffn_w_up': _L1_ffn_in['w_up'], 'L1_ffn_w_down': _L1_ffn_in['w_down']}

def reference(x, ctx_1024, mask_Bx1xSxS2_ik1, L0_xattn_w_out, L0_xattn_b_out, L0_ffn_router_w, L0_ffn_correction_bias, L0_ffn_gate_w, L0_ffn_up_w, L0_ffn_down_w, L0_ffn_shared_gate_w, L0_ffn_shared_up_w, L0_ffn_shared_down_w, L1_xattn_ln_m_g, L1_xattn_ln_m_b, L1_xattn_ln_l_g, L1_xattn_ln_l_b, L1_xattn_Wq, L1_xattn_Wkv, L1_xattn_Wout, L1_ffn_w_gate, L1_ffn_w_up, L1_ffn_w_down):
    import jax
    import jax.numpy as jnp

    def _L0_xattn_ref(value, key, query, mask, w_out, b_out):
        import jax, jax.numpy as jnp
        import numpy as np
        HEADS = 16
        EMBED = 128
        HEAD_DIM = EMBED // HEADS
        N, Q, E = query.shape
        K = key.shape[1]
        H, D = (HEADS, HEAD_DIM)
        q = query.reshape(N, Q, H, D)
        k = key.reshape(N, K, H, D)
        v = value.reshape(N, K, H, D)
        energy = jnp.einsum('nqhd,nkhd->nhqk', q, k)
        energy = jnp.where(mask == 0, jnp.float32(-1e+22), energy)
        attn = jax.nn.softmax(energy / jnp.sqrt(jnp.float32(E)), axis=-1)
        out = jnp.einsum('nhqk,nkhd->nqhd', attn, v).reshape(N, Q, H * D)
        return out @ w_out.T + b_out

    def _L0_ffn_ref(x, router_w, correction_bias, gate_w, up_w, down_w, shared_gate_w, shared_up_w, shared_down_w):
        import jax, jax.numpy as jnp
        import numpy as np
        E = 16
        G = 4
        EPG = E // G
        K = 4
        TOPK_GROUP = 2
        PER_GROUP_K = K // TOPK_GROUP

        def _route(xf, router_w, correction_bias):
            S = xf.shape[0]
            logits = xf @ router_w.T
            scores = jax.nn.sigmoid(logits)
            sb = scores + correction_bias
            grp_top = jax.lax.top_k(sb.reshape(S, G, EPG), PER_GROUP_K)[0]
            group_scores = grp_top.sum(axis=-1)
            _, group_idx = jax.lax.top_k(group_scores, TOPK_GROUP)
            group_mask = jnp.zeros((S, G), sb.dtype).at[jnp.arange(S)[:, None], group_idx].set(1.0)
            score_mask = jnp.broadcast_to(group_mask[:, :, None], (S, G, EPG)).reshape(S, E)
            masked = jnp.where(score_mask > 0, sb, -jnp.inf)
            _, topk_idx = jax.lax.top_k(masked, K)
            w = jnp.take_along_axis(scores, topk_idx, axis=1)
            w = w / (w.sum(axis=-1, keepdims=True) + 1e-20)
            return (topk_idx, w, scores)
        B, T, C = x.shape
        S = B * T
        xf = x.reshape(S, C)
        sg = xf @ shared_gate_w.T
        su = xf @ shared_up_w.T
        shared_out = jax.nn.silu(sg) * su @ shared_down_w.T
        topk_idx, w, _scores = _route(xf, router_w, correction_bias)
        combine = jnp.zeros((S, E), xf.dtype).at[jnp.arange(S)[:, None], topk_idx].add(w)
        g = jnp.einsum('sc,ech->esh', xf, gate_w)
        u = jnp.einsum('sc,ech->esh', xf, up_w)
        h = jax.nn.silu(g) * u
        hw = h * combine.T[:, :, None]
        routed = jnp.einsum('esh,ehc->sc', hw, down_w)
        return (shared_out + routed).reshape(B, T, C)

    def _L1_xattn_ref(x, latents, ln_m_g, ln_m_b, ln_l_g, ln_l_b, Wq, Wkv, Wout):
        import jax, jax.numpy as jnp
        import numpy as np
        EPS = 1e-05

        def layer_norm(x, g, b):
            mu = jnp.mean(x, axis=-1, keepdims=True)
            var = jnp.var(x, axis=-1, keepdims=True)
            return (x - mu) * jax.lax.rsqrt(var + EPS) * g + b
        heads, dim_head = (16, 64)
        scale = dim_head ** (-0.5)
        x = layer_norm(x, ln_m_g, ln_m_b)
        lat = layer_norm(latents, ln_l_g, ln_l_b)
        b, m, _ = lat.shape
        q = lat @ Wq
        kv_input = jnp.concatenate([x, lat], axis=1)
        kv = kv_input @ Wkv
        k, v = jnp.split(kv, 2, axis=-1)

        def split_heads(t):
            return t.reshape(t.shape[0], t.shape[1], heads, dim_head).transpose(0, 2, 1, 3)
        q, k, v = (split_heads(q), split_heads(k), split_heads(v))
        dots = jnp.einsum('bhid,bhjd->bhij', q, k) * scale
        attn = jax.nn.softmax(dots, axis=-1)
        out = jnp.einsum('bhij,bhjd->bhid', attn, v)
        out = out.transpose(0, 2, 1, 3).reshape(b, m, heads * dim_head)
        return out @ Wout

    def _L1_ffn_ref(x, w_gate, w_up, w_down):
        import jax, jax.numpy as jnp
        import numpy as np
        BLOCK = 32
        W_BITS = 4
        ACT_BITS = 16

        def act_qdq(x):
            qmax = 2.0 ** (ACT_BITS - 1) - 1.0
            scale = jnp.maximum(jnp.max(jnp.abs(x)) / qmax, 1e-12)
            return jnp.clip(jnp.round(x / scale), -qmax - 1.0, qmax) * scale

        def fixed_qdq_u16(x):
            scale = 1.0 / 65536.0
            return jnp.clip(jnp.round(x / scale), 0.0, 65535.0) * scale

        def lpbq_dequant(w):
            O, I = w.shape
            qmax = 2.0 ** (W_BITS - 1) - 1.0
            wb = w.reshape(O, I // BLOCK, BLOCK)
            s = jnp.maximum(jnp.max(jnp.abs(wb), axis=-1, keepdims=True) / qmax, 1e-12)
            wq = jnp.clip(jnp.round(wb / s), -qmax - 1.0, qmax) * s
            return wq.reshape(O, I)
        x = act_qdq(x)
        up = act_qdq(x @ lpbq_dequant(w_up).T)
        gate = act_qdq(x @ lpbq_dequant(w_gate).T)
        sig = fixed_qdq_u16(jax.nn.sigmoid(gate))
        gate = act_qdq(gate * sig)
        o = act_qdq(gate * up)
        return o @ lpbq_dequant(w_down).T
    x = x + _L0_xattn_ref(ctx_1024, ctx_1024, _layernorm(x, axis=-1), mask_Bx1xSxS2_ik1, L0_xattn_w_out, L0_xattn_b_out)
    x = x + _L0_ffn_ref(_layernorm(x, axis=-1), L0_ffn_router_w, L0_ffn_correction_bias, L0_ffn_gate_w, L0_ffn_up_w, L0_ffn_down_w, L0_ffn_shared_gate_w, L0_ffn_shared_up_w, L0_ffn_shared_down_w)
    x = x + _L1_xattn_ref(ctx_1024, _layernorm(x, axis=-1), L1_xattn_ln_m_g, L1_xattn_ln_m_b, L1_xattn_ln_l_g, L1_xattn_ln_l_b, L1_xattn_Wq, L1_xattn_Wkv, L1_xattn_Wout)
    x = x + _L1_ffn_ref(_layernorm(x, axis=-1), L1_ffn_w_gate, L1_ffn_w_up, L1_ffn_w_down)
    return x

_drawn_inputs = setup_inputs


def setup_inputs(seed=0):
    import zlib

    import numpy as np

    out = dict(_drawn_inputs(seed))
    spreads = {'L0_ffn_correction_bias': (0.0, 0.8),
     'L1_xattn_ln_m_g': (1.0, 0.2),
     'L1_xattn_ln_m_b': (0.0, 0.308),
     'L1_xattn_ln_l_g': (1.0, 0.2),
     'L1_xattn_ln_l_b': (0.0, 0.1)}
    factors = {'L0_xattn_b_out': 4.049,
     'L0_ffn_router_w': 8.0,
     'L0_ffn_gate_w': 8.0,
     'L0_ffn_up_w': 8.0,
     'L0_ffn_down_w': 8.0,
     'L0_ffn_shared_gate_w': 8.0,
     'L0_ffn_shared_up_w': 8.0,
     'L0_ffn_shared_down_w': 8.0,
     'L1_ffn_w_gate': 8.0,
     'L1_ffn_w_up': 8.0,
     'L1_ffn_w_down': 8.0}
    for name, (base, spread) in spreads.items():
        noise = np.random.default_rng([zlib.crc32(name.encode()), seed]).standard_normal(out[name].shape)
        drawn = base * np.exp(spread * noise) if base else spread * noise
        out[name] = jnp.asarray(drawn.astype(out[name].dtype))
    for name, factor in factors.items():
        out[name] = (out[name] * factor).astype(out[name].dtype)
    return out
```

```python
from contextlib import ExitStack

import numpy as np
import concourse.bass as bass
from concourse import mybir

F32 = mybir.dt.float32
F32R = mybir.dt.float32r
BF16 = mybir.dt.bfloat16
I32 = mybir.dt.int32
I16 = mybir.dt.int16
ALU = mybir.AluOpType
ACT = mybir.ActivationFunctionType
AX = mybir.AxisListType
RMAX = bass.bass_isa.ReduceOp.max

P = 128
EPS = 1e-5
MASKED = -(2.0 ** 73)
ROUND = 1.5 * 2.0 ** 23


def wait(eng, sem, value):
    if not isinstance(value, int) or value > 0:
        eng.wait_ge(sem, value)


def three_products(pe, out, a, b, start, stop):
    pe.matmul(out, a[0], b[0], start=start, stop=False)
    pe.matmul(out, a[0], b[1], start=False, stop=False)
    return pe.matmul(out, a[1], b[0], start=False, stop=stop)


def pipelined(eng, n, step):
    step(None, 0, 1)
    if n > 2:
        with eng.Fori(0, (n - 2) // 2) as i:
            step(2 * i, 2 * i + 1, 0)
            step(2 * i + 1, 2 * i + 2, 1)
    step(n - 2, n - 1, 0)
    step(n - 1, None, 1)


def pipelined_deep(eng, n, step):
    step(None, None, 0, 1, 1)
    step(None, 0, 1, 2, 0)
    step(0, 1, 2, 3, 1)
    with eng.Fori(1, n // 2 - 1) as i:
        step(2 * i - 1, 2 * i, 2 * i + 1, 2 * i + 2, 0)
        step(2 * i, 2 * i + 1, 2 * i + 2, 2 * i + 3, 1)
    step(n - 3, n - 2, n - 1, None, 0)
    step(n - 2, n - 1, None, None, 1)
    step(n - 1, None, None, None, 0)


class Core:

    def __init__(self, nc, stack):
        self.nc, self.stack = nc, stack

    def sb(self, name, shape, dt):
        return self.stack.enter_context(self.nc.sbuf_tensor(name, shape, dt))

    def sem(self, name):
        return self.stack.enter_context(self.nc.semaphore(name))


def load_and_prepare(nc, top, dram, T, bank):
    NB = T["batches"]
    with ExitStack() as stack:
        core = Core(nc, stack)
        wq = core.sb("wq_by_dim", [64, 16, P], F32)
        wk = core.sb("wk_by_dim", [64, 16, P], F32)
        wv = core.sb("wv_raw", [P, 1024], F32)
        gu = core.sb("gate_up_raw", [P, 2, 6, P], F32)
        x_in = core.sem("x_in")
        w_in = core.sem("weights_in")
        wv_hi = core.sem("wv_hi_done")
        gu_hi = core.sem("gate_up_hi_done")
        qk_done = core.sem("qk_products_done")
        qk_kept = core.sem("qk_products_kept")
        zeroed = core.sem("zeroed")
        prepared = core.sem("prepared")

        weights = [(T["ident"], dram["ident"]), (T["headmask"], dram["headmask"]), (T["groupmask"], dram["groupmask"]),
                   (T["tri"], dram["tri"]), (T["expert_rows"], dram["expert_rows"]), (T["blockstart"], dram["blockstart"]),
                   (wq, dram["wq"].rearrange("(h d) c -> d h c", d=64)), (wk, dram["wk"].rearrange("(h d) c -> d h c", d=64)),
                   (wv, dram["wv"]), (gu, dram["gate_up"].rearrange("c (s j h) -> c s j h", s=2, j=6)),
                   (T["down"], dram["down"].rearrange("(j h) c -> h j c", h=P)), (T["router"], dram["router"]),
                   (T["w_out0"], dram["w_out0"]), (T["w_out1"], dram["w_out1"].rearrange("(j d) c -> d j c", d=P)),
                   (T["bout_row"][0:1, :], dram["b_out0"].unsqueeze(0)),
                   (T["router_bias"], dram["router_bias"].partition_broadcast(P)),
                   (T["ln_cols"], dram["ln_cols"])]

        block = stack.enter_context(nc.Block())

        @block.sync
        def _(sp):
            q = NB // 4
            for k in range(4):
                sp.dma_start(T["x"][:, k * q:(k + 1) * q, :],
                             dram["x"][k * q:(k + 1) * q].rearrange("b t c -> t b c")).then_inc(x_in, 16)

        @block.scalar
        def _(act):
            act.wait_ge(zeroed, 1)
            for dst, src in weights:
                act.dma_start(dst[tuple(slice(None) for _ in dst.shape)], src).then_inc(w_in, 16)
            act.wait_ge(w_in, 16 * len(weights))
            nc.scalar.copy(T["wv"][0][:, :], wv[:, :]).then_inc(wv_hi, 1)
            nc.scalar.copy(T["gate_up"][0][:, :, :, :], gu[:, :, :, :]).then_inc(gu_hi, 1)
            for k in range(4):
                act.wait_ge(qk_done, k + 1)
                nc.scalar.copy(T["m"][:, 4 * k:4 * k + 4, :], bank[k][:, :].rearrange("p (h c) -> p h c", h=4)).then_inc(qk_kept, 1)
            act.wait_ge(prepared, 1)

        @block.tensor
        def _(pe):
            pe.wait_ge(w_in, 16 * len(weights))
            for h in range(16):
                mm = pe.matmul(bank[h // 4][:, (h % 4) * P:(h % 4 + 1) * P], wq[:, h, :], wk[:, h, :], start=True, stop=True)
                if h % 4 == 3:
                    mm.then_inc(qk_done, 1)

        @block.gpsimd
        def _(pool):
            nc.gpsimd.memset(T["bout_row"][:, :], 0.0).then_inc(zeroed, 1)

        @block.vector
        def _(dve):
            dve.wait_ge(w_in, 16 * len(weights))
            nc.vector.tensor_copy(T["identb"][:, :], T["ident"][:, :])
            nc.vector.tensor_copy(T["onerow"][:, :, :], T["ident"][:, 0:16].unsqueeze(2).to_broadcast([P, 16, P]))
            nc.vector.tensor_copy(T["onerow_f"][:, :], T["ident"][:, 0:1].to_broadcast([P, P]))
            dve.wait_ge(wv_hi, 1)
            nc.vector.tensor_tensor(T["wv"][1][:, :], wv[:, :], T["wv"][0][:, :].bitcast(F32), ALU.subtract)
            dve.wait_ge(gu_hi, 1)
            nc.vector.tensor_tensor(T["gate_up"][1][:, :, :, :], gu[:, :, :, :], T["gate_up"][0][:, :, :, :].bitcast(F32),
                                    ALU.subtract).then_inc(prepared, 1)
            dve.wait_ge(x_in, 64)
            with dve.Fori(0, NB) as b:
                nc.vector.bn_stats(T["x_stats"][:, b, :], T["x"][:, b, :])


def row_scales(nc, name, jobs):
    with ExitStack() as stack:
        core = Core(nc, stack)
        n = jobs[0][1].shape[1]
        mean_gap = core.sb(name + "_mean_gap", [P, n], F32)
        var = core.sb(name + "_var", [P, n], F32)
        root = core.sb(name + "_root", [P, n], F32)
        first = core.sb(name + "_first", [P, n], F32)
        step = core.sem(name + "_vector_step")
        var_ready = core.sem(name + "_var_ready")
        rooted = core.sem(name + "_rooted")
        block = stack.enter_context(nc.Block())

        @block.vector
        def _(dve):
            steps, roots = 0, 0

            def then(instruction):
                nonlocal steps
                instruction.then_inc(step, 1)
                steps += 1
                dve.wait_ge(step, steps)

            for stats, mean, rstd, p, twice in jobs:
                gap, v, r, f, m = mean_gap[0:p, :], var[0:p, :], root[0:p, :], first[0:p, :], mean[0:p, :, 0]
                then(nc.vector.tensor_tensor(gap, stats[0:p, :, 1], stats[0:p, :, 4], ALU.subtract))
                then(nc.vector.tensor_tensor(gap, gap, gap, ALU.mult))
                then(nc.vector.tensor_tensor(m, stats[0:p, :, 1], stats[0:p, :, 4], ALU.add))
                then(nc.vector.tensor_scalar(m, m, 0.5, None, ALU.mult))
                then(nc.vector.tensor_tensor(v, stats[0:p, :, 2], stats[0:p, :, 5], ALU.add))
                then(nc.vector.tensor_scalar(gap, gap, 0.25, EPS, ALU.mult, ALU.add))
                then(nc.vector.scalar_tensor_tensor(v, v, 1.0 / P, gap, ALU.mult, ALU.add))
                nc.vector.tensor_scalar(v, v, 0.0, None, ALU.add).then_inc(var_ready, 1)
                roots += 1
                dve.wait_ge(rooted, roots)
                if not twice:
                    then(nc.vector.reciprocal(rstd[0:p, :, 0], r))
                    continue
                then(nc.vector.reciprocal(f, r))
                then(nc.vector.tensor_scalar(v, v, -EPS, None, ALU.add))
                then(nc.vector.tensor_tensor(v, v, f, ALU.mult))
                then(nc.vector.tensor_tensor(v, v, f, ALU.mult))
                nc.vector.tensor_scalar(v, v, EPS, None, ALU.add).then_inc(var_ready, 1)
                roots += 1
                dve.wait_ge(rooted, roots)
                then(nc.vector.reciprocal(r, r))
                then(nc.vector.tensor_tensor(rstd[0:p, :, 0], r, f, ALU.mult))

        @block.scalar
        def _(act):
            roots = 0
            for stats, mean, rstd, p, twice in jobs:
                for _ in range(1 + twice):
                    roots += 1
                    act.wait_ge(var_ready, roots)
                    nc.scalar.activation(root[0:p, :], var[0:p, :], ACT.Sqrt).then_inc(rooted, 1)


def attention0(nc, dram, T, bank):
    NB = T["batches"]
    S = 77
    SP = 78
    D = 128
    SCALE = float(1.0 / np.sqrt(np.float32(D)))
    with ExitStack() as stack:
        core = Core(nc, stack)
        ctx = core.sb("a0_ctx", [S, 2, D], F32)
        mask = core.sb("a0_mask", [P, 2, S], I32)
        maskb = core.sb("a0_mask_bias", [P, 2, S], BF16)
        xn = core.sb("a0_xn", [P, D], F32)
        q_hi = core.sb("a0_q_hi", [P, 2, 4, P], F32R)
        q_lo = core.sb("a0_q_lo", [P, 2, 4, P], F32R)
        q_f = core.sb("a0_q_f", [P, 4, P], F32)
        k_hi = core.sb("a0_k_hi", [P, 2, 4 * SP], F32R)
        k_lo = core.sb("a0_k_lo", [P, 2, 4 * SP], F32R)
        k_f = core.sb("a0_k_f", [P, 4 * SP], F32)
        v1 = core.sb("a0_v_and_one", [S, 2, 16, 9], F32)
        ones = core.sb("a0_ones", [S, 16, 8], F32)
        negmax = core.sb("a0_negmax", [P, 16], F32)
        shift = core.sb("a0_shift", [P, 2, P], BF16)
        probs = core.sb("a0_probs", [S, 2, 512], F32)
        rden = core.sb("a0_rden", [P, 16], F32)
        o = core.sb("a0_o", [P, D], F32)
        oT = core.sb("a0_oT", [P, P], F32)

        ctx_in = [core.sem(f"a0_ctx_in{k}") for k in range(2)]
        mask_in = [core.sem(f"a0_mask_in{k}") for k in range(2)]
        zeroed = core.sem("a0_zeroed")
        mask_ready = core.sem("a0_mask_ready")
        v_ready = core.sem("a0_v_ready")
        xn_ready = core.sem("a0_xn_ready")
        qk_turned = core.sem("a0_qk_turned")
        blocked = core.sem("a0_blocked")
        hi_ready = core.sem("a0_hi_ready")
        lo_ready = core.sem("a0_lo_ready")
        rough_done = core.sem("a0_rough_done")
        max_done = core.sem("a0_max_done")
        max_turned = core.sem("a0_max_turned")
        shift_ready = core.sem("a0_shift_ready")
        scores_done = core.sem("a0_scores_done")
        exp_done = core.sem("a0_exp_done")
        av_done = core.sem("a0_av_done")
        rden_done = core.sem("a0_rden_done")
        o_ready = core.sem("a0_o_ready")
        o_turned = core.sem("a0_o_turned")
        oT_ready = core.sem("a0_oT_ready")
        y_done = core.sem("a0_y_done")
        x_ready = core.sem("a0_x_ready")
        ctx_stat_done = core.sem("a0_ctx_stat_done")

        TURN, MAXT, YT = bank[0], bank[1], bank[2]
        ROUGH, SCORES, AV = bank[3:5], bank[5:7], bank[7]
        block = stack.enter_context(nc.Block())

        @block.sync
        def _(sp):
            def load(b, k, first):
                if not first:
                    wait(sp, v_ready, b - 1)
                    wait(sp, ctx_stat_done, b - 1)
                    wait(sp, qk_turned, b - 1)
                    wait(sp, mask_ready, b - 1)
                sp.dma_start(ctx[:, k, :], dram["ctx"][b]).then_inc(ctx_in[k], 16)
                sp.dma_start(mask[:, k, :], dram["mask"][b]).then_inc(mask_in[k], 16)
            load(0, 0, True)
            load(1, 1, True)
            with sp.Fori(1, NB // 2) as pair:
                b = 2 * pair
                load(b, 0, False)
                load(b + 1, 1, False)

        @block.gpsimd
        def _(pool):
            nc.gpsimd.memset(v1[:, :, :, :], 1.0).then_inc(zeroed, 1)
            nc.gpsimd.memset(shift[:, :, :], 0.0).then_inc(zeroed, 1)
            nc.gpsimd.memset(k_f[:, :], 0.0).then_inc(zeroed, 1)
            nc.gpsimd.memset(ones[:, :, :], 1.0).then_inc(zeroed, 1)
            pool.wait_ge(zeroed, 4)

            def prepare(b, k, turn):
                pool.wait_ge(ctx_in[k], turn)
                wait(pool, av_done, 4 * (b - 1))
                nc.gpsimd.tensor_tensor(v1[:, k, :, 0:8], ctx[:, k, :].rearrange("s (h d) -> s h d", h=16),
                                        ones[:, :, :], ALU.mult).then_inc(v_ready, 1)
            prepare(0, 0, 16)
            prepare(1, 1, 16)
            with pool.Fori(1, NB // 2) as pair:
                for k in range(2):
                    prepare(2 * pair + k, k, 16 * pair + 16)

        @block.vector
        def _(dve):
            dve.wait_ge(zeroed, 3)

            def step(b, n, p):
                q = 1 - p
                if n is not None:
                    wait(dve, qk_turned, n)
                    nc.vector.tensor_scalar(xn[:, :], T["x"][:, n, :], T["mean"][:, n, :], T["rstd"][:, n, :], ALU.subtract, ALU.mult).then_inc(xn_ready, 1)
                    wait(dve, mask_in[q], n * 8 + 16 - 8 * q)
                    if b is not None:
                        wait(dve, scores_done, 4 * b)
                    nc.vector.tensor_scalar(maskb[:, q, :], mask[:, q, :], 0.0, MASKED, ALU.is_equal, ALU.mult).then_inc(mask_ready, 1)
                    dve.wait_ge(qk_turned, n + 1)
                    wait(dve, lo_ready, 2 * n)
                    wait(dve, hi_ready, 2 * n)
                    nc.vector.tensor_tensor(q_f[:, :, :], TURN[:, 0:P].unsqueeze(1).to_broadcast([P, 4, P]),
                                            T["headmask"][:, :].unsqueeze(2).to_broadcast([P, 4, P]), ALU.mult).then_inc(blocked, 1)
                    nc.vector.tensor_tensor(k_f[:, :].rearrange("p (g s) -> p g s", g=4)[:, :, 0:S],
                                            TURN[:, P:P + S].unsqueeze(1).to_broadcast([P, 4, S]),
                                            T["groupmask"][:, :].unsqueeze(2).to_broadcast([P, 4, S]), ALU.mult).then_inc(blocked, 1)
                    dve.wait_ge(hi_ready, 2 * n + 2)
                    if b is not None:
                        wait(dve, scores_done, 4 * b)
                    nc.vector.tensor_tensor(q_lo[:, q, :, :], q_f[:, :, :], q_hi[:, q, :, :].bitcast(F32), ALU.subtract).then_inc(lo_ready, 1)
                    nc.vector.tensor_tensor(k_lo[:, q, :], k_f[:, :], k_hi[:, q, :].bitcast(F32), ALU.subtract).then_inc(lo_ready, 1)
                    wait(dve, ctx_in[q], n * 8 + 16 - 8 * q)
                    nc.vector.bn_stats(T["ctx_stats"][0:S, n, :], ctx[:, q, :]).then_inc(ctx_stat_done, 1)
                    for i in range(4):
                        dve.wait_ge(rough_done, 4 * n + i + 1)
                        if i == 0:
                            wait(dve, max_turned, n)
                        nc.vector.tensor_reduce(negmax[:, 4 * i:4 * i + 4], ROUGH[i % 2][:, 0:4 * SP].rearrange("p (g s) -> p g s", g=4)[:, :, 0:S],
                                                AX.X, ALU.max, negate=True).then_inc(max_done, 1)
                if b is not None:
                    dve.wait_ge(av_done, 4 * b + 4)
                    av = AV[:, 0:144].rearrange("p (h d) -> p h d", h=16)
                    nc.vector.reciprocal(rden[:, :], av[:, :, 8]).then_inc(rden_done, 1)
                    dve.wait_ge(rden_done, b + 1)
                    wait(dve, o_turned, b)
                    nc.vector.tensor_tensor(o[:, :].rearrange("p (h d) -> p h d", h=16), av[:, :, 0:8],
                                            rden[:, :].unsqueeze(2).to_broadcast([P, 16, 8]), ALU.mult).then_inc(o_ready, 1)
                    dve.wait_ge(y_done, b + 1)
                    nc.vector.tensor_tensor(T["x"][:, b, :], TURN[:, 384:512], T["x"][:, b, :], ALU.add).then_inc(x_ready, 1)
                    dve.wait_ge(x_ready, b + 1)
                    nc.vector.bn_stats(T["x_stats"][:, b, :], T["x"][:, b, :])
            pipelined(dve, NB, step)

        @block.scalar
        def _(act):
            nc.scalar.preload_act_table(ACT.Exp)
            act.wait_ge(zeroed, 3)

            def step(b, n, p):
                q = 1 - p
                if n is not None:
                    act.wait_ge(blocked, 2 * n + 1)
                    if b is not None:
                        wait(act, scores_done, 4 * b)
                    nc.scalar.copy(q_hi[:, q, :, :], q_f[:, :, :]).then_inc(hi_ready, 1)
                    act.wait_ge(blocked, 2 * n + 2)
                    nc.scalar.copy(k_hi[:, q, :], k_f[:, :]).then_inc(hi_ready, 1)
                if b is not None:
                    for g in range(4):
                        act.wait_ge(scores_done, 4 * b + g + 1)
                        wait(act, av_done, 4 * b + g - 1 if g else 4 * b)
                        nc.scalar.activation(probs[:, g % 2, :], SCORES[g % 2][0:S, :], ACT.Exp, scale=SCALE).then_inc(exp_done, 1)
                if n is not None:
                    act.wait_ge(max_turned, n + 1)
                    nc.scalar.copy(shift[0:16, q, :], MAXT[0:16, 0:P]).then_inc(shift_ready, 1)
                if b is not None:
                    act.wait_ge(o_turned, b + 1)
                    wait(act, y_done, b)
                    nc.scalar.copy(oT[:, :], YT[:, 0:P]).then_inc(oT_ready, 1)
            pipelined(act, NB, step)

        @block.tensor
        def _(pe):
            pe.wait_ge(zeroed, 3)
            keep = T["identb"][:, :].unsqueeze(1).to_broadcast([P, 4, P])

            def step(b, n, p):
                q = 1 - p
                if n is not None:
                    pe.wait_ge(xn_ready, n + 1)
                    if b is not None:
                        wait(pe, x_ready, b)
                    pe.transpose(TURN[:, 0:P], xn[:, :], T["ident"][:, :])
                    pe.wait_ge(ctx_in[q], n * 8 + 16 - 8 * q)
                    pe.transpose(TURN[:, P:P + S], ctx[:, q, :], T["ident"][0:S, 0:S]).then_inc(qk_turned, 1)
                for g in range(4):
                    if b is not None:
                        wait(pe, exp_done, 4 * b + g - 1 if g else 4 * b)
                        kg = slice(g * SP, g * SP + S)
                        three_products(pe, SCORES[g % 2][0:S, :], (k_hi[:, p, kg], k_lo[:, p, kg]),
                                       (q_hi[:, p, :, :], q_lo[:, p, :, :]), True, False)
                        pe.matmul(SCORES[g % 2][0:S, :], maskb[:, p, :], keep, start=False, stop=False)
                        if g == 0:
                            pe.wait_ge(shift_ready, b + 1)
                        for i in range(4):
                            mm = pe.matmul(SCORES[g % 2][0:S, i * P:(i + 1) * P], T["onerow"][:, 4 * i + g, 0:S],
                                           shift[:, p, :], start=False, stop=(i == 3))
                        mm.then_inc(scores_done, 1)
                    if n is not None:
                        if g == 0:
                            pe.wait_ge(lo_ready, 2 * n + 2)
                            pe.wait_ge(mask_ready, n + 1)
                        wait(pe, max_done, 4 * n + g - 1 if g else 4 * n)
                        pe.matmul(ROUGH[g % 2][:, 0:4 * SP], q_hi[:, q, g, :], k_hi[:, q, :], start=True, stop=False)
                        pe.matmul(ROUGH[g % 2][:, 0:4 * SP].rearrange("p (g s) -> p g s", g=4)[:, :, 0:S], T["identb"][:, :],
                                  maskb[:, q, :].unsqueeze(1).to_broadcast([P, 4, S]), start=False, stop=True).then_inc(rough_done, 1)
                    if b is not None and g >= 1:
                        weigh(b, g - 1, p)
                if b is not None:
                    weigh(b, 3, p)
                if n is not None:
                    pe.wait_ge(max_done, 4 * n + 4)
                    wait(pe, shift_ready, n)
                    pe.transpose(MAXT[0:16, 0:P], negmax[:, :], T["ident"][:, :]).then_inc(max_turned, 1)
                if b is not None:
                    pe.wait_ge(o_ready, b + 1)
                    wait(pe, oT_ready, b)
                    pe.transpose(YT[:, 0:P], o[:, :], T["ident"][:, :]).then_inc(o_turned, 1)
                    pe.wait_ge(oT_ready, b + 1)
                    if n is not None:
                        pe.wait_ge(blocked, 2 * n + 2)
                    pe.matmul(TURN[:, 384:512], T["onerow_f"][:, :], T["bout_row"][:, :], start=True, stop=False)
                    pe.matmul(TURN[:, 384:512], oT[:, :], T["w_out0"][:, :], start=False, stop=True).then_inc(y_done, 1)

            def weigh(b, g, p):
                pe.wait_ge(exp_done, 4 * b + g + 1)
                if g == 0:
                    wait(pe, o_ready, b)
                    pe.wait_ge(v_ready, b + 1)
                for i in range(4):
                    h = 4 * g + i
                    mm = pe.matmul(AV[:, 9 * h:9 * h + 9], probs[:, g % 2, i * P:(i + 1) * P], v1[:, p, h, :], start=True, stop=True)
                mm.then_inc(av_done, 1)
            pipelined(pe, NB, step)


def ffn0(nc, T, bank):
    NG = T["batches"] // 4
    STEPS = 32
    BIG = 1e30
    with ExitStack() as stack:
        core = Core(nc, stack)
        xn = core.sb("f0_xn", [P, 4, P], F32)
        xT = core.sb("f0_xT", [P, 512], F32)
        xT_hi = core.sb("f0_xT_hi", [P, 2, 512], F32R)
        xT_lo = core.sb("f0_xT_lo", [P, 2, 512], F32R)
        score = core.sb("f0_score", [P, 4, 16], F32)
        biased = core.sb("f0_biased", [P, 4, 16], F32)
        hi2 = core.sb("f0_pair_max", [P, 16, 2], F32)
        lo2 = core.sb("f0_pair_min", [P, 16, 2], F32)
        best = core.sb("f0_best", [P, 16], F32)
        second = core.sb("f0_second", [P, 16], F32)
        third = core.sb("f0_third", [P, 16], F32)
        over = core.sb("f0_over", [P, 4, 4, 4], F32)
        tie = core.sb("f0_tie", [P, 4, 4, 4], F32)
        rank = core.sb("f0_rank", [P, 16], F32)
        penalty = core.sb("f0_penalty", [P, 16], F32)
        left = core.sb("f0_left", [P, 4, 16], F32)
        top8 = core.sb("f0_top8", [P, 4, 8], F32)
        above = core.sb("f0_above", [P, 4, 16], F32)
        equal = core.sb("f0_equal", [P, 4, 16], F32)
        place = core.sb("f0_place", [P, 4, 16], F32)
        count = core.sb("f0_count", [P, 4], F32)
        combine = core.sb("f0_combine", [P, 4, 16], F32)
        combT = core.sb("f0_combT", [16, 2, 512], F32)
        gate = core.sb("f0_gate_sigmoid", [P, 2, 512], F32)
        silu = core.sb("f0_silu", [P, 512], F32)
        hidden = core.sb("f0_hidden", [P, 6, 512], F32)

        xn_ready = core.sem("f0_xn_ready")
        turned = core.sem("f0_turned")
        xT_ready = core.sem("f0_xT_ready")
        hi_ready = core.sem("f0_hi_ready")
        lo_ready = core.sem("f0_lo_ready")
        logits_done = core.sem("f0_logits_done")
        score_ready = core.sem("f0_score_ready")
        route_step = core.sem("f0_route_step")
        comb_ready = core.sem("f0_comb_ready")
        comb_turned = core.sem("f0_comb_turned")
        combT_ready = core.sem("f0_combT_ready")
        gate_done = core.sem("f0_gate_done")
        up_done = core.sem("f0_up_done")
        spread_done = core.sem("f0_spread_done")
        sigmoid_done = core.sem("f0_sigmoid_done")
        silu_done = core.sem("f0_silu_done")
        hidden_done = core.sem("f0_hidden_done")
        weighed_done = core.sem("f0_weighed_done")
        y_done = core.sem("f0_y_done")
        x_ready = core.sem("f0_x_ready")

        TURN, ROUTE, GATE, UP, SPREAD, Y = bank[0], bank[1], bank[2:4], bank[4:6], bank[6], bank[7]
        block = stack.enter_context(nc.Block())

        @block.vector
        def _(dve):
            def route(n):
                steps = 0

                def then(instruction):
                    nonlocal steps
                    instruction.then_inc(route_step, 1)
                    steps += 1

                def settled():
                    dve.wait_ge(route_step, n * STEPS + steps)

                V = nc.vector
                dve.wait_ge(score_ready, n + 1)
                then(V.tensor_tensor(biased[:, :, :], score[:, :, :], T["router_bias"][:, :].unsqueeze(1).to_broadcast([P, 4, 16]), ALU.add))
                settled()
                pairs = biased[:, :, :].rearrange("p b (g e t) -> p (b g) e t", g=4, e=2)
                then(V.tensor_tensor(hi2[:, :, :], pairs[:, :, :, 0], pairs[:, :, :, 1], ALU.max))
                then(V.tensor_tensor(lo2[:, :, :], pairs[:, :, :, 0], pairs[:, :, :, 1], ALU.min))
                settled()
                then(V.tensor_tensor(best[:, :], hi2[:, :, 0], hi2[:, :, 1], ALU.max))
                then(V.tensor_tensor(second[:, :], hi2[:, :, 0], hi2[:, :, 1], ALU.min))
                then(V.tensor_tensor(third[:, :], lo2[:, :, 0], lo2[:, :, 1], ALU.max))
                settled()
                then(V.tensor_tensor(second[:, :], second[:, :], third[:, :], ALU.max))
                settled()
                then(V.tensor_tensor(best[:, :], best[:, :], second[:, :], ALU.add))
                settled()
                sums = best[:, :].rearrange("p (b g) -> p b g", b=4)
                mine = sums.unsqueeze(3).to_broadcast([P, 4, 4, 4])
                other = sums.unsqueeze(2).to_broadcast([P, 4, 4, 4])
                tri = T["tri"][:, :, :].unsqueeze(1).to_broadcast([P, 4, 4, 4])
                then(V.tensor_tensor(over[:, :, :, :], other, mine, ALU.is_gt))
                then(V.tensor_tensor(tie[:, :, :, :], other, mine, ALU.is_equal))
                settled()
                then(V.tensor_tensor(tie[:, :, :, :], tie[:, :, :, :], tri, ALU.mult))
                settled()
                then(V.tensor_tensor(over[:, :, :, :], over[:, :, :, :], tie[:, :, :, :], ALU.add))
                settled()
                then(V.tensor_reduce(rank[:, :], over[:, :, :, :], AX.X, ALU.add))
                settled()
                then(V.tensor_scalar(rank[:, :], rank[:, :], 2.0, None, ALU.is_lt))
                settled()
                then(V.tensor_scalar(penalty[:, :], rank[:, :], BIG, -BIG, ALU.mult, ALU.add))
                kept = rank[:, :].unsqueeze(2).to_broadcast([P, 16, 4])
                left16 = left[:, :, :].rearrange("p b (g e) -> p (b g) e", g=4)
                then(V.tensor_tensor(left16, biased[:, :, :].rearrange("p b (g e) -> p (b g) e", g=4), kept, ALU.mult))
                settled()
                then(V.tensor_tensor(left16, left16, penalty[:, :].unsqueeze(2).to_broadcast([P, 16, 4]), ALU.add))
                settled()
                V.memset(place[:, 0, 0:1], 0.0)
                for k in range(4):
                    then(V.max(top8[:, k, :], left[:, k, :]))
                settled()
                fourth = top8[:, :, 3:4].to_broadcast([P, 4, 16])
                then(V.tensor_tensor(above[:, :, :], left[:, :, :], fourth, ALU.is_gt))
                then(V.tensor_tensor(equal[:, :, :], left[:, :, :], fourth, ALU.is_equal))
                settled()
                then(V.tensor_reduce(count[:, :], above[:, :, :], AX.X, ALU.add))
                flat = lambda t: t[:, :, :].rearrange("p b e -> p (b e)")
                then(V.tensor_tensor_scan(flat(place), T["blockstart"][:, :], flat(equal), 0.0, ALU.mult, ALU.add))
                settled()
                then(V.tensor_tensor(place[:, :, :], place[:, :, :], count[:, :].unsqueeze(2).to_broadcast([P, 4, 16]), ALU.add))
                settled()
                then(V.scalar_tensor_tensor(flat(equal), flat(place), 4.0, flat(equal), ALU.is_le, ALU.mult))
                settled()
                then(V.tensor_tensor(above[:, :, :], above[:, :, :], equal[:, :, :], ALU.add))
                settled()
                then(V.tensor_tensor(above[:, :, :], above[:, :, :], score[:, :, :], ALU.mult))
                settled()
                then(V.tensor_reduce(count[:, :], above[:, :, :], AX.X, ALU.add))
                settled()
                then(V.tensor_scalar(count[:, :], count[:, :], 1e-20, None, ALU.add))
                settled()
                then(V.reciprocal(count[:, :], count[:, :]))
                settled()
                wait(dve, comb_turned, n)
                V.tensor_tensor(combine[:, :, :], above[:, :, :], count[:, :].unsqueeze(2).to_broadcast([P, 4, 16]),
                                ALU.mult).then_inc(comb_ready, 1)
                assert steps == STEPS, steps

            def hide(b, j):
                dve.wait_ge(sigmoid_done, 6 * b + j + 1)
                wait(dve, hidden_done, 6 * b + j)
                nc.vector.tensor_tensor(silu[:, :], GATE[j % 2][:, :], gate[:, j % 2, :], ALU.mult).then_inc(silu_done, 1)
                dve.wait_ge(silu_done, 6 * b + j + 1)
                dve.wait_ge(up_done, 6 * b + j + 1)
                if j == 0:
                    wait(dve, y_done, b)
                nc.vector.tensor_tensor(hidden[:, j, :], UP[j % 2][:, :], silu[:, :], ALU.mult).then_inc(hidden_done, 1)
                if j >= 2:
                    dve.wait_ge(hidden_done, 6 * b + j + 1)
                    dve.wait_ge(spread_done, 4 * b + j - 1)
                    nc.vector.tensor_tensor(hidden[:, j, :], SPREAD[:, :], hidden[:, j, :], ALU.mult).then_inc(weighed_done, 1)

            def step(b, n, p):
                if n is not None:
                    wait(dve, turned, n)
                    for k in range(4):
                        nc.vector.tensor_scalar(xn[:, k, :], T["x"][:, 4 * n + k, :], T["mean"][:, 4 * n + k, :],
                                                T["rstd"][:, 4 * n + k, :], ALU.subtract, ALU.mult).then_inc(xn_ready, 1)
                if b is not None:
                    hide(b, 0)
                    hide(b, 1)
                if n is not None:
                    dve.wait_ge(hi_ready, n + 1)
                    nc.vector.tensor_tensor(xT_lo[:, 1 - p, :], xT[:, :], xT_hi[:, 1 - p, :].bitcast(F32), ALU.subtract).then_inc(lo_ready, 1)
                if b is not None:
                    hide(b, 2)
                    hide(b, 3)
                if n is not None:
                    route(n)
                if b is not None:
                    hide(b, 4)
                    hide(b, 5)
                    dve.wait_ge(y_done, b + 1)
                    for k in range(4):
                        nc.vector.tensor_tensor(T["x"][:, 4 * b + k, :], Y[:, k * P:(k + 1) * P], T["x"][:, 4 * b + k, :], ALU.add).then_inc(x_ready, 1)
                    for k in range(4):
                        dve.wait_ge(x_ready, 4 * b + k + 1)
                        nc.vector.bn_stats(T["x_stats"][:, 4 * b + k, :], T["x"][:, 4 * b + k, :])
            pipelined(dve, NG, step)

        @block.scalar
        def _(act):
            nc.scalar.preload_act_table(ACT.Sigmoid)
            def sigmoid(b, j):
                act.wait_ge(gate_done, 6 * b + j + 1)
                wait(act, silu_done, 6 * b + j - 1 if j else 6 * b)
                nc.scalar.activation(gate[:, j % 2, :], GATE[j % 2][:, :], ACT.Sigmoid).then_inc(sigmoid_done, 1)

            def step(b, n, p):
                if b is not None:
                    sigmoid(b, 0)
                    sigmoid(b, 1)
                if n is not None:
                    act.wait_ge(turned, n + 1)
                    wait(act, lo_ready, n)
                    wait(act, logits_done, n)
                    nc.scalar.copy(xT[:, :], TURN[:, :]).then_inc(xT_ready, 1)
                    act.wait_ge(xT_ready, n + 1)
                    if b is not None:
                        wait(act, up_done, 6 * b)
                    nc.scalar.copy(xT_hi[:, 1 - p, :], xT[:, :]).then_inc(hi_ready, 1)
                if b is not None:
                    sigmoid(b, 2)
                if n is not None:
                    act.wait_ge(logits_done, n + 1)
                    wait(act, comb_ready, n)
                    nc.scalar.activation(score[:, :, :].rearrange("p b e -> p (b e)"), ROUTE[:, 0:64], ACT.Sigmoid).then_inc(score_ready, 1)
                if b is not None:
                    sigmoid(b, 3)
                    sigmoid(b, 4)
                    sigmoid(b, 5)
                if n is not None:
                    act.wait_ge(comb_turned, n + 1)
                    nc.scalar.copy(combT[:, 1 - p, :], ROUTE[0:16, :]).then_inc(combT_ready, 1)
            pipelined(act, NG, step)

        @block.tensor
        def _(pe):
            gu_hi, gu_lo = T["gate_up"]

            def expand(b, j, p):
                if j == 0:
                    pe.wait_ge(lo_ready, b + 1)
                x_parts = (xT_hi[:, p, :], xT_lo[:, p, :])
                wait(pe, silu_done, 6 * b + j - 1 if j else 6 * b)
                three_products(pe, GATE[j % 2][:, :], (gu_hi[:, 0, j, :], gu_lo[:, 0, j, :]), x_parts, True, True).then_inc(gate_done, 1)
                wait(pe, hidden_done, 6 * b + j - 1 if j else 6 * b)
                three_products(pe, UP[j % 2][:, :], (gu_hi[:, 1, j, :], gu_lo[:, 1, j, :]), x_parts, True, True).then_inc(up_done, 1)
                if j >= 2:
                    pe.wait_ge(combT_ready, b + 1)
                    wait(pe, weighed_done, 4 * b + j - 2)
                    pe.matmul(SPREAD[:, :], T["expert_rows"][:, j - 2, :], combT[:, p, :], start=True, stop=True).then_inc(spread_done, 1)

            def step(b, n, p):
                if b is not None:
                    expand(b, 0, p)
                if n is not None:
                    pe.wait_ge(xn_ready, 4 * n + 4)
                    wait(pe, xT_ready, n)
                    for k in range(4):
                        mm = pe.transpose(TURN[:, k * P:(k + 1) * P], xn[:, k, :], T["ident"][:, :])
                    mm.then_inc(turned, 1)
                if b is not None:
                    expand(b, 1, p)
                    expand(b, 2, p)
                if n is not None:
                    pe.wait_ge(xT_ready, n + 1)
                    wait(pe, combT_ready, n)
                    for k in range(4):
                        mm = pe.matmul(ROUTE[:, 16 * k:16 * k + 16], xT[:, k * P:(k + 1) * P], T["router"][:, :], start=True, stop=True)
                    mm.then_inc(logits_done, 1)
                if b is not None:
                    for j in range(3, 6):
                        expand(b, j, p)
                if n is not None:
                    pe.wait_ge(comb_ready, n + 1)
                    for k in range(4):
                        mm = pe.transpose(ROUTE[0:16, k * P:(k + 1) * P], combine[:, k, :], T["ident"][:, :])
                    mm.then_inc(comb_turned, 1)
                if b is not None:
                    pe.wait_ge(hidden_done, 6 * b + 6)
                    pe.wait_ge(weighed_done, 4 * b + 4)
                    wait(pe, x_ready, 4 * b)
                    for k in range(4):
                        for j in range(6):
                            mm = pe.matmul(Y[:, k * P:(k + 1) * P], hidden[:, j, k * P:(k + 1) * P], T["down"][:, j, :],
                                           start=(j == 0), stop=(j == 5))
                    mm.then_inc(y_done, 1)
            pipelined(pe, NG, step)


def attention1(nc, dram, T, bank):
    NB = T["batches"]
    S = 77
    BLOCKS = ((0, P), (P, S))
    J = P + S
    SCALE = 64 ** -0.5
    with ExitStack() as stack:
        core = Core(nc, stack)
        ctx = core.sb("a1_ctx", [S, 2, P], F32)
        xn = core.sb("a1_xn", [P, P], F32)
        cn = core.sb("a1_cn", [S, P], F32)
        kv = core.sb("a1_kv", [P, 256], F32)
        kv_hi = core.sb("a1_kv_hi", [P, 2, 256], F32R)
        kv_lo = core.sb("a1_kv_lo", [P, 2, 256], F32R)
        g_hi = core.sb("a1_g_hi", [P, 2, 16 * P], F32R)
        g_lo = core.sb("a1_g_lo", [P, 2, 16 * P], F32R)
        v1 = core.sb("a1_v_and_one", [P, 2, 2, 16, 65], F32)
        negmax = core.sb("a1_negmax", [P, 16], F32)
        shift = core.sb("a1_shift", [P, 2, P], BF16)
        probs = core.sb("a1_probs", [P, 2, 2, 512], F32)
        rden = core.sb("a1_rden", [P, 4], F32)
        o = core.sb("a1_o", [P, 16, 64], F32)
        oT = core.sb("a1_oT", [P, 8, P], F32)

        ctx_in = [core.sem(f"a1_ctx_in{k}") for k in range(2)]
        zeroed = core.sem("a1_zeroed")
        cn_ready = core.sem("a1_cn_ready")
        xn_ready = core.sem("a1_xn_ready")
        turned = core.sem("a1_turned")
        kv_ready = core.sem("a1_kv_ready")
        kv_hi_ready = core.sem("a1_kv_hi_ready")
        kv_lo_ready = core.sem("a1_kv_lo_ready")
        v_done = core.sem("a1_v_done")
        v_kept = core.sem("a1_v_kept")
        g_done = core.sem("a1_g_done")
        g_hi_ready = core.sem("a1_g_hi_ready")
        g_lo_ready = core.sem("a1_g_lo_ready")
        rough_done = core.sem("a1_rough_done")
        max_done = core.sem("a1_max_done")
        max_turned = core.sem("a1_max_turned")
        shift_ready = core.sem("a1_shift_ready")
        scores_done = core.sem("a1_scores_done")
        exp_done = core.sem("a1_exp_done")
        av_done = core.sem("a1_av_done")
        rden_done = core.sem("a1_rden_done")
        o_ready = core.sem("a1_o_ready")
        o_turned = core.sem("a1_o_turned")
        oT_ready = core.sem("a1_oT_ready")
        y_done = core.sem("a1_y_done")
        x_ready = core.sem("a1_x_ready")

        TURN, GB, VB, ROUGH, SCORES, AV = bank[0], bank[1], bank[2], bank[3:5], bank[5:7], bank[7]
        block = stack.enter_context(nc.Block())

        @block.sync
        def _(sp):
            sp.dma_start(ctx[:, 0, :], dram["ctx"][0]).then_inc(ctx_in[0], 16)
            sp.dma_start(ctx[:, 1, :], dram["ctx"][1]).then_inc(ctx_in[1], 16)
            with sp.Fori(1, NB // 2) as pair:
                for k in range(2):
                    sp.wait_ge(cn_ready, 2 * pair + k - 1)
                    sp.dma_start(ctx[:, k, :], dram["ctx"][2 * pair + k]).then_inc(ctx_in[k], 16)

        @block.gpsimd
        def _(pool):
            nc.gpsimd.memset(v1[:, :, :, :, :], 1.0).then_inc(zeroed, 1)
            nc.gpsimd.memset(shift[:, :, :], 0.0).then_inc(zeroed, 1)
            nc.gpsimd.memset(kv[:, :], 0.0).then_inc(zeroed, 1)

        @block.vector
        def _(dve):
            dve.wait_ge(zeroed, 3)

            def keep_max(n, k):
                dve.wait_ge(rough_done, 8 * n + k + 1)
                if k == 0:
                    wait(dve, max_turned, n)
                nc.vector.tensor_reduce(negmax[:, 2 * k:2 * k + 2], ROUGH[k % 2][:, :].rearrange("p (h j) -> p h j", h=2)[:, :, 0:J],
                                        AX.X, ALU.max, negate=True).then_inc(max_done, 1)

            def normalise(b, c):
                dve.wait_ge(av_done, 4 * b + c + 1)
                av = AV[:, 0:260].rearrange("p (h d) -> p h d", h=4)
                nc.vector.reciprocal(rden[:, :], av[:, :, 64]).then_inc(rden_done, 1)
                dve.wait_ge(rden_done, 4 * b + c + 1)
                if c % 2 == 0:
                    wait(dve, o_turned, 2 * b - 1 + c // 2)
                nc.vector.tensor_tensor(o[:, 4 * c:4 * c + 4, :], av[:, :, 0:64],
                                        rden[:, :].unsqueeze(2).to_broadcast([P, 4, 64]), ALU.mult).then_inc(o_ready, 1)

            def turn_rows(t, p):
                wait(dve, turned, t)
                nc.vector.tensor_scalar(xn[:, :], T["x"][:, t, :], T["mean"][:, t, :], T["rstd"][:, t, :],
                                        ALU.subtract, ALU.mult).then_inc(xn_ready, 1)
                wait(dve, ctx_in[p], t * 8 + 16 - 8 * p)
                nc.vector.tensor_scalar(cn[:, :], ctx[:, p, :], T["ctx_mean"][0:S, t, :], T["ctx_rstd"][0:S, t, :],
                                        ALU.subtract, ALU.mult).then_inc(cn_ready, 1)

            def scale_rows(t):
                dve.wait_ge(turned, t + 1)
                wait(dve, g_done, 4 * t)
                wait(dve, kv_hi_ready, t)
                wait(dve, kv_lo_ready, t)
                for k, (at, length) in enumerate(BLOCKS):
                    nc.vector.tensor_scalar(kv[:, at:at + length], TURN[:, at:at + length], T["ln_cols"][:, 2 * k:2 * k + 1],
                                            T["ln_cols"][:, 2 * k + 1:2 * k + 2], ALU.mult, ALU.add).then_inc(kv_ready, 1)

            def low_rows(t, p):
                dve.wait_ge(kv_hi_ready, t + 1)
                nc.vector.tensor_tensor(kv_lo[:, p, :], kv[:, :], kv_hi[:, p, :].bitcast(F32), ALU.subtract).then_inc(kv_lo_ready, 1)

            def low_queries(n, c, q):
                dve.wait_ge(g_hi_ready, 4 * n + c + 1)
                nc.vector.tensor_tensor(g_lo[:, q, 512 * c:512 * c + 512], GB[:, :], g_hi[:, q, 512 * c:512 * c + 512].bitcast(F32),
                                        ALU.subtract).then_inc(g_lo_ready, 1)

            def step(late, b, n, t, p):
                q = 1 - p
                if t is not None:
                    turn_rows(t, p)
                if n is not None:
                    low_queries(n, 0, q)
                if late is not None:
                    dve.wait_ge(y_done, late + 1)
                    nc.vector.tensor_tensor(T["x"][:, late, :], TURN[:, 384:512], T["x"][:, late, :], ALU.add).then_inc(x_ready, 1)
                    dve.wait_ge(x_ready, late + 1)
                    nc.vector.bn_stats(T["x_stats"][:, late, :], T["x"][:, late, :])
                for c in range(1, 4):
                    if n is not None:
                        low_queries(n, c, q)
                        keep_max(n, 2 * c - 2)
                        keep_max(n, 2 * c - 1)
                    if b is not None:
                        normalise(b, c - 1)
                if n is not None:
                    keep_max(n, 6)
                    keep_max(n, 7)
                if t is not None:
                    scale_rows(t)
                if b is not None:
                    normalise(b, 3)
                if t is not None:
                    low_rows(t, p)
            turn_rows(0, 0)
            scale_rows(0)
            low_rows(0, 0)
            pipelined_deep(dve, NB, step)

        @block.scalar
        def _(act):
            nc.scalar.preload_act_table(ACT.Exp)
            act.wait_ge(zeroed, 3)

            def exponential(b, c, k):
                rows = BLOCKS[k][1]
                act.wait_ge(scores_done, 8 * b + 2 * c + k + 1)
                wait(act, av_done, 4 * b + c - 1 if c else 4 * b)
                nc.scalar.activation(probs[0:rows, c % 2, k, :], SCORES[k][0:rows, :], ACT.Exp, scale=SCALE).then_inc(exp_done, 1)

            def turn_o(b, half):
                act.wait_ge(o_turned, 2 * b + half + 1)
                if half == 0:
                    wait(act, y_done, b)
                nc.scalar.copy(oT[:, 4 * half:4 * half + 4, :], VB[:, :].rearrange("p (k t) -> p k t", k=4)).then_inc(oT_ready, 1)

            def high_rows(t, b, p):
                act.wait_ge(kv_ready, 2 * t + 2)
                if b is not None:
                    act.wait_ge(scores_done, 8 * b + 8)
                nc.scalar.copy(kv_hi[:, p, :], kv[:, :]).then_inc(kv_hi_ready, 1)

            def step(late, b, n, t, p):
                q = 1 - p
                for c in range(4):
                    if b is not None:
                        exponential(b, c, 0)
                        exponential(b, c, 1)
                    if late is not None and c == 0:
                        turn_o(late, 1)
                    if n is not None:
                        k, half = divmod(c, 2)
                        rows = BLOCKS[k][1]
                        act.wait_ge(v_done, 4 * n + c + 1)
                        if b is not None and c == 0:
                            wait(act, av_done, 4 * b)
                        nc.scalar.copy(v1[0:rows, q, k, 8 * half:8 * half + 8, 0:64],
                                       VB[0:rows, :].rearrange("p (h d) -> p h d", h=8)).then_inc(v_kept, 1)
                        act.wait_ge(g_done, 4 * n + c + 1)
                        nc.scalar.copy(g_hi[:, q, 512 * c:512 * c + 512], GB[:, :]).then_inc(g_hi_ready, 1)
                if b is not None:
                    turn_o(b, 0)
                if t is not None:
                    high_rows(t, b, p)
                if n is not None:
                    act.wait_ge(max_turned, n + 1)
                    nc.scalar.copy(shift[0:16, q, :], VB[0:16, 0:P]).then_inc(shift_ready, 1)
            high_rows(0, None, 0)
            pipelined_deep(act, NB, step)

        @block.tensor
        def _(pe):
            pe.wait_ge(zeroed, 3)

            def score(b, c, k, p):
                at, rows = BLOCKS[k]
                wait(pe, exp_done, 8 * b + 2 * c + k - 1 if c else 8 * b)
                out = SCORES[k][0:rows, :]
                three_products(pe, out, (kv_hi[:, p, at:at + rows], kv_lo[:, p, at:at + rows]),
                               (g_hi[:, p, 512 * c:512 * c + 512], g_lo[:, p, 512 * c:512 * c + 512]), True, False)
                if c == 0 and k == 0:
                    pe.wait_ge(shift_ready, b + 1)
                for i in range(4):
                    mm = pe.matmul(out[:, i * P:(i + 1) * P], T["onerow"][:, 4 * c + i, 0:rows], shift[:, p, :], start=False, stop=(i == 3))
                mm.then_inc(scores_done, 1)

            def values(n, c, q):
                k, half = divmod(c, 2)
                at, rows = BLOCKS[k]
                if c == 0:
                    pe.wait_ge(kv_lo_ready, n + 1)
                    wait(pe, oT_ready, 2 * (n - 1))
                else:
                    pe.wait_ge(v_kept, 4 * n + c)
                w = slice(512 * half, 512 * half + 512)
                three_products(pe, VB[0:rows, :], (kv_hi[:, q, at:at + rows], kv_lo[:, q, at:at + rows]),
                               (T["wv"][0][:, w], T["wv"][1][:, w]), True, True).then_inc(v_done, 1)

            def queries(n, c):
                wait(pe, g_lo_ready, 4 * n + c)
                for i in range(4):
                    mm = pe.matmul(GB[:, i * P:(i + 1) * P], T["m"][:, 4 * c + i, :], kv[:, 0:P], start=True, stop=True)
                mm.then_inc(g_done, 1)

            def rough(n, k, q):
                pe.wait_ge(g_hi_ready, 4 * n + k // 2 + 1)
                wait(pe, max_done, 8 * n + max(k - 1, 0))
                for i in range(2):
                    h = 2 * k + i
                    mm = pe.matmul(ROUGH[k % 2][:, 256 * i:256 * i + 256], g_hi[:, q, h * P:(h + 1) * P], kv_hi[:, q, :], start=True, stop=True)
                mm.then_inc(rough_done, 1)

            def weigh(b, c, p):
                pe.wait_ge(exp_done, 8 * b + 2 * c + 2)
                wait(pe, o_ready, 4 * b + c)
                if c == 0:
                    pe.wait_ge(v_kept, 4 * b + 4)
                for i in range(4):
                    for k, (_, rows) in enumerate(BLOCKS):
                        mm = pe.matmul(AV[:, 65 * i:65 * i + 65], probs[0:rows, c % 2, k, i * P:(i + 1) * P],
                                       v1[0:rows, p, k, 4 * c + i, :], start=(k == 0), stop=(k == 1))
                mm.then_inc(av_done, 1)

            def turn_o(b, half, n):
                pe.wait_ge(o_ready, 4 * b + 2 * half + 2)
                if half:
                    pe.wait_ge(shift_ready, n)
                    pe.wait_ge(oT_ready, 2 * b + 1)
                elif n is not None:
                    pe.wait_ge(v_kept, 4 * n + 4)
                else:
                    pe.wait_ge(oT_ready, 2 * b)
                for i in range(4):
                    k = 4 * half + i
                    mm = pe.transpose(VB[:, i * P:(i + 1) * P], o[:, 2 * k:2 * k + 2, :].rearrange("p h d -> p (h d)"), T["ident"][:, :])
                mm.then_inc(o_turned, 1)

            def turn_rows(t):
                pe.wait_ge(xn_ready, t + 1)
                pe.wait_ge(cn_ready, t + 1)
                wait(pe, x_ready, t - 2)
                pe.transpose(TURN[:, 0:P], xn[:, :], T["ident"][:, :])
                pe.transpose(TURN[:, P:J], cn[:, :], T["ident"][0:S, 0:S]).then_inc(turned, 1)

            def step(late, b, n, t, p):
                q = 1 - p
                for c in range(4):
                    if b is not None:
                        score(b, c, 0, p)
                        score(b, c, 1, p)
                    if late is not None and c == 0:
                        turn_o(late, 1, late + 2 if b is not None else NB)
                    if n is not None:
                        values(n, c, q)
                        queries(n, c)
                    if late is not None and c == 0:
                        pe.wait_ge(oT_ready, 2 * late + 2)
                        if n is not None:
                            pe.wait_ge(kv_ready, 2 * n + 2)
                        for k in range(8):
                            mm = pe.matmul(TURN[:, 384:512], oT[:, k, :], T["w_out1"][:, k, :], start=(k == 0), stop=(k == 7))
                        mm.then_inc(y_done, 1)
                    if n is not None and c >= 1:
                        rough(n, 2 * c - 2, q)
                        rough(n, 2 * c - 1, q)
                    if b is not None and c >= 1:
                        weigh(b, c - 1, p)
                if b is not None:
                    turn_o(b, 0, n)
                if n is not None:
                    rough(n, 6, q)
                    rough(n, 7, q)
                if t is not None:
                    turn_rows(t)
                if b is not None:
                    weigh(b, 3, p)
                if n is not None:
                    pe.wait_ge(max_done, 8 * n + 8)
                    if b is not None:
                        pe.wait_ge(oT_ready, 2 * b + 1)
                    else:
                        pe.wait_ge(v_kept, 4 * n + 4)
                    pe.transpose(VB[0:16, 0:P], negmax[:, :], T["ident"][:, :]).then_inc(max_turned, 1)
            turn_rows(0)
            pipelined_deep(pe, NB, step)


def global_scale(nc, name, top, T, parts):
    with ExitStack() as stack:
        core = Core(nc, stack)
        row = core.sb(name + "_row_max", [P, len(parts)], F32)
        every = core.sb(name + "_all_max", [P, len(parts)], F32)
        reduced = core.sem(name + "_reduced")
        spread = core.sem(name + "_spread")
        clamped = core.sem(name + "_clamped")
        block = stack.enter_context(nc.Block())

        @block.vector
        def _(dve):
            for k, (maxima, _, _) in enumerate(parts):
                nc.vector.tensor_reduce(row[:, k:k + 1], maxima, AX.XY if len(maxima.shape) == 3 else AX.X, ALU.max).then_inc(reduced, 1)
            dve.wait_ge(spread, 1)
            for k, (_, step, inverse) in enumerate(parts):
                nc.vector.tensor_scalar(step, every[:, k:k + 1], 1.0 / 32767.0, 1e-12, ALU.mult, ALU.max).then_inc(clamped, 1)
            for k, (_, step, inverse) in enumerate(parts):
                dve.wait_ge(clamped, k + 1)
                nc.vector.reciprocal(inverse, step)

        @block.gpsimd
        def _(pool):
            pool.wait_ge(reduced, len(parts))
            nc.gpsimd.partition_all_reduce(every[:, :], row[:, :], P, RMAX).then_inc(spread, 1)


def quantise_weights(nc, dram, T, W, bank):
    with ExitStack() as stack:
        core = Core(nc, stack)
        raw = [core.sb(f"f1_{n}_raw", [P, 12, 32], F32) for n in ("gate", "up", "down")]
        step = core.sb("f1_weight_step", [P, 3, 12], F32)
        inverse = core.sb("f1_weight_inverse", [P, 3, 12], F32)
        turned = core.sb("f1_weight_turned", [P, 2, 3, P], F32)
        w_in = core.sem("f1_weights_in")
        chain = core.sem("f1_weight_step_done")
        turn_done = core.sem("f1_weight_turn_done")
        kept = core.sem("f1_weight_kept")
        hi_ready = core.sem("f1_weight_hi_ready")
        block = stack.enter_context(nc.Block())

        @block.sync
        def _(sp):
            for k, name in enumerate(("w_gate", "w_up")):
                sp.dma_start(raw[k][:, :, :].rearrange("p (j r) i -> p j (r i)", j=3), dram[name].rearrange("(j p) c -> p j c", p=P)).then_inc(w_in, 16)
            sp.dma_start(raw[2][:, :, :].rearrange("p r i -> p (r i)"), dram["w_down"]).then_inc(w_in, 16)

        @block.vector
        def _(dve):
            steps = 0

            def then(instruction):
                nonlocal steps
                instruction.then_inc(chain, 1)
                steps += 1
                dve.wait_ge(chain, steps)
            dve.wait_ge(w_in, 48)
            for k in range(3):
                w = raw[k][:, :, :]
                wide = lambda t: t[:, k, :].unsqueeze(2).to_broadcast([P, 12, 32])
                then(nc.vector.tensor_reduce(step[:, k, :], w, AX.X, ALU.max, apply_absolute_value=True))
                then(nc.vector.tensor_scalar(step[:, k, :], step[:, k, :], 1.0 / 7.0, 1e-12, ALU.mult, ALU.max))
                then(nc.vector.reciprocal(inverse[:, k, :], step[:, k, :]))
                then(nc.vector.tensor_tensor(w, w, wide(inverse), ALU.mult))
                then(nc.vector.tensor_scalar(w, w, ROUND, -ROUND, ALU.add, ALU.add))
                then(nc.vector.tensor_scalar(w, w, 7.0, -8.0, ALU.min, ALU.max))
                then(nc.vector.tensor_tensor(w, w, wide(step), ALU.mult))
            for k in range(2):
                dve.wait_ge(hi_ready, k + 1)
                nc.vector.tensor_tensor(W["gu"][1][:, k, :, :], turned[:, k, :, :], W["gu"][0][:, k, :, :].bitcast(F32), ALU.subtract)

        @block.tensor
        def _(pe):
            for k in range(3):
                pe.wait_ge(chain, 7 * k + 7)
                for j in range(3):
                    mm = pe.transpose(bank[k][:, j * P:(j + 1) * P], raw[k][:, 4 * j:4 * j + 4, :].rearrange("p r i -> p (r i)"), T["ident"][:, :])
                mm.then_inc(turn_done, 1)

        @block.scalar
        def _(act):
            for k in range(2):
                act.wait_ge(turn_done, k + 1)
                nc.scalar.copy(turned[:, k, :, :], bank[k][:, 0:384].rearrange("p (j c) -> p j c", j=3)).then_inc(kept, 1)
                act.wait_ge(kept, k + 1)
                nc.scalar.copy(W["gu"][0][:, k, :, :], turned[:, k, :, :]).then_inc(hi_ready, 1)
            act.wait_ge(turn_done, 3)
            nc.scalar.copy(W["down"][:, :, :], bank[2][:, 0:384].rearrange("p (j c) -> p j c", j=3))


def ffn1(nc, dram, T, bank, out):
    NB = T["batches"]
    NG = NB // 4
    with ExitStack() as kept:
        core = Core(nc, kept)
        W = {"gu": (core.sb("f1_gate_up_hi", [P, 2, 3, P], F32R), core.sb("f1_gate_up_lo", [P, 2, 3, P], F32R)),
             "down": core.sb("f1_down", [P, 3, P], F32)}
        codes = T["x"][:, 0:NB // 2, :].bitcast(I16).rearrange("p (g b) c -> p g (b c)", b=2)
        spare = T["x"][:, 32:64, :].rearrange("p b c -> p (b c)").rearrange("p (n k c) -> p n k c", n=4, k=2)
        peaks = core.sb("f1_row_peaks", [P, NG, 6], F32)
        scales = {n: (core.sb(f"f1_{n}_step", [P, 1], F32), core.sb(f"f1_{n}_inverse", [P, 1], F32))
                  for n in ("x", "gate", "up", "gated", "o")}
        round_col = core.sb("f1_round", [P, 1], F32)
        quantise_weights(nc, dram, T, W, bank)

        with ExitStack() as stack:
            passing = Core(nc, stack)
            xn = passing.sb("f1_xn", [P, NB, P], F32)
            x_peak = passing.sb("f1_x_peak", [P, NB, 1], F32)
            normal = passing.sem("f1_normal")
            parked = passing.sem("f1_x_parked")
            with ExitStack() as s2:
                block = s2.enter_context(nc.Block())

                @block.gpsimd
                def _(pool):
                    nc.gpsimd.memset(round_col[:, :], ROUND)

                @block.sync
                def _(sp):
                    sp.dma_start(dram["x_parked"].rearrange("b t c -> t b c"), T["x"][:, 0:NB, :]).then_inc(parked, 16)
                    sp.wait_ge(parked, 16)

                @block.vector
                def _(dve):
                    with dve.Fori(0, NB) as b:
                        nc.vector.tensor_scalar(xn[:, b, :], T["x"][:, b, :], T["mean"][:, b, :], T["rstd"][:, b, :],
                                                ALU.subtract, ALU.mult).then_inc(normal, 1)
                        dve.wait_ge(normal, b + 1)
                        nc.vector.tensor_reduce(x_peak[:, b, :], xn[:, b, :], AX.X, ALU.max, apply_absolute_value=True)
            global_scale(nc, "f1_x", kept, T, [(x_peak[:, :, 0], scales["x"][0][:, :], scales["x"][1][:, :])])
            quantise_x(nc, T, W, bank, xn, codes, peaks, scales)
        global_scale(nc, "f1_gu", kept, T, [(peaks[:, :, 0:3], scales["gate"][0][:, :], scales["gate"][1][:, :]),
                                            (peaks[:, :, 3:6], scales["up"][0][:, :], scales["up"][1][:, :])])
        gated = core.sb("f1_gated", [P, NG * 3, 512], F32)
        up = core.sb("f1_up_codes", [P, NG * 3, 512], I16)
        gate_and_up(nc, T, W, bank, codes, spare, peaks, scales, gated, up, round_col)
        global_scale(nc, "f1_gd", kept, T, [(peaks[:, :, 0:3], scales["gated"][0][:, :], scales["gated"][1][:, :])])
        multiply_up(nc, peaks, scales, gated, up, round_col)
        global_scale(nc, "f1_o", kept, T, [(peaks[:, :, 0:3], scales["o"][0][:, :], scales["o"][1][:, :])])
        project(nc, dram, W, bank, scales, gated, spare, round_col, out)


def quantise_x(nc, T, W, bank, xn, codes, peaks, scales):
    NG = codes.shape[1]
    with ExitStack() as stack:
        core = Core(nc, stack)
        c = core.sb("fq_codes", [P, 4, P], F32)
        xq = core.sb("fq_x", [P, 512], F32)
        hi = core.sb("fq_x_hi", [P, 2, 512], F32R)
        lo = core.sb("fq_x_lo", [P, 2, 512], F32R)
        scaled = core.sem("fq_scaled")
        rounded = core.sem("fq_rounded")
        turned = core.sem("fq_turned")
        kept = core.sem("fq_codes_kept")
        xq_ready = core.sem("fq_x_ready")
        hi_ready = core.sem("fq_hi_ready")
        lo_ready = core.sem("fq_lo_ready")
        product_done = core.sem("fq_product_done")
        peak_done = core.sem("fq_peak_done")
        TURN, OUT = bank[0], bank[1:7]
        step_x, inverse_x = scales["x"]
        block = stack.enter_context(nc.Block())

        @block.vector
        def _(dve):
            def step(b, n, p):
                if n is not None:
                    wait(dve, turned, n)
                    nc.vector.tensor_scalar(c[:, :, :], xn[:, bass.ds(4 * n, 4), :], inverse_x[:, :], ROUND, ALU.mult, ALU.add).then_inc(scaled, 1)
                    dve.wait_ge(scaled, n + 1)
                    nc.vector.tensor_scalar(c[:, :, :], c[:, :, :], -ROUND, None, ALU.add).then_inc(rounded, 1)
                    dve.wait_ge(kept, n + 1)
                    wait(dve, hi_ready, n)
                    wait(dve, lo_ready, n)
                    nc.vector.tensor_scalar(xq[:, :], TURN[:, :], step_x[:, :], None, ALU.mult).then_inc(xq_ready, 1)
                    dve.wait_ge(hi_ready, n + 1)
                    nc.vector.tensor_tensor(lo[:, 1 - p, :], xq[:, :], hi[:, 1 - p, :].bitcast(F32), ALU.subtract).then_inc(lo_ready, 1)
                if b is not None:
                    for j in range(6):
                        dve.wait_ge(product_done, 6 * b + j + 1)
                        nc.vector.tensor_reduce(peaks[:, b, j:j + 1], OUT[j][:, :], AX.X, ALU.max, apply_absolute_value=True).then_inc(peak_done, 1)
            pipelined(dve, NG, step)

        @block.scalar
        def _(act):
            def step(b, n, p):
                if n is not None:
                    act.wait_ge(turned, n + 1)
                    nc.scalar.copy(codes[:, n, :], TURN[:, :]).then_inc(kept, 1)
                    act.wait_ge(xq_ready, n + 1)
                    if b is not None:
                        wait(act, product_done, 6 * b)
                    nc.scalar.copy(hi[:, 1 - p, :], xq[:, :]).then_inc(hi_ready, 1)
            pipelined(act, NG, step)

        @block.tensor
        def _(pe):
            def step(b, n, p):
                if n is not None:
                    pe.wait_ge(rounded, n + 1)
                    wait(pe, xq_ready, n)
                    for k in range(4):
                        mm = pe.transpose(TURN[:, k * P:(k + 1) * P], c[:, k, :], T["ident"][:, :])
                    mm.then_inc(turned, 1)
                if b is not None:
                    pe.wait_ge(lo_ready, b + 1)
                    for j in range(6):
                        wait(pe, peak_done, 6 * b)
                        k, m = divmod(j, 3)
                        three_products(pe, OUT[j][:, :], (W["gu"][0][:, k, m, :], W["gu"][1][:, k, m, :]),
                                       (hi[:, p, :], lo[:, p, :]), True, True).then_inc(product_done, 1)
            pipelined(pe, NG, step)


def gate_and_up(nc, T, W, bank, codes, spare, peaks, scales, gated, up, round_col):
    NG = codes.shape[1]
    with ExitStack() as stack:
        core = Core(nc, stack)
        xq = core.sb("fg_x", [P, 512], F32)
        hi = core.sb("fg_x_hi", [P, 2, 512], F32R)
        lo = core.sb("fg_x_lo", [P, 2, 512], F32R)
        tg, tu, gate, sig = (spare[:, k, :, :] for k in range(4))
        sigr = core.sb("fg_sigmoid_rounded", [P, 2, 512], F32)
        xq_ready = core.sem("fg_x_ready")
        hi_ready = core.sem("fg_hi_ready")
        lo_ready = core.sem("fg_lo_ready")
        gate_done = core.sem("fg_gate_done")
        up_done = core.sem("fg_up_done")
        tg_ready = core.sem("fg_gate_scaled_ready")
        tu_ready = core.sem("fg_up_scaled_ready")
        gate_ready = core.sem("fg_gate_ready")
        sig_ready = core.sem("fg_sigmoid_ready")
        scaled_ready = core.sem("fg_sigmoid_scaled")
        rounded_ready = core.sem("fg_sigmoid_rounded")
        up_ready = core.sem("fg_up_ready")
        gated_ready = core.sem("fg_gated_ready")
        GATE, UP = bank[0:2], bank[2:4]
        block = stack.enter_context(nc.Block())

        @block.vector
        def _(dve):
            def restore(n, q):
                wait(dve, hi_ready, n)
                wait(dve, lo_ready, n)
                nc.vector.tensor_scalar(xq[:, :], codes[:, n, :], scales["x"][0][:, :], None, ALU.mult).then_inc(xq_ready, 1)
                dve.wait_ge(hi_ready, n + 1)
                nc.vector.tensor_tensor(lo[:, q, :], xq[:, :], hi[:, q, :].bitcast(F32), ALU.subtract).then_inc(lo_ready, 1)

            def chunk(g, j, k, p):
                dve.wait_ge(tg_ready, k + 1)
                nc.vector.tensor_scalar(gate[:, p, :], tg[:, p, :], -ROUND, scales["gate"][0][:, :], ALU.add, ALU.mult).then_inc(gate_ready, 1)
                dve.wait_ge(tu_ready, k + 1)
                nc.vector.tensor_scalar(up[:, k, :], tu[:, p, :], -ROUND, None, ALU.add).then_inc(up_ready, 1)

            def finish(g, j, k, p):
                dve.wait_ge(scaled_ready, k + 1)
                nc.vector.tensor_scalar(sigr[:, p, :], sigr[:, p, :], -ROUND, 65535.0, ALU.add, ALU.min).then_inc(rounded_ready, 1)
                dve.wait_ge(rounded_ready, k + 1)
                nc.vector.scalar_tensor_tensor(gated[:, k, :], sigr[:, p, :], 1.0 / 65536.0, gate[:, p, :], ALU.mult, ALU.mult).then_inc(gated_ready, 1)
                dve.wait_ge(gated_ready, k + 1)
                nc.vector.tensor_reduce(peaks[:, g, j:j + 1], gated[:, k, :], AX.X, ALU.max, apply_absolute_value=True)

            def group(g, more, half):
                for j in range(3):
                    k = 3 * g + j
                    p = (j + half) % 2
                    chunk(g, j, k, p)
                    if j:
                        finish(g, j - 1, k - 1, 1 - p)
                    if j == 1 and more:
                        restore(g + 1, 1 - half)
                finish(g, 2, 3 * g + 2, half)

            restore(0, 0)
            if NG > 2:
                with dve.Fori(0, (NG - 2) // 2) as i:
                    group(2 * i, True, 0)
                    group(2 * i + 1, True, 1)
            group(NG - 2, True, 0)
            group(NG - 1, False, 1)

        @block.scalar
        def _(act):
            nc.scalar.preload_act_table(ACT.Sigmoid)
            act_round = round_col[:, :]

            def split(n, q):
                act.wait_ge(xq_ready, n + 1)
                wait(act, up_done, 3 * (n - 1))
                nc.scalar.copy(hi[:, q, :], xq[:, :]).then_inc(hi_ready, 1)

            def chunk(g, j, k, p):
                act.wait_ge(gate_done, k + 1)
                wait(act, gate_ready, k - 1 if j else 3 * g)
                nc.scalar.activation(tg[:, p, :], GATE[p][:, :], ACT.Identity, bias=act_round, scale=scales["gate"][1][:, :]).then_inc(tg_ready, 1)
                act.wait_ge(up_done, k + 1)
                wait(act, up_ready, k - 1 if j else 3 * g)
                nc.scalar.activation(tu[:, p, :], UP[p][:, :], ACT.Identity, bias=act_round, scale=scales["up"][1][:, :]).then_inc(tu_ready, 1)
                act.wait_ge(gate_ready, k + 1)
                nc.scalar.activation(sig[:, p, :], gate[:, p, :], ACT.Sigmoid).then_inc(sig_ready, 1)
                act.wait_ge(sig_ready, k + 1)
                wait(act, gated_ready, k - 1 if j else 3 * g)
                nc.scalar.activation(sigr[:, p, :], sig[:, p, :], ACT.Identity, bias=act_round, scale=65536.0).then_inc(scaled_ready, 1)

            def group(g, more, half):
                for j in range(3):
                    chunk(g, j, 3 * g + j, (j + half) % 2)
                    if j == 1 and more:
                        split(g + 1, 1 - half)

            split(0, 0)
            if NG > 2:
                with act.Fori(0, (NG - 2) // 2) as i:
                    group(2 * i, True, 0)
                    group(2 * i + 1, True, 1)
            group(NG - 2, True, 0)
            group(NG - 1, False, 1)

        @block.tensor
        def _(pe):
            def group(g, half):
                pe.wait_ge(lo_ready, g + 1)
                for j in range(3):
                    k = 3 * g + j
                    p = (j + half) % 2
                    x_parts = (hi[:, half, :], lo[:, half, :])
                    wait(pe, tg_ready, k - 1 if j else 3 * g)
                    three_products(pe, GATE[p][:, :], (W["gu"][0][:, 0, j, :], W["gu"][1][:, 0, j, :]), x_parts, True, True).then_inc(gate_done, 1)
                    wait(pe, tu_ready, k - 1 if j else 3 * g)
                    three_products(pe, UP[p][:, :], (W["gu"][0][:, 1, j, :], W["gu"][1][:, 1, j, :]), x_parts, True, True).then_inc(up_done, 1)
            if NG > 2:
                with pe.Fori(0, (NG - 2) // 2) as i:
                    group(2 * i, 0)
                    group(2 * i + 1, 1)
            group(NG - 2, 0)
            group(NG - 1, 1)


def multiply_up(nc, peaks, scales, gated, up, round_col):
    NK = gated.shape[1]
    with ExitStack() as stack:
        core = Core(nc, stack)
        t = core.sb("fm_scaled", [P, 2, 512], F32)
        q = core.sb("fm_gated", [P, 2, 512], F32)
        t_ready = core.sem("fm_scaled_ready")
        q_ready = core.sem("fm_gated_ready")
        o_ready = core.sem("fm_o_ready")
        block = stack.enter_context(nc.Block())

        @block.scalar
        def _(act):
            nc.scalar.preload_act_table(ACT.Identity)
            with act.Fori(0, NK // 6) as g:
                for j in range(6):
                    k = 6 * g + j
                    act.wait_ge(q_ready, k - 1 if j else 6 * g)
                    nc.scalar.activation(t[:, j % 2, :], gated[:, k, :], ACT.Identity, bias=round_col[:, :], scale=scales["gated"][1][:, :]).then_inc(t_ready, 1)

        @block.vector
        def _(dve):
            with dve.Fori(0, NK // 6) as g:
                for j in range(6):
                    k = 6 * g + j
                    dve.wait_ge(t_ready, k + 1)
                    nc.vector.tensor_scalar(q[:, j % 2, :], t[:, j % 2, :], -ROUND, scales["gated"][0][:, :], ALU.add, ALU.mult).then_inc(q_ready, 1)
                    dve.wait_ge(q_ready, k + 1)
                    nc.vector.scalar_tensor_tensor(gated[:, k, :], up[:, k, :], scales["up"][0][:, :], q[:, j % 2, :], ALU.mult, ALU.mult).then_inc(o_ready, 1)
                    dve.wait_ge(o_ready, k + 1)
                    nc.vector.tensor_reduce(peaks[:, 2 * g + j // 3, j % 3:j % 3 + 1], gated[:, k, :], AX.X, ALU.max, apply_absolute_value=True)


def project(nc, dram, W, bank, scales, o, spare, round_col, out):
    NG = o.shape[1] // 3
    with ExitStack() as stack:
        core = Core(nc, stack)
        t = core.sb("fp_scaled", [P, 3, 512], F32)
        q = core.sb("fp_o", [P, 2, 3, 512], F32)
        y, x = (spare[:, k, :, :].rearrange("p k (b c) -> p k b c", b=4) for k in range(2))
        t_ready = core.sem("fp_scaled_ready")
        q_ready = core.sem("fp_o_ready")
        y_done = core.sem("fp_y_done")
        sum_ready = core.sem("fp_sum_ready")
        stored = [core.sem(f"fp_stored{k}") for k in range(2)]
        x_in = [core.sem(f"fp_x_in{k}") for k in range(2)]
        Y = bank[0:2]
        block = stack.enter_context(nc.Block())

        @block.scalar
        def _(act):
            nc.scalar.preload_act_table(ACT.Identity)
            with act.Fori(0, NG // 2) as i:
                for s in range(2):
                    g = 2 * i + s
                    for j in range(3):
                        act.wait_ge(q_ready, 3 * g)
                        nc.scalar.activation(t[:, j, :], o[:, 3 * g + j, :], ACT.Identity, bias=round_col[:, :], scale=scales["o"][1][:, :]).then_inc(t_ready, 1)

        @block.vector
        def _(dve):
            def quantised(n, p):
                wait(dve, y_done, n - 1)
                for j in range(3):
                    dve.wait_ge(t_ready, 3 * n + j + 1)
                    nc.vector.tensor_scalar(q[:, p, j, :], t[:, j, :], -ROUND, scales["o"][0][:, :], ALU.add, ALU.mult).then_inc(q_ready, 1)

            def add(b, p, turn):
                dve.wait_ge(y_done, b + 1)
                wait(dve, stored[p], turn)
                dve.wait_ge(x_in[p], turn + 16)
                nc.vector.tensor_tensor(y[:, p, :, :], Y[p][:, :].rearrange("p (k c) -> p k c", k=4), x[:, p, :, :], ALU.add).then_inc(sum_ready, 1)

            quantised(0, 0)
            quantised(1, 1)
            add(0, 0, 0)
            if NG > 2:
                with dve.Fori(1, NG // 2) as i:
                    quantised(2 * i, 0)
                    add(2 * i - 1, 1, 16 * i - 16)
                    quantised(2 * i + 1, 1)
                    add(2 * i, 0, 16 * i)
            add(NG - 1, 1, 16 * (NG // 2 - 1))

        @block.tensor
        def _(pe):
            with pe.Fori(0, NG // 2) as i:
                for p in range(2):
                    g = 2 * i + p
                    pe.wait_ge(q_ready, 3 * g + 3)
                    pe.wait_ge(sum_ready, g if p == 0 else 2 * i)
                    for k in range(4):
                        for j in range(3):
                            mm = pe.matmul(Y[p][:, k * P:(k + 1) * P], q[:, p, j, k * P:(k + 1) * P], W["down"][:, j, :],
                                           start=(j == 0), stop=(j == 2))
                    mm.then_inc(y_done, 1)

        @block.sync
        def _(sp):
            rows = lambda t, g: t[bass.ds(4 * g, 4)].rearrange("b t c -> t b c")

            def load(g, p):
                sp.dma_start(x[:, p, :, :], rows(dram["x_parked"], g)).then_inc(x_in[p], 16)

            def store(g, p):
                sp.wait_ge(sum_ready, g + 1)
                sp.dma_start(rows(out, g), y[:, p, :, :]).then_inc(stored[p], 16)

            load(0, 0)
            load(1, 1)
            if NG > 2:
                with sp.Fori(0, NG // 2 - 1) as i:
                    for p in range(2):
                        store(2 * i + p, p)
                        load(2 * i + 2 + p, p)
            store(NG - 2, 0)
            store(NG - 1, 1)
            for p in range(2):
                sp.wait_ge(stored[p], 16 * (NG // 2))


def build(nc, dram, out, stop_after=9):
    NB = dram["x"].shape[0]
    with ExitStack() as top:
        core = Core(nc, top)
        bank = [top.enter_context(nc.psum_tensor(f"bank{k}", [P, 512], F32)) for k in range(8)]
        T = {
            "batches": NB,
            "x": core.sb("x", [P, max(NB, 64), P], F32),
            "ident": core.sb("ident", [P, P], F32),
            "identb": core.sb("identb", [P, P], BF16),
            "x_stats": core.sb("x_stats", [P, NB, 6], F32),
            "ctx_stats": core.sb("ctx_stats", [P, NB, 6], F32),
            "mean": core.sb("x_mean", [P, NB, 1], F32),
            "ctx_mean": core.sb("ctx_mean", [P, NB, 1], F32),
            "rstd": core.sb("x_rstd", [P, NB, 1], F32),
            "ctx_rstd": core.sb("ctx_rstd", [P, NB, 1], F32),
        }
        with ExitStack() as mid:
            core = Core(nc, mid)
            T.update({
                "headmask": core.sb("headmask", [P, 4], F32),
                "groupmask": core.sb("groupmask", [P, 4], F32),
                "tri": core.sb("tri", [P, 4, 4], F32),
                "blockstart": core.sb("blockstart", [P, 64], F32),
                "expert_rows": core.sb("expert_rows", [16, 4, P], F32),
                "onerow": core.sb("onerow", [P, 16, P], BF16),
                "onerow_f": core.sb("onerow_f", [P, P], F32),
                "wv": (core.sb("wv_hi", [P, 1024], F32R), core.sb("wv_lo", [P, 1024], F32R)),
                "gate_up": (core.sb("gate_up_hi", [P, 2, 6, P], F32R), core.sb("gate_up_lo", [P, 2, 6, P], F32R)),
                "down": core.sb("down", [P, 6, P], F32),
                "router": core.sb("router", [P, 16], F32),
                "router_bias": core.sb("router_bias", [P, 16], F32),
                "w_out0": core.sb("w_out0", [P, P], F32),
                "bout_row": core.sb("bout_row", [P, P], F32),
                "w_out1": core.sb("w_out1", [P, 8, P], F32),
                "ln_cols": core.sb("ln_cols", [P, 4], F32),
                "m": core.sb("wq_wk", [P, 16, P], F32),
            })
            load_and_prepare(nc, top, dram, T, bank)
            x_rows = (T["x_stats"], T["mean"], T["rstd"], P)
            ctx_rows = (T["ctx_stats"], T["ctx_mean"], T["ctx_rstd"], 77)
            row_scales(nc, "rows0", [x_rows + (False,)])
            if stop_after >= 1:
                attention0(nc, dram, T, bank)
            if stop_after >= 2:
                row_scales(nc, "rows1", [x_rows + (False,)])
                ffn0(nc, T, bank)
            if stop_after >= 3:
                row_scales(nc, "rows2", [x_rows + (True,), ctx_rows + (False,)])
                attention1(nc, dram, T, bank)
        if stop_after >= 4:
            row_scales(nc, "rows3", [x_rows + (False,)])
            ffn1(nc, dram, T, bank, out)
            return
        with ExitStack() as s:
            done = s.enter_context(nc.semaphore("dump"))
            blk = s.enter_context(nc.Block())

            @blk.sync
            def _(sp):
                sp.dma_start(out.rearrange("b t c -> t b c"), T["x"][:, :, :]).then_inc(done, 16)
                sp.wait_ge(done, 16)


def kernel(**inputs):
    import numpy as _np
    import concourse.bacc as _bacc
    from concourse import mybir as _mybir
    from concourse.bass_utils import run_bass_kernel_spmd as _run

    a = {k: _np.asarray(v) for k, v in inputs.items()}
    nb = a["x"].shape[0]
    rows = _np.arange(128)
    tri = _np.tril(_np.ones((4, 4), _np.float32), -1)
    start = (_np.arange(64) % 16 != 0).astype(_np.float32)
    by_c = lambda w: w.transpose(1, 0, 2).reshape(128, 512)
    arrays = {
        "x": a["x"], "ctx": a["ctx_1024"], "mask": a["mask_Bx1xSxS2_ik1"].reshape(nb, 128, 77),
        "w_out0": a["L0_xattn_w_out"].T, "b_out0": a["L0_xattn_b_out"],
        "router": a["L0_ffn_router_w"].T, "router_bias": a["L0_ffn_correction_bias"],
        "gate_up": _np.concatenate([a["L0_ffn_shared_gate_w"].T, by_c(a["L0_ffn_gate_w"]),
                                    a["L0_ffn_shared_up_w"].T, by_c(a["L0_ffn_up_w"])], axis=1),
        "down": _np.concatenate([a["L0_ffn_shared_down_w"].T, a["L0_ffn_down_w"].reshape(512, 128)], axis=0),
        "ln_cols": _np.stack([a["L1_xattn_ln_l_g"], a["L1_xattn_ln_l_b"], a["L1_xattn_ln_m_g"], a["L1_xattn_ln_m_b"]], axis=1),
        "wq": a["L1_xattn_Wq"].T, "wk": a["L1_xattn_Wkv"][:, :1024].T, "wv": a["L1_xattn_Wkv"][:, 1024:],
        "w_out1": a["L1_xattn_Wout"],
        "w_gate": a["L1_ffn_w_gate"], "w_up": a["L1_ffn_w_up"], "w_down": a["L1_ffn_w_down"],
        "ident": _np.eye(128, dtype=_np.float32),
        "headmask": (rows[:, None] // 8 % 4 == _np.arange(4)[None, :]).astype(_np.float32),
        "groupmask": (rows[:, None] // 32 == _np.arange(4)[None, :]).astype(_np.float32),
        "tri": _np.ascontiguousarray(_np.broadcast_to(tri, (128, 4, 4))),
        "blockstart": _np.ascontiguousarray(_np.broadcast_to(start, (128, 64))),
        "expert_rows": _np.stack([(_np.arange(16)[:, None] == 4 * j + rows[None, :] // 32) for j in range(4)], axis=1).astype(_np.float32),
    }
    arrays = {k: _np.ascontiguousarray(v) for k, v in arrays.items()}
    nc = _bacc.Bacc("TRN2", target_bir_lowering=False, num_devices=1)
    dram = {k: nc.dram_tensor(f"in_{k}", v.shape, _mybir.dt.from_np(v.dtype), kind="ExternalInput").ap() for k, v in arrays.items()}
    out = nc.dram_tensor("out_x", (nb, 128, 128), _mybir.dt.from_np(_np.dtype("float32")), kind="ExternalOutput").ap()
    dram["x_parked"] = nc.dram_tensor("x_parked", (nb, 128, 128), _mybir.dt.float32, kind="Internal").ap()
    build(nc, dram, out)
    r = _run(nc, [{f"in_{k}": v for k, v in arrays.items()}], core_ids=[0])
    return r.results[0]["out_x"]
```

```python
from contextlib import ExitStack

import numpy as np
import concourse.bass as bass
from concourse import mybir

F32 = mybir.dt.float32
F32R = mybir.dt.float32r
BF16 = mybir.dt.bfloat16
I32 = mybir.dt.int32
I16 = mybir.dt.int16
ALU = mybir.AluOpType
ACT = mybir.ActivationFunctionType
AX = mybir.AxisListType
RMAX = bass.bass_isa.ReduceOp.max

P = 128
EPS = 1e-5
MASKED = -(2.0 ** 73)
ROUND = 1.5 * 2.0 ** 23


def wait(eng, sem, value):
    if not isinstance(value, int) or value > 0:
        eng.wait_ge(sem, value)


def three_products(pe, out, a, b, start, stop):
    pe.matmul(out, a[0], b[0], start=start, stop=False)
    pe.matmul(out, a[0], b[1], start=False, stop=False)
    return pe.matmul(out, a[1], b[0], start=False, stop=stop)


def pipelined(eng, n, step):
    step(None, 0, 1)
    step(0, 1, 0)
    step(1, 2, 1)
    if n > 4:
        with eng.Fori(1, (n - 2) // 2) as i:
            step(2 * i, 2 * i + 1, 0)
            step(2 * i + 1, 2 * i + 2, 1)
    step(n - 2, n - 1, 0)
    step(n - 1, None, 1)


def pipelined_deep(eng, n, step):
    step(None, None, 0, 1, 1)
    step(None, 0, 1, 2, 0)
    step(0, 1, 2, 3, 1)
    if n > 4:
        with eng.Fori(1, n // 2 - 1) as i:
            step(2 * i - 1, 2 * i, 2 * i + 1, 2 * i + 2, 0)
            step(2 * i, 2 * i + 1, 2 * i + 2, 2 * i + 3, 1)
    step(n - 3, n - 2, n - 1, None, 0)
    step(n - 2, n - 1, None, None, 1)
    step(n - 1, None, None, None, 0)


class Core:

    def __init__(self, nc, stack):
        self.nc, self.stack = nc, stack

    def sb(self, name, shape, dt):
        return self.stack.enter_context(self.nc.sbuf_tensor(name, shape, dt))

    def sem(self, name):
        return self.stack.enter_context(self.nc.semaphore(name))


def load_and_prepare(nc, top, dram, T, bank):
    NB = T["batches"]
    with ExitStack() as stack:
        core = Core(nc, stack)
        wq = core.sb("wq_by_dim", [64, 16, P], F32)
        wk = core.sb("wk_by_dim", [64, 16, P], F32)
        wv = core.sb("wv_raw", [P, 1024], F32)
        gu = core.sb("gate_up_raw", [P, 2, 6, P], F32)
        x_in = core.sem("x_in")
        w_in = core.sem("weights_in")
        wv_hi = core.sem("wv_hi_done")
        gu_hi = core.sem("gate_up_hi_done")
        qk_done = core.sem("qk_products_done")
        qk_kept = core.sem("qk_products_kept")
        zeroed = core.sem("zeroed")
        prepared = core.sem("prepared")

        weights = [(T["ident"], dram["ident"]), (T["headmask"], dram["headmask"]), (T["groupmask"], dram["groupmask"]),
                   (T["tri"], dram["tri"]), (T["expert_rows"], dram["expert_rows"]), (T["blockstart"], dram["blockstart"]),
                   (wq, dram["wq"].rearrange("(h d) c -> d h c", d=64)), (wk, dram["wk"].rearrange("(h d) c -> d h c", d=64)),
                   (wv, dram["wv"]), (gu, dram["gate_up"].rearrange("c (s j h) -> c s j h", s=2, j=6)),
                   (T["down"], dram["down"].rearrange("(j h) c -> h j c", h=P)), (T["router"], dram["router"]),
                   (T["w_out0"], dram["w_out0"]), (T["w_out1"], dram["w_out1"].rearrange("(j d) c -> d j c", d=P)),
                   (T["bout_row"][0:1, :], dram["b_out0"].unsqueeze(0)),
                   (T["router_bias"], dram["router_bias"].partition_broadcast(P)),
                   (T["ln_cols"], dram["ln_cols"])]

        block = stack.enter_context(nc.Block())

        @block.sync
        def _(sp):
            q = NB // 4
            for k in range(4):
                sp.dma_start(T["x"][:, k * q:(k + 1) * q, :],
                             dram["x"][k * q:(k + 1) * q].rearrange("b t c -> t b c")).then_inc(x_in, 16)

        @block.scalar
        def _(act):
            act.wait_ge(zeroed, 1)
            for dst, src in weights:
                act.dma_start(dst[tuple(slice(None) for _ in dst.shape)], src).then_inc(w_in, 16)
            act.wait_ge(w_in, 16 * len(weights))
            nc.scalar.copy(T["wv"][0][:, :], wv[:, :]).then_inc(wv_hi, 1)
            nc.scalar.copy(T["gate_up"][0][:, :, :, :], gu[:, :, :, :]).then_inc(gu_hi, 1)
            for k in range(4):
                act.wait_ge(qk_done, k + 1)
                nc.scalar.copy(T["m"][:, 4 * k:4 * k + 4, :], bank[k][:, :].rearrange("p (h c) -> p h c", h=4)).then_inc(qk_kept, 1)
            act.wait_ge(prepared, 1)

        @block.tensor
        def _(pe):
            pe.wait_ge(w_in, 16 * len(weights))
            for h in range(16):
                mm = pe.matmul(bank[h // 4][:, (h % 4) * P:(h % 4 + 1) * P], wq[:, h, :], wk[:, h, :], start=True, stop=True)
                if h % 4 == 3:
                    mm.then_inc(qk_done, 1)

        @block.gpsimd
        def _(pool):
            nc.gpsimd.memset(T["bout_row"][:, :], 0.0).then_inc(zeroed, 1)

        @block.vector
        def _(dve):
            dve.wait_ge(w_in, 16 * len(weights))
            nc.vector.tensor_copy(T["identb"][:, :], T["ident"][:, :])
            nc.vector.tensor_copy(T["onerow"][:, :, :], T["ident"][:, 0:16].unsqueeze(2).to_broadcast([P, 16, P]))
            nc.vector.tensor_copy(T["onerow_f"][:, :], T["ident"][:, 0:1].to_broadcast([P, P]))
            dve.wait_ge(wv_hi, 1)
            nc.vector.tensor_tensor(T["wv"][1][:, :], wv[:, :], T["wv"][0][:, :].bitcast(F32), ALU.subtract)
            dve.wait_ge(gu_hi, 1)
            nc.vector.tensor_tensor(T["gate_up"][1][:, :, :, :], gu[:, :, :, :], T["gate_up"][0][:, :, :, :].bitcast(F32),
                                    ALU.subtract).then_inc(prepared, 1)
            dve.wait_ge(x_in, 64)
            with dve.Fori(0, NB) as b:
                nc.vector.bn_stats(T["x_stats"][:, b, :], T["x"][:, b, :])


def row_scales(nc, name, jobs):
    with ExitStack() as stack:
        core = Core(nc, stack)
        n = jobs[0][1].shape[1]
        mean_gap = core.sb(name + "_mean_gap", [P, n], F32)
        var = core.sb(name + "_var", [P, n], F32)
        root = core.sb(name + "_root", [P, n], F32)
        first = core.sb(name + "_first", [P, n], F32)
        step = core.sem(name + "_vector_step")
        var_ready = core.sem(name + "_var_ready")
        rooted = core.sem(name + "_rooted")
        block = stack.enter_context(nc.Block())

        @block.vector
        def _(dve):
            steps, roots = 0, 0

            def then(instruction):
                nonlocal steps
                instruction.then_inc(step, 1)
                steps += 1
                dve.wait_ge(step, steps)

            for stats, mean, rstd, p, twice in jobs:
                gap, v, r, f, m = mean_gap[0:p, :], var[0:p, :], root[0:p, :], first[0:p, :], mean[0:p, :, 0]
                then(nc.vector.tensor_tensor(gap, stats[0:p, :, 1], stats[0:p, :, 4], ALU.subtract))
                then(nc.vector.tensor_tensor(gap, gap, gap, ALU.mult))
                then(nc.vector.tensor_tensor(m, stats[0:p, :, 1], stats[0:p, :, 4], ALU.add))
                then(nc.vector.tensor_scalar(m, m, 0.5, None, ALU.mult))
                then(nc.vector.tensor_tensor(v, stats[0:p, :, 2], stats[0:p, :, 5], ALU.add))
                then(nc.vector.tensor_scalar(gap, gap, 0.25, EPS, ALU.mult, ALU.add))
                then(nc.vector.scalar_tensor_tensor(v, v, 1.0 / P, gap, ALU.mult, ALU.add))
                nc.vector.tensor_scalar(v, v, 0.0, None, ALU.add).then_inc(var_ready, 1)
                roots += 1
                dve.wait_ge(rooted, roots)
                if not twice:
                    then(nc.vector.reciprocal(rstd[0:p, :, 0], r))
                    continue
                then(nc.vector.reciprocal(f, r))
                then(nc.vector.tensor_scalar(v, v, -EPS, None, ALU.add))
                then(nc.vector.tensor_tensor(v, v, f, ALU.mult))
                then(nc.vector.tensor_tensor(v, v, f, ALU.mult))
                nc.vector.tensor_scalar(v, v, EPS, None, ALU.add).then_inc(var_ready, 1)
                roots += 1
                dve.wait_ge(rooted, roots)
                then(nc.vector.reciprocal(r, r))
                then(nc.vector.tensor_tensor(rstd[0:p, :, 0], r, f, ALU.mult))

        @block.scalar
        def _(act):
            roots = 0
            for stats, mean, rstd, p, twice in jobs:
                for _ in range(1 + twice):
                    roots += 1
                    act.wait_ge(var_ready, roots)
                    nc.scalar.activation(root[0:p, :], var[0:p, :], ACT.Sqrt).then_inc(rooted, 1)


def attention0(nc, dram, T, bank):
    NB = T["batches"]
    S = 77
    SP = 78
    D = 128
    SCALE = float(1.0 / np.sqrt(np.float32(D)))
    with ExitStack() as stack:
        core = Core(nc, stack)
        ctx = core.sb("a0_ctx", [S, 2, D], F32)
        mask = core.sb("a0_mask", [P, 2, S], I32)
        maskb = core.sb("a0_mask_bias", [P, 2, S], BF16)
        xn = core.sb("a0_xn", [P, D], F32)
        q_hi = core.sb("a0_q_hi", [P, 2, 4, P], F32R)
        q_lo = core.sb("a0_q_lo", [P, 2, 4, P], F32R)
        q_f = core.sb("a0_q_f", [P, 4, P], F32)
        k_hi = core.sb("a0_k_hi", [P, 2, 4 * SP], F32R)
        k_lo = core.sb("a0_k_lo", [P, 2, 4 * SP], F32R)
        k_f = core.sb("a0_k_f", [P, 4 * SP], F32)
        v1 = core.sb("a0_v_and_one", [S, 2, 16, 9], F32)
        ones = core.sb("a0_ones", [S, 16, 8], F32)
        negmax = core.sb("a0_negmax", [P, 16], F32)
        shift = core.sb("a0_shift", [P, 2, P], BF16)
        probs = core.sb("a0_probs", [S, 2, 512], F32)
        rden = core.sb("a0_rden", [P, 16], F32)
        o = core.sb("a0_o", [P, D], F32)
        oT = core.sb("a0_oT", [P, P], F32)

        ctx_in = [core.sem(f"a0_ctx_in{k}") for k in range(2)]
        mask_in = [core.sem(f"a0_mask_in{k}") for k in range(2)]
        zeroed = core.sem("a0_zeroed")
        mask_ready = core.sem("a0_mask_ready")
        v_ready = core.sem("a0_v_ready")
        xn_ready = core.sem("a0_xn_ready")
        qk_turned = core.sem("a0_qk_turned")
        blocked = core.sem("a0_blocked")
        hi_ready = core.sem("a0_hi_ready")
        lo_ready = core.sem("a0_lo_ready")
        rough_done = core.sem("a0_rough_done")
        max_done = core.sem("a0_max_done")
        max_turned = core.sem("a0_max_turned")
        shift_ready = core.sem("a0_shift_ready")
        scores_done = core.sem("a0_scores_done")
        exp_done = core.sem("a0_exp_done")
        av_done = core.sem("a0_av_done")
        rden_done = core.sem("a0_rden_done")
        o_ready = core.sem("a0_o_ready")
        o_turned = core.sem("a0_o_turned")
        oT_ready = core.sem("a0_oT_ready")
        y_done = core.sem("a0_y_done")
        x_ready = core.sem("a0_x_ready")
        ctx_stat_done = core.sem("a0_ctx_stat_done")

        TURN, MAXT, YT = bank[0], bank[1], bank[2]
        ROUGH, SCORES, AV = bank[3:5], bank[5:7], bank[7]
        block = stack.enter_context(nc.Block())

        @block.sync
        def _(sp):
            def load(b, k, first):
                if not first:
                    wait(sp, v_ready, b - 1)
                    wait(sp, ctx_stat_done, b - 1)
                    wait(sp, qk_turned, b - 1)
                    wait(sp, mask_ready, b - 1)
                sp.dma_start(ctx[:, k, :], dram["ctx"][b]).then_inc(ctx_in[k], 16)
                sp.dma_start(mask[:, k, :], dram["mask"][b]).then_inc(mask_in[k], 16)
            load(0, 0, True)
            load(1, 1, True)
            with sp.Fori(1, NB // 2) as pair:
                b = 2 * pair
                load(b, 0, False)
                load(b + 1, 1, False)

        @block.gpsimd
        def _(pool):
            nc.gpsimd.memset(v1[:, :, :, :], 1.0).then_inc(zeroed, 1)
            nc.gpsimd.memset(shift[:, :, :], 0.0).then_inc(zeroed, 1)
            nc.gpsimd.memset(k_f[:, :], 0.0).then_inc(zeroed, 1)
            nc.gpsimd.memset(ones[:, :, :], 1.0).then_inc(zeroed, 1)
            pool.wait_ge(zeroed, 4)

            def prepare(b, k, turn):
                pool.wait_ge(ctx_in[k], turn)
                wait(pool, av_done, 4 * (b - 1))
                nc.gpsimd.tensor_tensor(v1[:, k, :, 0:8], ctx[:, k, :].rearrange("s (h d) -> s h d", h=16),
                                        ones[:, :, :], ALU.mult).then_inc(v_ready, 1)
            prepare(0, 0, 16)
            prepare(1, 1, 16)
            with pool.Fori(1, NB // 2) as pair:
                for k in range(2):
                    prepare(2 * pair + k, k, 16 * pair + 16)

        @block.vector
        def _(dve):
            dve.wait_ge(zeroed, 3)

            def normal_rows(t):
                wait(dve, qk_turned, t)
                nc.vector.tensor_scalar(xn[:, :], T["x"][:, t, :], T["mean"][:, t, :], T["rstd"][:, t, :], ALU.subtract, ALU.mult).then_inc(xn_ready, 1)

            def block_rows(t):
                dve.wait_ge(qk_turned, t + 1)
                wait(dve, lo_ready, 2 * t)
                wait(dve, hi_ready, 2 * t)
                nc.vector.tensor_tensor(q_f[:, :, :], TURN[:, 0:P].unsqueeze(1).to_broadcast([P, 4, P]),
                                        T["headmask"][:, :].unsqueeze(2).to_broadcast([P, 4, P]), ALU.mult).then_inc(blocked, 1)
                nc.vector.tensor_tensor(k_f[:, :].rearrange("p (g s) -> p g s", g=4)[:, :, 0:S],
                                        TURN[:, P:P + S].unsqueeze(1).to_broadcast([P, 4, S]),
                                        T["groupmask"][:, :].unsqueeze(2).to_broadcast([P, 4, S]), ALU.mult).then_inc(blocked, 1)

            def mask_and_split(t, p, b):
                wait(dve, mask_in[p], t * 8 + 16 - 8 * p)
                if b is not None:
                    dve.wait_ge(scores_done, 4 * b + 4)
                nc.vector.tensor_scalar(maskb[:, p, :], mask[:, p, :], 0.0, MASKED, ALU.is_equal, ALU.mult).then_inc(mask_ready, 1)
                dve.wait_ge(hi_ready, 2 * t + 1)
                nc.vector.tensor_tensor(q_lo[:, p, :, :], q_f[:, :, :], q_hi[:, p, :, :].bitcast(F32), ALU.subtract).then_inc(lo_ready, 1)
                dve.wait_ge(hi_ready, 2 * t + 2)
                nc.vector.tensor_tensor(k_lo[:, p, :], k_f[:, :], k_hi[:, p, :].bitcast(F32), ALU.subtract).then_inc(lo_ready, 1)

            def ctx_statistics(t, p):
                wait(dve, ctx_in[p], t * 8 + 16 - 8 * p)
                nc.vector.bn_stats(T["ctx_stats"][0:S, t, :], ctx[:, p, :]).then_inc(ctx_stat_done, 1)

            def keep_max(n, i):
                dve.wait_ge(rough_done, 4 * n + i + 1)
                if i == 0:
                    wait(dve, max_turned, n)
                nc.vector.tensor_reduce(negmax[:, 4 * i:4 * i + 4], ROUGH[i % 2][:, 0:4 * SP].rearrange("p (g s) -> p g s", g=4)[:, :, 0:S],
                                        AX.X, ALU.max, negate=True).then_inc(max_done, 1)

            def step(late, b, n, t, p):
                if t is not None:
                    normal_rows(t)
                    ctx_statistics(t, p)
                if n is not None:
                    keep_max(n, 0)
                    keep_max(n, 1)
                if late is not None:
                    dve.wait_ge(y_done, late + 1)
                    nc.vector.tensor_tensor(T["x"][:, late, :], TURN[:, 384:512], T["x"][:, late, :], ALU.add).then_inc(x_ready, 1)
                if t is not None:
                    block_rows(t)
                if n is not None:
                    keep_max(n, 2)
                if late is not None:
                    dve.wait_ge(x_ready, late + 1)
                    nc.vector.bn_stats(T["x_stats"][:, late, :], T["x"][:, late, :])
                if n is not None:
                    keep_max(n, 3)
                if t is not None:
                    mask_and_split(t, p, b)
                if b is not None:
                    dve.wait_ge(av_done, 4 * b + 4)
                    av = AV[:, 0:144].rearrange("p (h d) -> p h d", h=16)
                    nc.vector.reciprocal(rden[:, :], av[:, :, 8]).then_inc(rden_done, 1)
                    dve.wait_ge(rden_done, b + 1)
                    wait(dve, o_turned, b)
                    nc.vector.tensor_tensor(o[:, :].rearrange("p (h d) -> p h d", h=16), av[:, :, 0:8],
                                            rden[:, :].unsqueeze(2).to_broadcast([P, 16, 8]), ALU.mult).then_inc(o_ready, 1)
            normal_rows(0)
            ctx_statistics(0, 0)
            block_rows(0)
            mask_and_split(0, 0, None)
            pipelined_deep(dve, NB, step)

        @block.scalar
        def _(act):
            nc.scalar.preload_act_table(ACT.Exp)
            act.wait_ge(zeroed, 3)

            def exponential(b, g):
                act.wait_ge(scores_done, 4 * b + g + 1)
                wait(act, av_done, 4 * b + g - 1 if g else 4 * b)
                nc.scalar.activation(probs[:, g % 2, :], SCORES[g % 2][0:S, :], ACT.Exp, scale=SCALE).then_inc(exp_done, 1)

            def high_rows(t, b, p):
                act.wait_ge(blocked, 2 * t + 1)
                if b is not None:
                    act.wait_ge(scores_done, 4 * b + 4)
                nc.scalar.copy(q_hi[:, p, :, :], q_f[:, :, :]).then_inc(hi_ready, 1)
                act.wait_ge(blocked, 2 * t + 2)
                nc.scalar.copy(k_hi[:, p, :], k_f[:, :]).then_inc(hi_ready, 1)

            def step(late, b, n, t, p):
                if b is not None:
                    exponential(b, 0)
                if late is not None:
                    act.wait_ge(o_turned, late + 1)
                    wait(act, y_done, late)
                    nc.scalar.copy(oT[:, :], YT[:, 0:P]).then_inc(oT_ready, 1)
                if b is not None:
                    for g in range(1, 4):
                        exponential(b, g)
                if t is not None:
                    high_rows(t, b, p)
                if n is not None:
                    act.wait_ge(max_turned, n + 1)
                    nc.scalar.copy(shift[0:16, 1 - p, :], MAXT[0:16, 0:P]).then_inc(shift_ready, 1)
            high_rows(0, None, 0)
            pipelined_deep(act, NB, step)

        @block.tensor
        def _(pe):
            pe.wait_ge(zeroed, 3)
            keep = T["identb"][:, :].unsqueeze(1).to_broadcast([P, 4, P])

            def turn_rows(t, p):
                pe.wait_ge(xn_ready, t + 1)
                pe.wait_ge(ctx_in[p], t * 8 + 16 - 8 * p)
                wait(pe, x_ready, t - 2)
                pe.transpose(TURN[:, 0:P], xn[:, :], T["ident"][:, :])
                pe.transpose(TURN[:, P:P + S], ctx[:, p, :], T["ident"][0:S, 0:S]).then_inc(qk_turned, 1)

            def score(b, g, p):
                wait(pe, exp_done, 4 * b + g - 1 if g else 4 * b)
                if g == 0:
                    pe.wait_ge(lo_ready, 2 * b + 2)
                kg = slice(g * SP, g * SP + S)
                three_products(pe, SCORES[g % 2][0:S, :], (k_hi[:, p, kg], k_lo[:, p, kg]),
                               (q_hi[:, p, :, :], q_lo[:, p, :, :]), True, False)
                pe.matmul(SCORES[g % 2][0:S, :], maskb[:, p, :], keep, start=False, stop=False)
                if g == 0:
                    pe.wait_ge(shift_ready, b + 1)
                for i in range(4):
                    mm = pe.matmul(SCORES[g % 2][0:S, i * P:(i + 1) * P], T["onerow"][:, 4 * i + g, 0:S],
                                   shift[:, p, :], start=False, stop=(i == 3))
                mm.then_inc(scores_done, 1)

            def rough(n, i, q):
                if i == 0:
                    pe.wait_ge(hi_ready, 2 * n + 2)
                    pe.wait_ge(mask_ready, n + 1)
                wait(pe, max_done, 4 * n + i - 1 if i else 4 * n)
                pe.matmul(ROUGH[i % 2][:, 0:4 * SP], q_hi[:, q, i, :], k_hi[:, q, :], start=True, stop=False)
                pe.matmul(ROUGH[i % 2][:, 0:4 * SP].rearrange("p (g s) -> p g s", g=4)[:, :, 0:S], T["identb"][:, :],
                          maskb[:, q, :].unsqueeze(1).to_broadcast([P, 4, S]), start=False, stop=True).then_inc(rough_done, 1)

            def weigh(b, g, p):
                pe.wait_ge(exp_done, 4 * b + g + 1)
                if g == 0:
                    wait(pe, o_ready, b)
                    pe.wait_ge(v_ready, b + 1)
                for i in range(4):
                    h = 4 * g + i
                    mm = pe.matmul(AV[:, 9 * h:9 * h + 9], probs[:, g % 2, i * P:(i + 1) * P], v1[:, p, h, :], start=True, stop=True)
                mm.then_inc(av_done, 1)

            def step(late, b, n, t, p):
                q = 1 - p
                if b is not None:
                    score(b, 0, p)
                if late is not None:
                    pe.wait_ge(o_ready, late + 1)
                    wait(pe, oT_ready, late)
                    pe.transpose(YT[:, 0:P], o[:, :], T["ident"][:, :]).then_inc(o_turned, 1)
                if n is not None:
                    rough(n, 0, q)
                if b is not None:
                    score(b, 1, p)
                if n is not None:
                    rough(n, 1, q)
                if late is not None:
                    pe.wait_ge(oT_ready, late + 1)
                    if n is not None:
                        pe.wait_ge(blocked, 2 * n + 2)
                    pe.matmul(TURN[:, 384:512], T["onerow_f"][:, :], T["bout_row"][:, :], start=True, stop=False)
                    pe.matmul(TURN[:, 384:512], oT[:, :], T["w_out0"][:, :], start=False, stop=True).then_inc(y_done, 1)
                if b is not None:
                    weigh(b, 0, p)
                    score(b, 2, p)
                if t is not None:
                    turn_rows(t, p)
                if n is not None:
                    rough(n, 2, q)
                if b is not None:
                    weigh(b, 1, p)
                    score(b, 3, p)
                if n is not None:
                    rough(n, 3, q)
                if b is not None:
                    weigh(b, 2, p)
                if n is not None:
                    pe.wait_ge(max_done, 4 * n + 4)
                    wait(pe, shift_ready, n)
                    pe.transpose(MAXT[0:16, 0:P], negmax[:, :], T["ident"][:, :]).then_inc(max_turned, 1)
                if b is not None:
                    weigh(b, 3, p)
            turn_rows(0, 0)
            pipelined_deep(pe, NB, step)


def ffn0(nc, T, bank):
    NB = T["batches"]
    NG = NB // 4
    BIG = 1e30
    with ExitStack() as stack:
        core = Core(nc, stack)
        xT_all = core.sb("f0_xT_all", [P, NG, 512], F32)
        above = core.sb("f0_weight", [P, NB, 16], F32)
        share = core.sb("f0_share", [P, NB, 1], F32)
        with ExitStack() as s:
            route_all(nc, Core(nc, s), T, bank, xT_all, above, share)

        rows_r = core.sb("f0_expert_rows_r", [16, 4, P], F32R)
        xT_hi = core.sb("f0_xT_hi", [P, 2, 512], F32R)
        xT_lo = core.sb("f0_xT_lo", [P, 2, 512], F32R)
        combine = core.sb("f0_combine", [P, 4, 16], F32)
        combT_hi = core.sb("f0_combT_hi", [16, 2, 512], F32R)
        combT_lo = core.sb("f0_combT_lo", [16, 2, 512], F32R)
        gate = core.sb("f0_gate_sigmoid", [P, 2, 512], F32)
        silu = core.sb("f0_silu", [P, 512], F32)
        hidden = core.sb("f0_hidden", [P, 2, 6, 512], F32)

        rows_ready = core.sem("f0_expert_rows_ready")
        hi_ready = core.sem("f0_hi_ready")
        lo_ready = core.sem("f0_lo_ready")
        comb_ready = core.sem("f0_comb_ready")
        comb_turned = core.sem("f0_comb_turned")
        comb_hi_ready = core.sem("f0_comb_hi_ready")
        comb_lo_ready = core.sem("f0_comb_lo_ready")
        gate_done = core.sem("f0_gate_done")
        up_done = core.sem("f0_up_done")
        spread_done = core.sem("f0_spread_done")
        sigmoid_done = core.sem("f0_sigmoid_done")
        silu_done = core.sem("f0_silu_done")
        hidden_done = core.sem("f0_hidden_done")
        weighed_done = core.sem("f0_weighed_done")
        y_done = core.sem("f0_y_done")
        x_ready = core.sem("f0_x_ready")

        COMB, GATE, UP, SPREAD, Y = bank[0], bank[2:4], bank[4:6], bank[6], bank[7]
        block = stack.enter_context(nc.Block())

        @block.vector
        def _(dve):
            def hide(b, j, p):
                dve.wait_ge(sigmoid_done, 6 * b + j + 1)
                wait(dve, hidden_done, 6 * b + j)
                nc.vector.tensor_tensor(silu[:, :], GATE[j % 2][:, :], gate[:, j % 2, :], ALU.mult).then_inc(silu_done, 1)
                dve.wait_ge(silu_done, 6 * b + j + 1)
                dve.wait_ge(up_done, 6 * b + j + 1)
                if j == 0:
                    wait(dve, y_done, b - 1)
                nc.vector.tensor_tensor(hidden[:, p, j, :], UP[j % 2][:, :], silu[:, :], ALU.mult).then_inc(hidden_done, 1)
                if j >= 2:
                    dve.wait_ge(hidden_done, 6 * b + j + 1)
                    dve.wait_ge(spread_done, 4 * b + j - 1)
                    nc.vector.tensor_tensor(hidden[:, p, j, :], SPREAD[:, :], hidden[:, p, j, :], ALU.mult).then_inc(weighed_done, 1)

            def step(late, b, n, t, p):
                q = 1 - p
                if n is not None:
                    wait(dve, comb_turned, n)
                    nc.vector.tensor_tensor(combine[:, :, :], above[:, bass.ds(4 * n, 4), :],
                                            share[:, bass.ds(4 * n, 4), :].to_broadcast([P, 4, 16]), ALU.mult).then_inc(comb_ready, 1)
                if b is not None:
                    hide(b, 0, p)
                    hide(b, 1, p)
                if n is not None:
                    dve.wait_ge(hi_ready, n + 1)
                    nc.vector.tensor_tensor(xT_lo[:, q, :], xT_all[:, n, :], xT_hi[:, q, :].bitcast(F32), ALU.subtract).then_inc(lo_ready, 1)
                if b is not None:
                    hide(b, 2, p)
                    hide(b, 3, p)
                if n is not None:
                    dve.wait_ge(comb_hi_ready, n + 1)
                    nc.vector.tensor_tensor(combT_lo[:, q, :], COMB[0:16, :], combT_hi[:, q, :].bitcast(F32), ALU.subtract).then_inc(comb_lo_ready, 1)
                if b is not None:
                    hide(b, 4, p)
                    hide(b, 5, p)
                if late is not None:
                    dve.wait_ge(y_done, late + 1)
                    for k in range(4):
                        nc.vector.tensor_tensor(T["x"][:, 4 * late + k, :], Y[:, k * P:(k + 1) * P], T["x"][:, 4 * late + k, :], ALU.add).then_inc(x_ready, 1)
                    for k in range(4):
                        dve.wait_ge(x_ready, 4 * late + k + 1)
                        nc.vector.bn_stats(T["x_stats"][:, 4 * late + k, :], T["x"][:, 4 * late + k, :])
            pipelined_deep(dve, NG, step)

        @block.scalar
        def _(act):
            nc.scalar.preload_act_table(ACT.Sigmoid)
            nc.scalar.copy(rows_r[:, :, :], T["expert_rows"][:, :, :]).then_inc(rows_ready, 1)

            def sigmoid(b, j):
                act.wait_ge(gate_done, 6 * b + j + 1)
                wait(act, silu_done, 6 * b + j - 1 if j else 6 * b)
                nc.scalar.activation(gate[:, j % 2, :], GATE[j % 2][:, :], ACT.Sigmoid).then_inc(sigmoid_done, 1)

            def step(late, b, n, t, p):
                q = 1 - p
                if b is not None:
                    sigmoid(b, 0)
                    sigmoid(b, 1)
                if n is not None:
                    if b is not None:
                        wait(act, up_done, 6 * b)
                    nc.scalar.copy(xT_hi[:, q, :], xT_all[:, n, :]).then_inc(hi_ready, 1)
                if b is not None:
                    sigmoid(b, 2)
                if n is not None:
                    act.wait_ge(comb_turned, n + 1)
                    if b is not None:
                        wait(act, spread_done, 4 * b)
                    nc.scalar.copy(combT_hi[:, q, :], COMB[0:16, :]).then_inc(comb_hi_ready, 1)
                if b is not None:
                    sigmoid(b, 3)
                    sigmoid(b, 4)
                    sigmoid(b, 5)
            pipelined_deep(act, NG, step)

        @block.tensor
        def _(pe):
            gu_hi, gu_lo = T["gate_up"]
            pe.wait_ge(rows_ready, 1)

            def expand(b, j, p):
                if j == 0:
                    pe.wait_ge(lo_ready, b + 1)
                x_parts = (xT_hi[:, p, :], xT_lo[:, p, :])
                wait(pe, silu_done, 6 * b + j - 1 if j else 6 * b)
                three_products(pe, GATE[j % 2][:, :], (gu_hi[:, 0, j, :], gu_lo[:, 0, j, :]), x_parts, True, True).then_inc(gate_done, 1)
                wait(pe, hidden_done, 6 * b + j - 1 if j else 6 * b)
                three_products(pe, UP[j % 2][:, :], (gu_hi[:, 1, j, :], gu_lo[:, 1, j, :]), x_parts, True, True).then_inc(up_done, 1)
                if j >= 2:
                    if j == 2:
                        pe.wait_ge(comb_lo_ready, b + 1)
                    wait(pe, weighed_done, 4 * b + j - 2)
                    pe.matmul(SPREAD[:, :], rows_r[:, j - 2, :], combT_hi[:, p, :], start=True, stop=False)
                    pe.matmul(SPREAD[:, :], rows_r[:, j - 2, :], combT_lo[:, p, :], start=False, stop=True).then_inc(spread_done, 1)

            def down(b, k, p):
                if k == 0:
                    pe.wait_ge(hidden_done, 6 * b + 6)
                    pe.wait_ge(weighed_done, 4 * b + 4)
                    wait(pe, x_ready, 4 * b)
                for j in range(6):
                    mm = pe.matmul(Y[:, k * P:(k + 1) * P], hidden[:, p, j, k * P:(k + 1) * P], T["down"][:, j, :],
                                   start=(j == 0), stop=(j == 5))
                if k == 3:
                    mm.then_inc(y_done, 1)

            def step(late, b, n, t, p):
                for j in range(6):
                    if b is not None:
                        expand(b, j, p)
                    if late is not None and 1 <= j <= 4:
                        down(late, j - 1, 1 - p)
                    if n is not None and j == 1:
                        pe.wait_ge(comb_ready, n + 1)
                        wait(pe, comb_lo_ready, n)
                        for k in range(4):
                            mm = pe.transpose(COMB[0:16, k * P:(k + 1) * P], combine[:, k, :], T["ident"][:, :])
                        mm.then_inc(comb_turned, 1)
            pipelined_deep(pe, NG, step)


def route_all(nc, core, T, bank, xT_all, above, share):
    NB = T["batches"]
    NG = NB // 4
    BIG = 1e30
    xn = core.sb("fr_xn", [P, 2, 4, P], F32)
    xT = core.sb("fr_xT", [P, 2, 512], F32)
    score = core.sb("fr_score", [P, NB, 16], F32)
    biased = core.sb("fr_biased", [P, NB, 16], F32)
    hi2 = core.sb("fr_pair_max", [P, 4 * NB, 2], F32)
    lo2 = core.sb("fr_pair_min", [P, 4 * NB, 2], F32)
    best = core.sb("fr_best", [P, 4 * NB], F32)
    second = core.sb("fr_second", [P, 4 * NB], F32)
    third = core.sb("fr_third", [P, 4 * NB], F32)
    over = core.sb("fr_over", [P, NB, 4, 4], F32)
    tie = core.sb("fr_tie", [P, NB, 4, 4], F32)
    left = core.sb("fr_left", [P, NB, 16], F32)
    top8 = core.sb("fr_top8", [P, NB, 8], F32)
    xn_ready = core.sem("fr_xn_ready")
    turned = core.sem("fr_turned")
    xT_ready = core.sem("fr_xT_ready")
    xT_kept = core.sem("fr_xT_kept")
    logits_done = core.sem("fr_logits_done")
    score_ready = core.sem("fr_score_ready")
    route_step = core.sem("fr_route_step")
    TURN, LOGITS = bank[0:2], bank[2:4]
    with nc.Block() as block:

        @block.scalar
        def _(act):
            nc.scalar.preload_act_table(ACT.Sigmoid)

            def step(b, n, p):
                q = 1 - p
                if n is not None:
                    act.wait_ge(turned, n + 1)
                    wait(act, logits_done, n - 1)
                    nc.scalar.copy(xT[:, q, :], TURN[q][:, :]).then_inc(xT_ready, 1)
                    nc.scalar.copy(xT_all[:, n, :], TURN[q][:, :]).then_inc(xT_kept, 1)
                if b is not None:
                    act.wait_ge(logits_done, b + 1)
                    nc.scalar.activation(score[:, bass.ds(4 * b, 4), :].rearrange("p b e -> p (b e)"),
                                         LOGITS[p][:, 0:64], ACT.Sigmoid).then_inc(score_ready, 1)
            pipelined(act, NG, step)

        @block.tensor
        def _(pe):
            def step(b, n, p):
                q = 1 - p
                if n is not None:
                    pe.wait_ge(xn_ready, 4 * n + 4)
                    wait(pe, xT_kept, n - 1)
                    for k in range(4):
                        mm = pe.transpose(TURN[q][:, k * P:(k + 1) * P], xn[:, q, k, :], T["ident"][:, :])
                    mm.then_inc(turned, 1)
                if b is not None:
                    pe.wait_ge(xT_ready, b + 1)
                    wait(pe, score_ready, b - 1)
                    for k in range(4):
                        mm = pe.matmul(LOGITS[p][:, 16 * k:16 * k + 16], xT[:, p, k * P:(k + 1) * P], T["router"][:, :], start=True, stop=True)
                    mm.then_inc(logits_done, 1)
            pipelined(pe, NG, step)

        @block.vector
        def _(dve):
            def step(b, n, p):
                if n is not None:
                    wait(dve, turned, n - 1)
                    for k in range(4):
                        nc.vector.tensor_scalar(xn[:, 1 - p, k, :], T["x"][:, 4 * n + k, :], T["mean"][:, 4 * n + k, :],
                                                T["rstd"][:, 4 * n + k, :], ALU.subtract, ALU.mult).then_inc(xn_ready, 1)
            pipelined(dve, NG, step)

            steps = 0

            def then(instruction):
                nonlocal steps
                instruction.then_inc(route_step, 1)
                steps += 1

            def settled():
                dve.wait_ge(route_step, steps)

            V = nc.vector
            wide = [P, NB, 16]
            dve.wait_ge(score_ready, NG)
            then(V.tensor_tensor(biased[:, :, :], score[:, :, :], T["router_bias"][:, :].unsqueeze(1).to_broadcast(wide), ALU.add))
            settled()
            pairs = biased[:, :, :].rearrange("p b (g e t) -> p (b g) e t", g=4, e=2)
            then(V.tensor_tensor(hi2[:, :, :], pairs[:, :, :, 0], pairs[:, :, :, 1], ALU.max))
            then(V.tensor_tensor(lo2[:, :, :], pairs[:, :, :, 0], pairs[:, :, :, 1], ALU.min))
            settled()
            then(V.tensor_tensor(best[:, :], hi2[:, :, 0], hi2[:, :, 1], ALU.max))
            then(V.tensor_tensor(second[:, :], hi2[:, :, 0], hi2[:, :, 1], ALU.min))
            then(V.tensor_tensor(third[:, :], lo2[:, :, 0], lo2[:, :, 1], ALU.max))
            settled()
            then(V.tensor_tensor(second[:, :], second[:, :], third[:, :], ALU.max))
            settled()
            then(V.tensor_tensor(best[:, :], best[:, :], second[:, :], ALU.add))
            settled()
            sums = best[:, :].rearrange("p (b g) -> p b g", g=4)
            mine = sums.unsqueeze(3).to_broadcast([P, NB, 4, 4])
            other = sums.unsqueeze(2).to_broadcast([P, NB, 4, 4])
            tri = T["tri"][:, :, :].unsqueeze(1).to_broadcast([P, NB, 4, 4])
            then(V.tensor_tensor(over[:, :, :, :], other, mine, ALU.is_gt))
            then(V.tensor_tensor(tie[:, :, :, :], other, mine, ALU.is_equal))
            settled()
            then(V.tensor_tensor(tie[:, :, :, :], tie[:, :, :, :], tri, ALU.mult))
            settled()
            then(V.tensor_tensor(over[:, :, :, :], over[:, :, :, :], tie[:, :, :, :], ALU.add))
            settled()
            rank, penalty = second, third
            then(V.tensor_reduce(rank[:, :], over[:, :, :, :], AX.X, ALU.add))
            settled()
            then(V.tensor_scalar(rank[:, :], rank[:, :], 2.0, None, ALU.is_lt))
            settled()
            then(V.tensor_scalar(penalty[:, :], rank[:, :], BIG, -BIG, ALU.mult, ALU.add))
            kept = rank[:, :].unsqueeze(2).to_broadcast([P, 4 * NB, 4])
            left16 = left[:, :, :].rearrange("p b (g e) -> p (b g) e", g=4)
            then(V.tensor_tensor(left16, biased[:, :, :].rearrange("p b (g e) -> p (b g) e", g=4), kept, ALU.mult))
            settled()
            then(V.tensor_tensor(left16, left16, penalty[:, :].unsqueeze(2).to_broadcast([P, 4 * NB, 4]), ALU.add))
            settled()
            V.memset(share[:, 0, :], 0.0)
            for b in range(NB):
                then(V.max(top8[:, b, :], left[:, b, :]))
            settled()
            equal = over[:, :, :, :].rearrange("p b i j -> p b (i j)")
            place = tie[:, :, :, :].rearrange("p b i j -> p b (i j)")
            fourth = top8[:, :, 3:4].to_broadcast(wide)
            then(V.tensor_tensor(above[:, :, :], left[:, :, :], fourth, ALU.is_gt))
            then(V.tensor_tensor(equal, left[:, :, :], fourth, ALU.is_equal))
            settled()
            then(V.tensor_reduce(share[:, :, 0], above[:, :, :], AX.X, ALU.add))
            then(V.tensor_tensor_scan(place.rearrange("p b e -> p (b e)"), T["blockstart"][:, 0:16 * NB],
                                      equal.rearrange("p b e -> p (b e)"), 0.0, ALU.mult, ALU.add))
            settled()
            then(V.tensor_tensor(place, place, share[:, :, :].to_broadcast(wide), ALU.add))
            settled()
            then(V.scalar_tensor_tensor(equal, place, 4.0, equal, ALU.is_le, ALU.mult))
            settled()
            then(V.tensor_tensor(above[:, :, :], above[:, :, :], equal, ALU.add))
            settled()
            then(V.tensor_tensor(above[:, :, :], above[:, :, :], score[:, :, :], ALU.mult))
            settled()
            then(V.tensor_reduce(share[:, :, 0], above[:, :, :], AX.X, ALU.add))
            settled()
            then(V.tensor_scalar(share[:, :, 0], share[:, :, 0], 1e-20, None, ALU.add))
            settled()
            then(V.reciprocal(share[:, :, 0], share[:, :, 0]))


def attention1(nc, dram, T, bank):
    NB = T["batches"]
    S = 77
    BLOCKS = ((0, P), (P, S))
    J = P + S
    SCALE = 64 ** -0.5
    with ExitStack() as stack:
        core = Core(nc, stack)
        ctx = core.sb("a1_ctx", [S, 2, P], F32)
        xn = core.sb("a1_xn", [P, P], F32)
        cn = core.sb("a1_cn", [S, P], F32)
        kv = core.sb("a1_kv", [P, 256], F32)
        kv_hi = core.sb("a1_kv_hi", [P, 2, 256], F32R)
        kv_lo = core.sb("a1_kv_lo", [P, 2, 256], F32R)
        g_hi = core.sb("a1_g_hi", [P, 2, 16 * P], F32R)
        g_lo = core.sb("a1_g_lo", [P, 2, 16 * P], F32R)
        v1 = core.sb("a1_v_and_one", [P, 2, 2, 16, 65], F32)
        negmax = core.sb("a1_negmax", [P, 16], F32)
        shift = core.sb("a1_shift", [P, 2, P], BF16)
        probs = core.sb("a1_probs", [P, 2, 2, 512], F32)
        rden = core.sb("a1_rden", [P, 4], F32)
        o = core.sb("a1_o", [P, 16, 64], F32)
        oT = core.sb("a1_oT", [P, 8, P], F32)

        ctx_in = [core.sem(f"a1_ctx_in{k}") for k in range(2)]
        zeroed = core.sem("a1_zeroed")
        cn_ready = core.sem("a1_cn_ready")
        xn_ready = core.sem("a1_xn_ready")
        turned = core.sem("a1_turned")
        kv_ready = core.sem("a1_kv_ready")
        kv_hi_ready = core.sem("a1_kv_hi_ready")
        kv_lo_ready = core.sem("a1_kv_lo_ready")
        v_done = core.sem("a1_v_done")
        v_kept = core.sem("a1_v_kept")
        g_done = core.sem("a1_g_done")
        g_hi_ready = core.sem("a1_g_hi_ready")
        g_lo_ready = core.sem("a1_g_lo_ready")
        rough_done = core.sem("a1_rough_done")
        max_done = core.sem("a1_max_done")
        max_turned = core.sem("a1_max_turned")
        shift_ready = core.sem("a1_shift_ready")
        scores_done = core.sem("a1_scores_done")
        exp_done = core.sem("a1_exp_done")
        av_done = core.sem("a1_av_done")
        rden_done = core.sem("a1_rden_done")
        o_ready = core.sem("a1_o_ready")
        o_turned = core.sem("a1_o_turned")
        oT_ready = core.sem("a1_oT_ready")
        y_done = core.sem("a1_y_done")
        x_ready = core.sem("a1_x_ready")

        TURN, GB, VB, ROUGH, SCORES, AV = bank[0], bank[1], bank[2], bank[3:5], bank[5:7], bank[7]
        block = stack.enter_context(nc.Block())

        @block.sync
        def _(sp):
            sp.dma_start(ctx[:, 0, :], dram["ctx"][0]).then_inc(ctx_in[0], 16)
            sp.dma_start(ctx[:, 1, :], dram["ctx"][1]).then_inc(ctx_in[1], 16)
            with sp.Fori(1, NB // 2) as pair:
                for k in range(2):
                    sp.wait_ge(cn_ready, 2 * pair + k - 1)
                    sp.dma_start(ctx[:, k, :], dram["ctx"][2 * pair + k]).then_inc(ctx_in[k], 16)

        @block.gpsimd
        def _(pool):
            nc.gpsimd.memset(v1[:, :, :, :, :], 1.0).then_inc(zeroed, 1)
            nc.gpsimd.memset(shift[:, :, :], 0.0).then_inc(zeroed, 1)
            nc.gpsimd.memset(kv[:, :], 0.0).then_inc(zeroed, 1)

        @block.vector
        def _(dve):
            dve.wait_ge(zeroed, 3)

            def keep_max(n, k):
                dve.wait_ge(rough_done, 8 * n + k + 1)
                if k == 0:
                    wait(dve, max_turned, n)
                nc.vector.tensor_reduce(negmax[:, 2 * k:2 * k + 2], ROUGH[k % 2][:, :].rearrange("p (h j) -> p h j", h=2)[:, :, 0:J],
                                        AX.X, ALU.max, negate=True).then_inc(max_done, 1)

            def normalise(b, c):
                dve.wait_ge(av_done, 4 * b + c + 1)
                av = AV[:, 0:260].rearrange("p (h d) -> p h d", h=4)
                nc.vector.reciprocal(rden[:, :], av[:, :, 64]).then_inc(rden_done, 1)
                dve.wait_ge(rden_done, 4 * b + c + 1)
                if c % 2 == 0:
                    wait(dve, o_turned, 2 * b - 1 + c // 2)
                nc.vector.tensor_tensor(o[:, 4 * c:4 * c + 4, :], av[:, :, 0:64],
                                        rden[:, :].unsqueeze(2).to_broadcast([P, 4, 64]), ALU.mult).then_inc(o_ready, 1)

            def turn_rows(t, p):
                wait(dve, turned, t)
                nc.vector.tensor_scalar(xn[:, :], T["x"][:, t, :], T["mean"][:, t, :], T["rstd"][:, t, :],
                                        ALU.subtract, ALU.mult).then_inc(xn_ready, 1)
                wait(dve, ctx_in[p], t * 8 + 16 - 8 * p)
                nc.vector.tensor_scalar(cn[:, :], ctx[:, p, :], T["ctx_mean"][0:S, t, :], T["ctx_rstd"][0:S, t, :],
                                        ALU.subtract, ALU.mult).then_inc(cn_ready, 1)

            def scale_rows(t):
                dve.wait_ge(turned, t + 1)
                wait(dve, g_done, 4 * t)
                wait(dve, kv_hi_ready, t)
                wait(dve, kv_lo_ready, t)
                for k, (at, length) in enumerate(BLOCKS):
                    nc.vector.tensor_scalar(kv[:, at:at + length], TURN[:, at:at + length], T["ln_cols"][:, 2 * k:2 * k + 1],
                                            T["ln_cols"][:, 2 * k + 1:2 * k + 2], ALU.mult, ALU.add).then_inc(kv_ready, 1)

            def low_rows(t, p):
                dve.wait_ge(kv_hi_ready, t + 1)
                nc.vector.tensor_tensor(kv_lo[:, p, :], kv[:, :], kv_hi[:, p, :].bitcast(F32), ALU.subtract).then_inc(kv_lo_ready, 1)

            def low_queries(n, c, q):
                dve.wait_ge(g_hi_ready, 4 * n + c + 1)
                nc.vector.tensor_tensor(g_lo[:, q, 512 * c:512 * c + 512], GB[:, :], g_hi[:, q, 512 * c:512 * c + 512].bitcast(F32),
                                        ALU.subtract).then_inc(g_lo_ready, 1)

            def step(late, b, n, t, p):
                q = 1 - p
                if t is not None:
                    turn_rows(t, p)
                if n is not None:
                    low_queries(n, 0, q)
                if late is not None:
                    dve.wait_ge(y_done, late + 1)
                    nc.vector.tensor_tensor(T["x"][:, late, :], TURN[:, 384:512], T["x"][:, late, :], ALU.add).then_inc(x_ready, 1)
                    dve.wait_ge(x_ready, late + 1)
                    nc.vector.bn_stats(T["x_stats"][:, late, :], T["x"][:, late, :])
                for c in range(1, 4):
                    if n is not None:
                        low_queries(n, c, q)
                        keep_max(n, 2 * c - 2)
                        keep_max(n, 2 * c - 1)
                    if b is not None:
                        normalise(b, c - 1)
                if n is not None:
                    keep_max(n, 6)
                    keep_max(n, 7)
                if t is not None:
                    scale_rows(t)
                if b is not None:
                    normalise(b, 3)
                if t is not None:
                    low_rows(t, p)
            turn_rows(0, 0)
            scale_rows(0)
            low_rows(0, 0)
            pipelined_deep(dve, NB, step)

        @block.scalar
        def _(act):
            nc.scalar.preload_act_table(ACT.Exp)
            act.wait_ge(zeroed, 3)

            def exponential(b, c, k):
                rows = BLOCKS[k][1]
                act.wait_ge(scores_done, 8 * b + 2 * c + k + 1)
                wait(act, av_done, 4 * b + c - 1 if c else 4 * b)
                nc.scalar.activation(probs[0:rows, c % 2, k, :], SCORES[k][0:rows, :], ACT.Exp, scale=SCALE).then_inc(exp_done, 1)

            def turn_o(b, half):
                act.wait_ge(o_turned, 2 * b + half + 1)
                if half == 0:
                    wait(act, y_done, b)
                nc.scalar.copy(oT[:, 4 * half:4 * half + 4, :], VB[:, :].rearrange("p (k t) -> p k t", k=4)).then_inc(oT_ready, 1)

            def high_rows(t, b, p):
                act.wait_ge(kv_ready, 2 * t + 2)
                if b is not None:
                    act.wait_ge(scores_done, 8 * b + 8)
                nc.scalar.copy(kv_hi[:, p, :], kv[:, :]).then_inc(kv_hi_ready, 1)

            def step(late, b, n, t, p):
                q = 1 - p
                for c in range(4):
                    if b is not None:
                        exponential(b, c, 0)
                        exponential(b, c, 1)
                    if late is not None and c == 0:
                        turn_o(late, 1)
                    if n is not None:
                        k, half = divmod(c, 2)
                        rows = BLOCKS[k][1]
                        act.wait_ge(v_done, 4 * n + c + 1)
                        if b is not None and c == 0:
                            wait(act, av_done, 4 * b)
                        nc.scalar.copy(v1[0:rows, q, k, 8 * half:8 * half + 8, 0:64],
                                       VB[0:rows, :].rearrange("p (h d) -> p h d", h=8)).then_inc(v_kept, 1)
                        act.wait_ge(g_done, 4 * n + c + 1)
                        nc.scalar.copy(g_hi[:, q, 512 * c:512 * c + 512], GB[:, :]).then_inc(g_hi_ready, 1)
                if b is not None:
                    turn_o(b, 0)
                if t is not None:
                    high_rows(t, b, p)
                if n is not None:
                    act.wait_ge(max_turned, n + 1)
                    nc.scalar.copy(shift[0:16, q, :], VB[0:16, 0:P]).then_inc(shift_ready, 1)
            high_rows(0, None, 0)
            pipelined_deep(act, NB, step)

        @block.tensor
        def _(pe):
            pe.wait_ge(zeroed, 3)

            def score(b, c, k, p):
                at, rows = BLOCKS[k]
                wait(pe, exp_done, 8 * b + 2 * c + k - 1 if c else 8 * b)
                out = SCORES[k][0:rows, :]
                three_products(pe, out, (kv_hi[:, p, at:at + rows], kv_lo[:, p, at:at + rows]),
                               (g_hi[:, p, 512 * c:512 * c + 512], g_lo[:, p, 512 * c:512 * c + 512]), True, False)
                if c == 0 and k == 0:
                    pe.wait_ge(shift_ready, b + 1)
                for i in range(4):
                    mm = pe.matmul(out[:, i * P:(i + 1) * P], T["onerow"][:, 4 * c + i, 0:rows], shift[:, p, :], start=False, stop=(i == 3))
                mm.then_inc(scores_done, 1)

            def values(n, c, q):
                k, half = divmod(c, 2)
                at, rows = BLOCKS[k]
                if c == 0:
                    pe.wait_ge(kv_lo_ready, n + 1)
                    wait(pe, oT_ready, 2 * (n - 1))
                else:
                    pe.wait_ge(v_kept, 4 * n + c)
                w = slice(512 * half, 512 * half + 512)
                three_products(pe, VB[0:rows, :], (kv_hi[:, q, at:at + rows], kv_lo[:, q, at:at + rows]),
                               (T["wv"][0][:, w], T["wv"][1][:, w]), True, True).then_inc(v_done, 1)

            def queries(n, c):
                wait(pe, g_lo_ready, 4 * n + c)
                for i in range(4):
                    mm = pe.matmul(GB[:, i * P:(i + 1) * P], T["m"][:, 4 * c + i, :], kv[:, 0:P], start=True, stop=True)
                mm.then_inc(g_done, 1)

            def rough(n, k, q):
                pe.wait_ge(g_hi_ready, 4 * n + k // 2 + 1)
                wait(pe, max_done, 8 * n + max(k - 1, 0))
                for i in range(2):
                    h = 2 * k + i
                    mm = pe.matmul(ROUGH[k % 2][:, 256 * i:256 * i + 256], g_hi[:, q, h * P:(h + 1) * P], kv_hi[:, q, :], start=True, stop=True)
                mm.then_inc(rough_done, 1)

            def weigh(b, c, p):
                pe.wait_ge(exp_done, 8 * b + 2 * c + 2)
                wait(pe, o_ready, 4 * b + c)
                if c == 0:
                    pe.wait_ge(v_kept, 4 * b + 4)
                for i in range(4):
                    for k, (_, rows) in enumerate(BLOCKS):
                        mm = pe.matmul(AV[:, 65 * i:65 * i + 65], probs[0:rows, c % 2, k, i * P:(i + 1) * P],
                                       v1[0:rows, p, k, 4 * c + i, :], start=(k == 0), stop=(k == 1))
                mm.then_inc(av_done, 1)

            def turn_o(b, half, n):
                pe.wait_ge(o_ready, 4 * b + 2 * half + 2)
                if half:
                    pe.wait_ge(shift_ready, n)
                    pe.wait_ge(oT_ready, 2 * b + 1)
                elif n is not None:
                    pe.wait_ge(v_kept, 4 * n + 4)
                else:
                    pe.wait_ge(oT_ready, 2 * b)
                for i in range(4):
                    k = 4 * half + i
                    mm = pe.transpose(VB[:, i * P:(i + 1) * P], o[:, 2 * k:2 * k + 2, :].rearrange("p h d -> p (h d)"), T["ident"][:, :])
                mm.then_inc(o_turned, 1)

            def turn_rows(t):
                pe.wait_ge(xn_ready, t + 1)
                pe.wait_ge(cn_ready, t + 1)
                wait(pe, x_ready, t - 2)
                pe.transpose(TURN[:, 0:P], xn[:, :], T["ident"][:, :])
                pe.transpose(TURN[:, P:J], cn[:, :], T["ident"][0:S, 0:S]).then_inc(turned, 1)

            def step(late, b, n, t, p):
                q = 1 - p
                for c in range(4):
                    if b is not None:
                        score(b, c, 0, p)
                        score(b, c, 1, p)
                    if late is not None and c == 0:
                        turn_o(late, 1, late + 2 if b is not None else NB)
                    if n is not None:
                        values(n, c, q)
                        queries(n, c)
                    if late is not None and c == 0:
                        pe.wait_ge(oT_ready, 2 * late + 2)
                        if n is not None:
                            pe.wait_ge(kv_ready, 2 * n + 2)
                        for k in range(8):
                            mm = pe.matmul(TURN[:, 384:512], oT[:, k, :], T["w_out1"][:, k, :], start=(k == 0), stop=(k == 7))
                        mm.then_inc(y_done, 1)
                    if n is not None and c >= 1:
                        rough(n, 2 * c - 2, q)
                        rough(n, 2 * c - 1, q)
                    if b is not None and c >= 1:
                        weigh(b, c - 1, p)
                if b is not None:
                    turn_o(b, 0, n)
                if n is not None:
                    rough(n, 6, q)
                    rough(n, 7, q)
                if t is not None:
                    turn_rows(t)
                if b is not None:
                    weigh(b, 3, p)
                if n is not None:
                    pe.wait_ge(max_done, 8 * n + 8)
                    if b is not None:
                        pe.wait_ge(oT_ready, 2 * b + 1)
                    else:
                        pe.wait_ge(v_kept, 4 * n + 4)
                    pe.transpose(VB[0:16, 0:P], negmax[:, :], T["ident"][:, :]).then_inc(max_turned, 1)
            turn_rows(0)
            pipelined_deep(pe, NB, step)


def global_scale(nc, name, top, T, parts):
    with ExitStack() as stack:
        core = Core(nc, stack)
        row = core.sb(name + "_row_max", [P, len(parts)], F32)
        every = core.sb(name + "_all_max", [P, len(parts)], F32)
        reduced = core.sem(name + "_reduced")
        spread = core.sem(name + "_spread")
        clamped = core.sem(name + "_clamped")
        block = stack.enter_context(nc.Block())

        @block.vector
        def _(dve):
            for k, (maxima, _, _) in enumerate(parts):
                nc.vector.tensor_reduce(row[:, k:k + 1], maxima, AX.XY if len(maxima.shape) == 3 else AX.X, ALU.max).then_inc(reduced, 1)
            dve.wait_ge(spread, 1)
            for k, (_, step, inverse) in enumerate(parts):
                nc.vector.tensor_scalar(step, every[:, k:k + 1], 1.0 / 32767.0, 1e-12, ALU.mult, ALU.max).then_inc(clamped, 1)
            for k, (_, step, inverse) in enumerate(parts):
                dve.wait_ge(clamped, k + 1)
                nc.vector.reciprocal(inverse, step)

        @block.gpsimd
        def _(pool):
            pool.wait_ge(reduced, len(parts))
            nc.gpsimd.partition_all_reduce(every[:, :], row[:, :], P, RMAX).then_inc(spread, 1)


def quantise_weights(nc, dram, T, W, bank):
    with ExitStack() as stack:
        core = Core(nc, stack)
        raw = [core.sb(f"f1_{n}_raw", [P, 12, 32], F32) for n in ("gate", "up", "down")]
        step = core.sb("f1_weight_step", [P, 3, 12], F32)
        inverse = core.sb("f1_weight_inverse", [P, 3, 12], F32)
        turned = core.sb("f1_weight_turned", [P, 2, 3, P], F32)
        w_in = core.sem("f1_weights_in")
        chain = core.sem("f1_weight_step_done")
        turn_done = core.sem("f1_weight_turn_done")
        kept = core.sem("f1_weight_kept")
        hi_ready = core.sem("f1_weight_hi_ready")
        block = stack.enter_context(nc.Block())

        @block.sync
        def _(sp):
            for k, name in enumerate(("w_gate", "w_up")):
                sp.dma_start(raw[k][:, :, :].rearrange("p (j r) i -> p j (r i)", j=3), dram[name].rearrange("(j p) c -> p j c", p=P)).then_inc(w_in, 16)
            sp.dma_start(raw[2][:, :, :].rearrange("p r i -> p (r i)"), dram["w_down"]).then_inc(w_in, 16)

        @block.vector
        def _(dve):
            steps = 0

            def then(instruction):
                nonlocal steps
                instruction.then_inc(chain, 1)
                steps += 1
                dve.wait_ge(chain, steps)
            dve.wait_ge(w_in, 48)
            for k in range(3):
                w = raw[k][:, :, :]
                wide = lambda t: t[:, k, :].unsqueeze(2).to_broadcast([P, 12, 32])
                then(nc.vector.tensor_reduce(step[:, k, :], w, AX.X, ALU.max, apply_absolute_value=True))
                then(nc.vector.tensor_scalar(step[:, k, :], step[:, k, :], 1.0 / 7.0, 1e-12, ALU.mult, ALU.max))
                then(nc.vector.reciprocal(inverse[:, k, :], step[:, k, :]))
                then(nc.vector.tensor_tensor(w, w, wide(inverse), ALU.mult))
                then(nc.vector.tensor_scalar(w, w, ROUND, -ROUND, ALU.add, ALU.add))
                then(nc.vector.tensor_scalar(w, w, 7.0, -8.0, ALU.min, ALU.max))
                then(nc.vector.tensor_tensor(w, w, wide(step), ALU.mult))
            for k in range(2):
                dve.wait_ge(hi_ready, k + 1)
                nc.vector.tensor_tensor(W["gu"][1][:, k, :, :], turned[:, k, :, :], W["gu"][0][:, k, :, :].bitcast(F32), ALU.subtract)

        @block.tensor
        def _(pe):
            for k in range(3):
                pe.wait_ge(chain, 7 * k + 7)
                for j in range(3):
                    mm = pe.transpose(bank[k][:, j * P:(j + 1) * P], raw[k][:, 4 * j:4 * j + 4, :].rearrange("p r i -> p (r i)"), T["ident"][:, :])
                mm.then_inc(turn_done, 1)

        @block.scalar
        def _(act):
            for k in range(2):
                act.wait_ge(turn_done, k + 1)
                nc.scalar.copy(turned[:, k, :, :], bank[k][:, 0:384].rearrange("p (j c) -> p j c", j=3)).then_inc(kept, 1)
                act.wait_ge(kept, k + 1)
                nc.scalar.copy(W["gu"][0][:, k, :, :], turned[:, k, :, :]).then_inc(hi_ready, 1)
            act.wait_ge(turn_done, 3)
            nc.scalar.copy(W["down"][:, :, :], bank[2][:, 0:384].rearrange("p (j c) -> p j c", j=3))


def ffn1(nc, dram, T, bank, out):
    NB = T["batches"]
    NG = NB // 4
    with ExitStack() as kept:
        core = Core(nc, kept)
        W = {"gu": (core.sb("f1_gate_up_hi", [P, 2, 3, P], F32R), core.sb("f1_gate_up_lo", [P, 2, 3, P], F32R)),
             "down": core.sb("f1_down", [P, 3, P], F32)}
        codes = T["x"][:, 0:NB // 2, :].bitcast(I16).rearrange("p (g b) c -> p g (b c)", b=2)
        spare = T["x"][:, 32:64, :].rearrange("p b c -> p (b c)").rearrange("p (n k c) -> p n k c", n=4, k=2)
        peaks = core.sb("f1_row_peaks", [P, NG, 6], F32)
        scales = {n: (core.sb(f"f1_{n}_step", [P, 1], F32), core.sb(f"f1_{n}_inverse", [P, 1], F32))
                  for n in ("x", "gate", "up", "gated", "o")}
        round_col = core.sb("f1_round", [P, 1], F32)
        quantise_weights(nc, dram, T, W, bank)

        with ExitStack() as stack:
            passing = Core(nc, stack)
            xn = passing.sb("f1_xn", [P, NB, P], F32)
            x_peak = passing.sb("f1_x_peak", [P, NB, 1], F32)
            normal = passing.sem("f1_normal")
            parked = passing.sem("f1_x_parked")
            with ExitStack() as s2:
                block = s2.enter_context(nc.Block())

                @block.gpsimd
                def _(pool):
                    nc.gpsimd.memset(round_col[:, :], ROUND)

                @block.sync
                def _(sp):
                    sp.dma_start(dram["x_parked"].rearrange("b t c -> t b c"), T["x"][:, 0:NB, :]).then_inc(parked, 16)
                    sp.wait_ge(parked, 16)

                @block.vector
                def _(dve):
                    with dve.Fori(0, NB) as b:
                        nc.vector.tensor_scalar(xn[:, b, :], T["x"][:, b, :], T["mean"][:, b, :], T["rstd"][:, b, :],
                                                ALU.subtract, ALU.mult).then_inc(normal, 1)
                        dve.wait_ge(normal, b + 1)
                        nc.vector.tensor_reduce(x_peak[:, b, :], xn[:, b, :], AX.X, ALU.max, apply_absolute_value=True)
            global_scale(nc, "f1_x", kept, T, [(x_peak[:, :, 0], scales["x"][0][:, :], scales["x"][1][:, :])])
            quantise_x(nc, T, W, bank, xn, codes, peaks, scales)
        global_scale(nc, "f1_gu", kept, T, [(peaks[:, :, 0:3], scales["gate"][0][:, :], scales["gate"][1][:, :]),
                                            (peaks[:, :, 3:6], scales["up"][0][:, :], scales["up"][1][:, :])])
        gated = core.sb("f1_gated", [P, NG * 3, 512], F32)
        up = core.sb("f1_up_codes", [P, NG * 3, 512], I16)
        gate_and_up(nc, T, W, bank, codes, spare, peaks, scales, gated, up, round_col)
        global_scale(nc, "f1_gd", kept, T, [(peaks[:, :, 0:3], scales["gated"][0][:, :], scales["gated"][1][:, :])])
        multiply_up(nc, peaks, scales, gated, up, round_col)
        global_scale(nc, "f1_o", kept, T, [(peaks[:, :, 0:3], scales["o"][0][:, :], scales["o"][1][:, :])])
        project(nc, dram, W, bank, scales, gated, spare, round_col, out)


def quantise_x(nc, T, W, bank, xn, codes, peaks, scales):
    NG = codes.shape[1]
    with ExitStack() as stack:
        core = Core(nc, stack)
        c = core.sb("fq_codes", [P, 4, P], F32)
        xq = core.sb("fq_x", [P, 512], F32)
        hi = core.sb("fq_x_hi", [P, 2, 512], F32R)
        lo = core.sb("fq_x_lo", [P, 2, 512], F32R)
        scaled = core.sem("fq_scaled")
        rounded = core.sem("fq_rounded")
        turned = core.sem("fq_turned")
        kept = core.sem("fq_codes_kept")
        xq_ready = core.sem("fq_x_ready")
        hi_ready = core.sem("fq_hi_ready")
        lo_ready = core.sem("fq_lo_ready")
        product_done = core.sem("fq_product_done")
        peak_done = core.sem("fq_peak_done")
        TURN, OUT = bank[0], bank[1:7]
        step_x, inverse_x = scales["x"]
        block = stack.enter_context(nc.Block())

        @block.vector
        def _(dve):
            def step(b, n, p):
                if n is not None:
                    wait(dve, turned, n)
                    nc.vector.tensor_scalar(c[:, :, :], xn[:, bass.ds(4 * n, 4), :], inverse_x[:, :], ROUND, ALU.mult, ALU.add).then_inc(scaled, 1)
                    dve.wait_ge(scaled, n + 1)
                    nc.vector.tensor_scalar(c[:, :, :], c[:, :, :], -ROUND, None, ALU.add).then_inc(rounded, 1)
                    dve.wait_ge(kept, n + 1)
                    wait(dve, hi_ready, n)
                    wait(dve, lo_ready, n)
                    nc.vector.tensor_scalar(xq[:, :], TURN[:, :], step_x[:, :], None, ALU.mult).then_inc(xq_ready, 1)
                    dve.wait_ge(hi_ready, n + 1)
                    nc.vector.tensor_tensor(lo[:, 1 - p, :], xq[:, :], hi[:, 1 - p, :].bitcast(F32), ALU.subtract).then_inc(lo_ready, 1)
                if b is not None:
                    for j in range(6):
                        dve.wait_ge(product_done, 6 * b + j + 1)
                        nc.vector.tensor_reduce(peaks[:, b, j:j + 1], OUT[j][:, :], AX.X, ALU.max, apply_absolute_value=True).then_inc(peak_done, 1)
            pipelined(dve, NG, step)

        @block.scalar
        def _(act):
            def step(b, n, p):
                if n is not None:
                    act.wait_ge(turned, n + 1)
                    nc.scalar.copy(codes[:, n, :], TURN[:, :]).then_inc(kept, 1)
                    act.wait_ge(xq_ready, n + 1)
                    if b is not None:
                        wait(act, product_done, 6 * b)
                    nc.scalar.copy(hi[:, 1 - p, :], xq[:, :]).then_inc(hi_ready, 1)
            pipelined(act, NG, step)

        @block.tensor
        def _(pe):
            def step(b, n, p):
                if n is not None:
                    pe.wait_ge(rounded, n + 1)
                    wait(pe, xq_ready, n)
                    for k in range(4):
                        mm = pe.transpose(TURN[:, k * P:(k + 1) * P], c[:, k, :], T["ident"][:, :])
                    mm.then_inc(turned, 1)
                if b is not None:
                    pe.wait_ge(lo_ready, b + 1)
                    for j in range(6):
                        wait(pe, peak_done, 6 * b)
                        k, m = divmod(j, 3)
                        three_products(pe, OUT[j][:, :], (W["gu"][0][:, k, m, :], W["gu"][1][:, k, m, :]),
                                       (hi[:, p, :], lo[:, p, :]), True, True).then_inc(product_done, 1)
            pipelined(pe, NG, step)


def gate_and_up(nc, T, W, bank, codes, spare, peaks, scales, gated, up, round_col):
    NG = codes.shape[1]
    with ExitStack() as stack:
        core = Core(nc, stack)
        xq = core.sb("fg_x", [P, 512], F32)
        hi = core.sb("fg_x_hi", [P, 2, 512], F32R)
        lo = core.sb("fg_x_lo", [P, 2, 512], F32R)
        tg, tu, gate, sig = (spare[:, k, :, :] for k in range(4))
        sigr = core.sb("fg_sigmoid_rounded", [P, 2, 512], F32)
        xq_ready = core.sem("fg_x_ready")
        hi_ready = core.sem("fg_hi_ready")
        lo_ready = core.sem("fg_lo_ready")
        gate_done = core.sem("fg_gate_done")
        up_done = core.sem("fg_up_done")
        tg_ready = core.sem("fg_gate_scaled_ready")
        tu_ready = core.sem("fg_up_scaled_ready")
        gate_ready = core.sem("fg_gate_ready")
        sig_ready = core.sem("fg_sigmoid_ready")
        scaled_ready = core.sem("fg_sigmoid_scaled")
        rounded_ready = core.sem("fg_sigmoid_rounded")
        up_ready = core.sem("fg_up_ready")
        gated_ready = core.sem("fg_gated_ready")
        GATE, UP = bank[0:2], bank[2:4]
        block = stack.enter_context(nc.Block())

        @block.vector
        def _(dve):
            def restore(n, q):
                wait(dve, hi_ready, n)
                wait(dve, lo_ready, n)
                nc.vector.tensor_scalar(xq[:, :], codes[:, n, :], scales["x"][0][:, :], None, ALU.mult).then_inc(xq_ready, 1)
                dve.wait_ge(hi_ready, n + 1)
                nc.vector.tensor_tensor(lo[:, q, :], xq[:, :], hi[:, q, :].bitcast(F32), ALU.subtract).then_inc(lo_ready, 1)

            def chunk(g, j, k, p):
                dve.wait_ge(tg_ready, k + 1)
                nc.vector.tensor_scalar(gate[:, p, :], tg[:, p, :], -ROUND, scales["gate"][0][:, :], ALU.add, ALU.mult).then_inc(gate_ready, 1)
                dve.wait_ge(tu_ready, k + 1)
                nc.vector.tensor_scalar(up[:, k, :], tu[:, p, :], -ROUND, None, ALU.add).then_inc(up_ready, 1)

            def finish(g, j, k, p):
                dve.wait_ge(scaled_ready, k + 1)
                nc.vector.tensor_scalar(sigr[:, p, :], sigr[:, p, :], -ROUND, 65535.0, ALU.add, ALU.min).then_inc(rounded_ready, 1)
                dve.wait_ge(rounded_ready, k + 1)
                nc.vector.scalar_tensor_tensor(gated[:, k, :], sigr[:, p, :], 1.0 / 65536.0, gate[:, p, :], ALU.mult, ALU.mult).then_inc(gated_ready, 1)
                dve.wait_ge(gated_ready, k + 1)
                nc.vector.tensor_reduce(peaks[:, g, j:j + 1], gated[:, k, :], AX.X, ALU.max, apply_absolute_value=True)

            def group(g, more, half):
                for j in range(3):
                    k = 3 * g + j
                    p = (j + half) % 2
                    chunk(g, j, k, p)
                    if j:
                        finish(g, j - 1, k - 1, 1 - p)
                    if j == 1 and more:
                        restore(g + 1, 1 - half)
                finish(g, 2, 3 * g + 2, half)

            restore(0, 0)
            if NG > 2:
                with dve.Fori(0, (NG - 2) // 2) as i:
                    group(2 * i, True, 0)
                    group(2 * i + 1, True, 1)
            group(NG - 2, True, 0)
            group(NG - 1, False, 1)

        @block.scalar
        def _(act):
            nc.scalar.preload_act_table(ACT.Sigmoid)
            act_round = round_col[:, :]

            def split(n, q):
                act.wait_ge(xq_ready, n + 1)
                wait(act, up_done, 3 * (n - 1))
                nc.scalar.copy(hi[:, q, :], xq[:, :]).then_inc(hi_ready, 1)

            def chunk(g, j, k, p):
                act.wait_ge(gate_done, k + 1)
                wait(act, gate_ready, k - 1 if j else 3 * g)
                nc.scalar.activation(tg[:, p, :], GATE[p][:, :], ACT.Identity, bias=act_round, scale=scales["gate"][1][:, :]).then_inc(tg_ready, 1)
                act.wait_ge(up_done, k + 1)
                wait(act, up_ready, k - 1 if j else 3 * g)
                nc.scalar.activation(tu[:, p, :], UP[p][:, :], ACT.Identity, bias=act_round, scale=scales["up"][1][:, :]).then_inc(tu_ready, 1)
                act.wait_ge(gate_ready, k + 1)
                nc.scalar.activation(sig[:, p, :], gate[:, p, :], ACT.Sigmoid).then_inc(sig_ready, 1)
                act.wait_ge(sig_ready, k + 1)
                wait(act, gated_ready, k - 1 if j else 3 * g)
                nc.scalar.activation(sigr[:, p, :], sig[:, p, :], ACT.Identity, bias=act_round, scale=65536.0).then_inc(scaled_ready, 1)

            def group(g, more, half):
                for j in range(3):
                    chunk(g, j, 3 * g + j, (j + half) % 2)
                    if j == 1 and more:
                        split(g + 1, 1 - half)

            split(0, 0)
            if NG > 2:
                with act.Fori(0, (NG - 2) // 2) as i:
                    group(2 * i, True, 0)
                    group(2 * i + 1, True, 1)
            group(NG - 2, True, 0)
            group(NG - 1, False, 1)

        @block.tensor
        def _(pe):
            def group(g, half):
                pe.wait_ge(lo_ready, g + 1)
                for j in range(3):
                    k = 3 * g + j
                    p = (j + half) % 2
                    x_parts = (hi[:, half, :], lo[:, half, :])
                    wait(pe, tg_ready, k - 1 if j else 3 * g)
                    three_products(pe, GATE[p][:, :], (W["gu"][0][:, 0, j, :], W["gu"][1][:, 0, j, :]), x_parts, True, True).then_inc(gate_done, 1)
                    wait(pe, tu_ready, k - 1 if j else 3 * g)
                    three_products(pe, UP[p][:, :], (W["gu"][0][:, 1, j, :], W["gu"][1][:, 1, j, :]), x_parts, True, True).then_inc(up_done, 1)
            if NG > 2:
                with pe.Fori(0, (NG - 2) // 2) as i:
                    group(2 * i, 0)
                    group(2 * i + 1, 1)
            group(NG - 2, 0)
            group(NG - 1, 1)


def multiply_up(nc, peaks, scales, gated, up, round_col):
    NK = gated.shape[1]
    with ExitStack() as stack:
        core = Core(nc, stack)
        t = core.sb("fm_scaled", [P, 2, 512], F32)
        q = core.sb("fm_gated", [P, 2, 512], F32)
        t_ready = core.sem("fm_scaled_ready")
        q_ready = core.sem("fm_gated_ready")
        o_ready = core.sem("fm_o_ready")
        block = stack.enter_context(nc.Block())

        @block.scalar
        def _(act):
            nc.scalar.preload_act_table(ACT.Identity)
            with act.Fori(0, NK // 6) as g:
                for j in range(6):
                    k = 6 * g + j
                    act.wait_ge(q_ready, k - 1 if j else 6 * g)
                    nc.scalar.activation(t[:, j % 2, :], gated[:, k, :], ACT.Identity, bias=round_col[:, :], scale=scales["gated"][1][:, :]).then_inc(t_ready, 1)

        @block.vector
        def _(dve):
            with dve.Fori(0, NK // 6) as g:
                for j in range(6):
                    k = 6 * g + j
                    dve.wait_ge(t_ready, k + 1)
                    nc.vector.tensor_scalar(q[:, j % 2, :], t[:, j % 2, :], -ROUND, scales["gated"][0][:, :], ALU.add, ALU.mult).then_inc(q_ready, 1)
                    dve.wait_ge(q_ready, k + 1)
                    nc.vector.scalar_tensor_tensor(gated[:, k, :], up[:, k, :], scales["up"][0][:, :], q[:, j % 2, :], ALU.mult, ALU.mult).then_inc(o_ready, 1)
                    dve.wait_ge(o_ready, k + 1)
                    nc.vector.tensor_reduce(peaks[:, 2 * g + j // 3, j % 3:j % 3 + 1], gated[:, k, :], AX.X, ALU.max, apply_absolute_value=True)


def project(nc, dram, W, bank, scales, o, spare, round_col, out):
    NG = o.shape[1] // 3
    with ExitStack() as stack:
        core = Core(nc, stack)
        t = core.sb("fp_scaled", [P, 3, 512], F32)
        q = core.sb("fp_o", [P, 2, 3, 512], F32)
        y, x = (spare[:, k, :, :].rearrange("p k (b c) -> p k b c", b=4) for k in range(2))
        t_ready = core.sem("fp_scaled_ready")
        q_ready = core.sem("fp_o_ready")
        y_done = core.sem("fp_y_done")
        sum_ready = core.sem("fp_sum_ready")
        stored = [core.sem(f"fp_stored{k}") for k in range(2)]
        x_in = [core.sem(f"fp_x_in{k}") for k in range(2)]
        Y = bank[0:2]
        block = stack.enter_context(nc.Block())

        @block.scalar
        def _(act):
            nc.scalar.preload_act_table(ACT.Identity)
            with act.Fori(0, NG // 2) as i:
                for s in range(2):
                    g = 2 * i + s
                    for j in range(3):
                        act.wait_ge(q_ready, 3 * g)
                        nc.scalar.activation(t[:, j, :], o[:, 3 * g + j, :], ACT.Identity, bias=round_col[:, :], scale=scales["o"][1][:, :]).then_inc(t_ready, 1)

        @block.vector
        def _(dve):
            def quantised(n, p):
                wait(dve, y_done, n - 1)
                for j in range(3):
                    dve.wait_ge(t_ready, 3 * n + j + 1)
                    nc.vector.tensor_scalar(q[:, p, j, :], t[:, j, :], -ROUND, scales["o"][0][:, :], ALU.add, ALU.mult).then_inc(q_ready, 1)

            def add(b, p, turn):
                dve.wait_ge(y_done, b + 1)
                wait(dve, stored[p], turn)
                dve.wait_ge(x_in[p], turn + 16)
                nc.vector.tensor_tensor(y[:, p, :, :], Y[p][:, :].rearrange("p (k c) -> p k c", k=4), x[:, p, :, :], ALU.add).then_inc(sum_ready, 1)

            quantised(0, 0)
            quantised(1, 1)
            add(0, 0, 0)
            if NG > 2:
                with dve.Fori(1, NG // 2) as i:
                    quantised(2 * i, 0)
                    add(2 * i - 1, 1, 16 * i - 16)
                    quantised(2 * i + 1, 1)
                    add(2 * i, 0, 16 * i)
            add(NG - 1, 1, 16 * (NG // 2 - 1))

        @block.tensor
        def _(pe):
            with pe.Fori(0, NG // 2) as i:
                for p in range(2):
                    g = 2 * i + p
                    pe.wait_ge(q_ready, 3 * g + 3)
                    pe.wait_ge(sum_ready, g if p == 0 else 2 * i)
                    for k in range(4):
                        for j in range(3):
                            mm = pe.matmul(Y[p][:, k * P:(k + 1) * P], q[:, p, j, k * P:(k + 1) * P], W["down"][:, j, :],
                                           start=(j == 0), stop=(j == 2))
                    mm.then_inc(y_done, 1)

        @block.sync
        def _(sp):
            rows = lambda t, g: t[bass.ds(4 * g, 4)].rearrange("b t c -> t b c")

            def load(g, p):
                sp.dma_start(x[:, p, :, :], rows(dram["x_parked"], g)).then_inc(x_in[p], 16)

            def store(g, p):
                sp.wait_ge(sum_ready, g + 1)
                sp.dma_start(rows(out, g), y[:, p, :, :]).then_inc(stored[p], 16)

            load(0, 0)
            load(1, 1)
            if NG > 2:
                with sp.Fori(0, NG // 2 - 1) as i:
                    for p in range(2):
                        store(2 * i + p, p)
                        load(2 * i + 2 + p, p)
            store(NG - 2, 0)
            store(NG - 1, 1)
            for p in range(2):
                sp.wait_ge(stored[p], 16 * (NG // 2))


def build(nc, dram, out, stop_after=9):
    NB = dram["x"].shape[0]
    with ExitStack() as top:
        core = Core(nc, top)
        bank = [top.enter_context(nc.psum_tensor(f"bank{k}", [P, 512], F32)) for k in range(8)]
        T = {
            "batches": NB,
            "x": core.sb("x", [P, max(NB, 64), P], F32),
            "ident": core.sb("ident", [P, P], F32),
            "identb": core.sb("identb", [P, P], BF16),
            "x_stats": core.sb("x_stats", [P, NB, 6], F32),
            "ctx_stats": core.sb("ctx_stats", [P, NB, 6], F32),
            "mean": core.sb("x_mean", [P, NB, 1], F32),
            "ctx_mean": core.sb("ctx_mean", [P, NB, 1], F32),
            "rstd": core.sb("x_rstd", [P, NB, 1], F32),
            "ctx_rstd": core.sb("ctx_rstd", [P, NB, 1], F32),
        }
        with ExitStack() as mid:
            core = Core(nc, mid)
            T.update({
                "headmask": core.sb("headmask", [P, 4], F32),
                "groupmask": core.sb("groupmask", [P, 4], F32),
                "tri": core.sb("tri", [P, 4, 4], F32),
                "blockstart": core.sb("blockstart", [P, 1024], F32),
                "expert_rows": core.sb("expert_rows", [16, 4, P], F32),
                "onerow": core.sb("onerow", [P, 16, P], BF16),
                "onerow_f": core.sb("onerow_f", [P, P], F32),
                "wv": (core.sb("wv_hi", [P, 1024], F32R), core.sb("wv_lo", [P, 1024], F32R)),
                "gate_up": (core.sb("gate_up_hi", [P, 2, 6, P], F32R), core.sb("gate_up_lo", [P, 2, 6, P], F32R)),
                "down": core.sb("down", [P, 6, P], F32),
                "router": core.sb("router", [P, 16], F32),
                "router_bias": core.sb("router_bias", [P, 16], F32),
                "w_out0": core.sb("w_out0", [P, P], F32),
                "bout_row": core.sb("bout_row", [P, P], F32),
                "w_out1": core.sb("w_out1", [P, 8, P], F32),
                "ln_cols": core.sb("ln_cols", [P, 4], F32),
                "m": core.sb("wq_wk", [P, 16, P], F32),
            })
            load_and_prepare(nc, top, dram, T, bank)
            x_rows = (T["x_stats"], T["mean"], T["rstd"], P)
            ctx_rows = (T["ctx_stats"], T["ctx_mean"], T["ctx_rstd"], 77)
            row_scales(nc, "rows0", [x_rows + (False,)])
            if stop_after >= 1:
                attention0(nc, dram, T, bank)
            if stop_after >= 2:
                row_scales(nc, "rows1", [x_rows + (False,)])
                ffn0(nc, T, bank)
            if stop_after >= 3:
                row_scales(nc, "rows2", [x_rows + (True,), ctx_rows + (False,)])
                attention1(nc, dram, T, bank)
        if stop_after >= 4:
            row_scales(nc, "rows3", [x_rows + (False,)])
            ffn1(nc, dram, T, bank, out)
            return
        with ExitStack() as s:
            done = s.enter_context(nc.semaphore("dump"))
            blk = s.enter_context(nc.Block())

            @blk.sync
            def _(sp):
                sp.dma_start(out.rearrange("b t c -> t b c"), T["x"][:, 0:NB, :]).then_inc(done, 16)
                sp.wait_ge(done, 16)


def kernel(**inputs):
    import numpy as _np
    import concourse.bacc as _bacc
    from concourse import mybir as _mybir
    from concourse.bass_utils import run_bass_kernel_spmd as _run

    a = {k: _np.asarray(v) for k, v in inputs.items()}
    nb = a["x"].shape[0]
    rows = _np.arange(128)
    tri = _np.tril(_np.ones((4, 4), _np.float32), -1)
    start = (_np.arange(1024) % 16 != 0).astype(_np.float32)
    by_c = lambda w: w.transpose(1, 0, 2).reshape(128, 512)
    arrays = {
        "x": a["x"], "ctx": a["ctx_1024"], "mask": a["mask_Bx1xSxS2_ik1"].reshape(nb, 128, 77),
        "w_out0": a["L0_xattn_w_out"].T, "b_out0": a["L0_xattn_b_out"],
        "router": a["L0_ffn_router_w"].T, "router_bias": a["L0_ffn_correction_bias"],
        "gate_up": _np.concatenate([a["L0_ffn_shared_gate_w"].T, by_c(a["L0_ffn_gate_w"]),
                                    a["L0_ffn_shared_up_w"].T, by_c(a["L0_ffn_up_w"])], axis=1),
        "down": _np.concatenate([a["L0_ffn_shared_down_w"].T, a["L0_ffn_down_w"].reshape(512, 128)], axis=0),
        "ln_cols": _np.stack([a["L1_xattn_ln_l_g"], a["L1_xattn_ln_l_b"], a["L1_xattn_ln_m_g"], a["L1_xattn_ln_m_b"]], axis=1),
        "wq": a["L1_xattn_Wq"].T, "wk": a["L1_xattn_Wkv"][:, :1024].T, "wv": a["L1_xattn_Wkv"][:, 1024:],
        "w_out1": a["L1_xattn_Wout"],
        "w_gate": a["L1_ffn_w_gate"], "w_up": a["L1_ffn_w_up"], "w_down": a["L1_ffn_w_down"],
        "ident": _np.eye(128, dtype=_np.float32),
        "headmask": (rows[:, None] // 8 % 4 == _np.arange(4)[None, :]).astype(_np.float32),
        "groupmask": (rows[:, None] // 32 == _np.arange(4)[None, :]).astype(_np.float32),
        "tri": _np.ascontiguousarray(_np.broadcast_to(tri, (128, 4, 4))),
        "blockstart": _np.ascontiguousarray(_np.broadcast_to(start, (128, 1024))),
        "expert_rows": _np.stack([(_np.arange(16)[:, None] == 4 * j + rows[None, :] // 32) for j in range(4)], axis=1).astype(_np.float32),
    }
    arrays = {k: _np.ascontiguousarray(v) for k, v in arrays.items()}
    nc = _bacc.Bacc("TRN2", target_bir_lowering=False, num_devices=1)
    dram = {k: nc.dram_tensor(f"in_{k}", v.shape, _mybir.dt.from_np(v.dtype), kind="ExternalInput").ap() for k, v in arrays.items()}
    out = nc.dram_tensor("out_x", (nb, 128, 128), _mybir.dt.from_np(_np.dtype("float32")), kind="ExternalOutput").ap()
    dram["x_parked"] = nc.dram_tensor("x_parked", (nb, 128, 128), _mybir.dt.float32, kind="Internal").ap()
    build(nc, dram, out)
    r = _run(nc, [{f"in_{k}": v for k, v in arrays.items()}], core_ids=[0])
    return r.results[0]["out_x"]
```

```python
from contextlib import ExitStack

import numpy as np
import concourse.bass as bass
from concourse import mybir

F32 = mybir.dt.float32
F32R = mybir.dt.float32r
BF16 = mybir.dt.bfloat16
I32 = mybir.dt.int32
I16 = mybir.dt.int16
ALU = mybir.AluOpType
ACT = mybir.ActivationFunctionType
AX = mybir.AxisListType
RMAX = bass.bass_isa.ReduceOp.max

P = 128
EPS = 1e-5
MASKED = -(2.0 ** 73)
ROUND = 1.5 * 2.0 ** 23


def wait(eng, sem, value):
    if not isinstance(value, int) or value > 0:
        eng.wait_ge(sem, value)


def three_products(pe, out, a, b, start, stop):
    pe.matmul(out, a[0], b[0], start=start, stop=False)
    pe.matmul(out, a[0], b[1], start=False, stop=False)
    return pe.matmul(out, a[1], b[0], start=False, stop=stop)


def pipelined(eng, n, step):
    step(None, 0, 1)
    step(0, 1, 0)
    step(1, 2, 1)
    if n > 4:
        with eng.Fori(1, (n - 2) // 2) as i:
            step(2 * i, 2 * i + 1, 0)
            step(2 * i + 1, 2 * i + 2, 1)
    step(n - 2, n - 1, 0)
    step(n - 1, None, 1)


def pipelined_deep(eng, n, step):
    step(None, None, 0, 1, 1)
    step(None, 0, 1, 2, 0)
    step(0, 1, 2, 3, 1)
    if n > 4:
        with eng.Fori(1, n // 2 - 1) as i:
            step(2 * i - 1, 2 * i, 2 * i + 1, 2 * i + 2, 0)
            step(2 * i, 2 * i + 1, 2 * i + 2, 2 * i + 3, 1)
    step(n - 3, n - 2, n - 1, None, 0)
    step(n - 2, n - 1, None, None, 1)
    step(n - 1, None, None, None, 0)


def staggered(eng, n, stages):
    def at(i, m, ends):
        for lag, f in stages:
            k = 6 * i + m - lag
            if not ends or 0 <= k < n:
                f(k, 2 * i + (m - lag) // 3, (m - lag) % 6)

    for m in range(6):
        at(0, m, True)
    if n > 12:
        with eng.Fori(1, n // 6 - 1) as i:
            for m in range(6):
                at(i, m, False)
    for m in range(6 + max(lag for lag, _ in stages)):
        at(n // 6 - 1, m, True)


class Core:

    def __init__(self, nc, stack):
        self.nc, self.stack = nc, stack

    def sb(self, name, shape, dt):
        return self.stack.enter_context(self.nc.sbuf_tensor(name, shape, dt))

    def sem(self, name):
        return self.stack.enter_context(self.nc.semaphore(name))


def load_and_prepare(nc, dram, T, bank):
    NB = T["batches"]
    with ExitStack() as stack:
        core = Core(nc, stack)
        wq = core.sb("wq_by_dim", [64, 16, P], F32)
        wk = core.sb("wk_by_dim", [64, 16, P], F32)
        wv = core.sb("wv_raw", [P, 1024], F32)
        gu = core.sb("gate_up_raw", [P, 2, 6, P], F32)
        x_in = [core.sem(f"x_in{k}") for k in range(4)]
        w_in = core.sem("weights_in")
        wv_hi = core.sem("wv_hi_done")
        gu_hi = core.sem("gate_up_hi_done")
        qk_done = core.sem("qk_products_done")
        qk_kept = core.sem("qk_products_kept")
        prepared = core.sem("prepared")

        weights = [(T["headmask"], dram["headmask"]), (T["groupmask"], dram["groupmask"]),
                   (T["tri"], dram["tri"]), (T["expert_rows"], dram["expert_rows"]), (T["blockstart"], dram["blockstart"]),
                   (wq, dram["wq"].rearrange("(h d) c -> d h c", d=64)), (wk, dram["wk"].rearrange("(h d) c -> d h c", d=64)),
                   (wv, dram["wv"]), (gu, dram["gate_up"].rearrange("c (s j h) -> c s j h", s=2, j=6)),
                   (T["down"], dram["down"].rearrange("(j h) c -> h j c", h=P)), (T["router"], dram["router"]),
                   (T["w_out0"], dram["w_out0"]), (T["w_out1"], dram["w_out1"].rearrange("(j d) c -> d j c", d=P)),
                   (T["bout_row"][0:1, :], dram["b_out0"].unsqueeze(0)),
                   (T["router_bias"], dram["router_bias"].partition_broadcast(P)),
                   (T["ln_cols"], dram["ln_cols"])]
        quantise_weights(nc, dram, T, T["ffn1"], bank, x_in, weights, w_in)

        block = stack.enter_context(nc.Block())

        @block.scalar
        def _(act):
            act.wait_ge(w_in, 16 * len(weights))
            nc.scalar.copy(T["wv"][0][:, :], wv[:, :]).then_inc(wv_hi, 1)
            nc.scalar.copy(T["gate_up"][0][:, :, :, :], gu[:, :, :, :]).then_inc(gu_hi, 1)
            for k in range(4):
                act.wait_ge(qk_done, k + 1)
                nc.scalar.copy(T["m"][:, 4 * k:4 * k + 4, :], bank[k][:, :].rearrange("p (h c) -> p h c", h=4)).then_inc(qk_kept, 1)
            act.wait_ge(prepared, 1)

        @block.tensor
        def _(pe):
            pe.wait_ge(w_in, 16 * len(weights))
            for h in range(16):
                mm = pe.matmul(bank[h // 4][:, (h % 4) * P:(h % 4 + 1) * P], wq[:, h, :], wk[:, h, :], start=True, stop=True)
                if h % 4 == 3:
                    mm.then_inc(qk_done, 1)

        @block.vector
        def _(dve):
            def statistics(k):
                dve.wait_ge(x_in[k], 16)
                with dve.Fori(k * NB // 16, (k + 1) * NB // 16) as i:
                    for b in range(4):
                        nc.vector.bn_stats(T["x_stats"][:, 4 * i + b, :], T["x"][:, 4 * i + b, :])

            for k in range(3):
                statistics(k)
            dve.wait_ge(w_in, 16 * len(weights))
            nc.vector.tensor_copy(T["identb"][:, :], T["ident"][:, :])
            nc.vector.tensor_copy(T["onerow"][:, :, :], T["ident"][:, 0:16].unsqueeze(2).to_broadcast([P, 16, P]))
            nc.vector.tensor_copy(T["onerow_f"][:, :], T["ident"][:, 0:1].to_broadcast([P, P]))
            dve.wait_ge(wv_hi, 1)
            nc.vector.tensor_tensor(T["wv"][1][:, :], wv[:, :], T["wv"][0][:, :].bitcast(F32), ALU.subtract)
            dve.wait_ge(gu_hi, 1)
            nc.vector.tensor_tensor(T["gate_up"][1][:, :, :, :], gu[:, :, :, :], T["gate_up"][0][:, :, :, :].bitcast(F32),
                                    ALU.subtract).then_inc(prepared, 1)
            statistics(3)


def row_scales(nc, name, jobs):
    with ExitStack() as stack:
        core = Core(nc, stack)
        n = jobs[0][1].shape[1]
        mean_gap = core.sb(name + "_mean_gap", [P, n], F32)
        var = core.sb(name + "_var", [P, n], F32)
        root = core.sb(name + "_root", [P, n], F32)
        first = core.sb(name + "_first", [P, n], F32)
        step = core.sem(name + "_vector_step")
        var_ready = core.sem(name + "_var_ready")
        rooted = core.sem(name + "_rooted")
        block = stack.enter_context(nc.Block())

        @block.vector
        def _(dve):
            steps, roots = 0, 0

            def then(instruction):
                nonlocal steps
                instruction.then_inc(step, 1)
                steps += 1
                dve.wait_ge(step, steps)

            for stats, mean, rstd, p, twice in jobs:
                gap, v, r, f, m = mean_gap[0:p, :], var[0:p, :], root[0:p, :], first[0:p, :], mean[0:p, :, 0]
                then(nc.vector.tensor_tensor(gap, stats[0:p, :, 1], stats[0:p, :, 4], ALU.subtract))
                then(nc.vector.tensor_tensor(gap, gap, gap, ALU.mult))
                then(nc.vector.tensor_tensor(m, stats[0:p, :, 1], stats[0:p, :, 4], ALU.add))
                then(nc.vector.tensor_scalar(m, m, 0.5, None, ALU.mult))
                then(nc.vector.tensor_tensor(v, stats[0:p, :, 2], stats[0:p, :, 5], ALU.add))
                then(nc.vector.tensor_scalar(gap, gap, 0.25, EPS, ALU.mult, ALU.add))
                then(nc.vector.scalar_tensor_tensor(v, v, 1.0 / P, gap, ALU.mult, ALU.add))
                nc.vector.tensor_scalar(v, v, 0.0, None, ALU.add).then_inc(var_ready, 1)
                roots += 1
                dve.wait_ge(rooted, roots)
                if not twice:
                    then(nc.vector.reciprocal(rstd[0:p, :, 0], r))
                    continue
                then(nc.vector.reciprocal(f, r))
                then(nc.vector.tensor_scalar(v, v, -EPS, None, ALU.add))
                then(nc.vector.tensor_tensor(v, v, f, ALU.mult))
                then(nc.vector.tensor_tensor(v, v, f, ALU.mult))
                nc.vector.tensor_scalar(v, v, EPS, None, ALU.add).then_inc(var_ready, 1)
                roots += 1
                dve.wait_ge(rooted, roots)
                then(nc.vector.reciprocal(r, r))
                then(nc.vector.tensor_tensor(rstd[0:p, :, 0], r, f, ALU.mult))

        @block.scalar
        def _(act):
            roots = 0
            for stats, mean, rstd, p, twice in jobs:
                for _ in range(1 + twice):
                    roots += 1
                    act.wait_ge(var_ready, roots)
                    nc.scalar.activation(root[0:p, :], var[0:p, :], ACT.Sqrt).then_inc(rooted, 1)


def attention0(nc, dram, T, bank):
    NB = T["batches"]
    S = 77
    SP = 78
    D = 128
    SCALE = float(1.0 / np.sqrt(np.float32(D)))
    with ExitStack() as stack:
        core = Core(nc, stack)
        ctx = core.sb("a0_ctx", [S, 2, D], F32)
        mask = core.sb("a0_mask", [P, 2, S], I32)
        maskb = core.sb("a0_mask_bias", [P, 2, S], BF16)
        xn = core.sb("a0_xn", [P, D], F32)
        q_hi = core.sb("a0_q_hi", [P, 2, 4, P], F32R)
        q_lo = core.sb("a0_q_lo", [P, 2, 4, P], F32R)
        q_f = core.sb("a0_q_f", [P, 4, P], F32)
        k_hi = core.sb("a0_k_hi", [P, 2, 4 * SP], F32R)
        k_lo = core.sb("a0_k_lo", [P, 2, 4 * SP], F32R)
        k_f = core.sb("a0_k_f", [P, 4 * SP], F32)
        v1 = core.sb("a0_v_and_one", [S, 2, 16, 9], F32)
        ones = core.sb("a0_ones", [S, 16, 8], F32)
        negmax = core.sb("a0_negmax", [P, 16], F32)
        bias = core.sb("a0_bias", [P, 2, 16, SP], BF16)
        any_key = core.sb("a0_any_key", [P, 1], F32)
        scale_q = core.sb("a0_query_scale", [P, 1], F32)
        probs = core.sb("a0_probs", [S, 2, 512], F32)
        rden = core.sb("a0_rden", [P, 16], F32)
        o = core.sb("a0_o", [P, D], F32)
        oT = core.sb("a0_oT", [P, P], F32)

        ctx_in = [core.sem(f"a0_ctx_in{k}") for k in range(2)]
        mask_in = [core.sem(f"a0_mask_in{k}") for k in range(2)]
        zeroed = core.sem("a0_zeroed")
        mask_ready = core.sem("a0_mask_ready")
        v_ready = core.sem("a0_v_ready")
        xn_ready = core.sem("a0_xn_ready")
        qk_turned = core.sem("a0_qk_turned")
        blocked = core.sem("a0_blocked")
        hi_ready = core.sem("a0_hi_ready")
        lo_ready = core.sem("a0_lo_ready")
        rough_done = core.sem("a0_rough_done")
        max_done = core.sem("a0_max_done")
        scale_step = core.sem("a0_query_scale_step")
        bias_ready = core.sem("a0_bias_ready")
        scores_done = core.sem("a0_scores_done")
        exp_done = core.sem("a0_exp_done")
        av_done = core.sem("a0_av_done")
        rden_done = core.sem("a0_rden_done")
        o_ready = core.sem("a0_o_ready")
        o_turned = core.sem("a0_o_turned")
        oT_ready = core.sem("a0_oT_ready")
        y_done = core.sem("a0_y_done")
        x_ready = core.sem("a0_x_ready")
        ctx_stat_done = core.sem("a0_ctx_stat_done")

        TURN, YT = bank[0], bank[2]
        ROUGH, SCORES, AV = bank[3:5], bank[5:7], bank[7]
        block = stack.enter_context(nc.Block())

        @block.sync
        def _(sp):
            def load(b, k, first):
                if not first:
                    wait(sp, v_ready, b - 1)
                    wait(sp, ctx_stat_done, b - 1)
                    wait(sp, qk_turned, b - 1)
                    wait(sp, mask_ready, b - 1)
                sp.dma_start(ctx[:, k, :], dram["ctx"][b]).then_inc(ctx_in[k], 16)
                sp.dma_start(mask[:, k, :], dram["mask"][b]).then_inc(mask_in[k], 16)
            load(0, 0, True)
            load(1, 1, True)
            with sp.Fori(1, NB // 2) as pair:
                b = 2 * pair
                load(b, 0, False)
                load(b + 1, 1, False)

        @block.gpsimd
        def _(pool):
            nc.gpsimd.memset(v1[:, :, :, :], 1.0).then_inc(zeroed, 1)
            nc.gpsimd.memset(k_f[:, :], 0.0).then_inc(zeroed, 1)
            nc.gpsimd.memset(ones[:, :, :], 1.0).then_inc(zeroed, 1)
            pool.wait_ge(zeroed, 3)

            def biases(n, i, q, b):
                pool.wait_ge(max_done, 4 * n + i + 1)
                if b is not None and i == 0:
                    pool.wait_ge(scores_done, 4 * b)
                nc.gpsimd.tensor_tensor(bias[:, q, 4 * i:4 * i + 4, 0:S], maskb[:, q, :].unsqueeze(1).to_broadcast([P, 4, S]),
                                        negmax[:, 4 * i:4 * i + 4].unsqueeze(2).to_broadcast([P, 4, S]), ALU.add).then_inc(bias_ready, 1)

            def prepare(t, p):
                pool.wait_ge(ctx_in[p], t * 8 + 16 - 8 * p)
                wait(pool, av_done, 4 * (t - 1))
                nc.gpsimd.tensor_tensor(v1[:, p, :, 0:8], ctx[:, p, :].rearrange("s (h d) -> s h d", h=16),
                                        ones[:, :, :], ALU.mult).then_inc(v_ready, 1)

            def step(late, b, n, t, p):
                if n is not None:
                    for i in range(4):
                        biases(n, i, 1 - p, b)
                if t is not None:
                    prepare(t, p)
            prepare(0, 0)
            pipelined_deep(pool, NB, step)

        @block.vector
        def _(dve):
            dve.wait_ge(zeroed, 3)

            def mask_rows(t, p):
                wait(dve, mask_in[p], t * 8 + 16 - 8 * p)
                wait(dve, rough_done, 4 * (t - 1))
                wait(dve, bias_ready, 4 * (t - 1))
                nc.vector.tensor_scalar(maskb[:, p, :], mask[:, p, :], 0.0, MASKED, ALU.is_equal, ALU.mult).then_inc(mask_ready, 1)
                dve.wait_ge(mask_ready, t + 1)
                nc.vector.tensor_reduce(any_key[:, :], maskb[:, p, :], AX.X, ALU.max).then_inc(scale_step, 1)

            def normal_rows(t):
                dve.wait_ge(scale_step, 2 * t + 1)
                nc.vector.tensor_scalar(scale_q[:, :], any_key[:, :], 0.0, T["rstd"][:, t, :], ALU.is_equal, ALU.mult).then_inc(scale_step, 1)
                dve.wait_ge(scale_step, 2 * t + 2)
                wait(dve, qk_turned, t)
                nc.vector.tensor_scalar(xn[:, :], T["x"][:, t, :], T["mean"][:, t, :], scale_q[:, :], ALU.subtract, ALU.mult).then_inc(xn_ready, 1)

            def block_rows(t):
                dve.wait_ge(qk_turned, t + 1)
                wait(dve, lo_ready, 2 * t)
                wait(dve, hi_ready, 2 * t)
                nc.vector.tensor_tensor(q_f[:, :, :], TURN[:, 0:P].unsqueeze(1).to_broadcast([P, 4, P]),
                                        T["headmask"][:, :].unsqueeze(2).to_broadcast([P, 4, P]), ALU.mult).then_inc(blocked, 1)
                nc.vector.tensor_tensor(k_f[:, :].rearrange("p (g s) -> p g s", g=4)[:, :, 0:S],
                                        TURN[:, P:P + S].unsqueeze(1).to_broadcast([P, 4, S]),
                                        T["groupmask"][:, :].unsqueeze(2).to_broadcast([P, 4, S]), ALU.mult).then_inc(blocked, 1)

            def low_queries(t, p, b):
                if b is not None:
                    dve.wait_ge(scores_done, 4 * b + 4)
                dve.wait_ge(hi_ready, 2 * t + 1)
                nc.vector.tensor_tensor(q_lo[:, p, :, :], q_f[:, :, :], q_hi[:, p, :, :].bitcast(F32), ALU.subtract).then_inc(lo_ready, 1)

            def low_keys(t, p):
                dve.wait_ge(hi_ready, 2 * t + 2)
                nc.vector.tensor_tensor(k_lo[:, p, :], k_f[:, :], k_hi[:, p, :].bitcast(F32), ALU.subtract).then_inc(lo_ready, 1)

            def ctx_statistics(t, p):
                wait(dve, ctx_in[p], t * 8 + 16 - 8 * p)
                nc.vector.bn_stats(T["ctx_stats"][0:S, t, :], ctx[:, p, :]).then_inc(ctx_stat_done, 1)

            def keep_max(n, i):
                dve.wait_ge(rough_done, 4 * n + i + 1)
                nc.vector.tensor_reduce(negmax[:, 4 * i:4 * i + 4], ROUGH[i % 2][:, 0:4 * SP].rearrange("p (g s) -> p g s", g=4)[:, :, 0:S],
                                        AX.X, ALU.max, negate=True).then_inc(max_done, 1)

            def normalise(b):
                dve.wait_ge(av_done, 4 * b + 4)
                av = AV[:, 0:144].rearrange("p (h d) -> p h d", h=16)
                nc.vector.reciprocal(rden[:, :], av[:, :, 8]).then_inc(rden_done, 1)
                dve.wait_ge(rden_done, b + 1)
                wait(dve, o_turned, b)
                nc.vector.tensor_tensor(o[:, :].rearrange("p (h d) -> p h d", h=16), av[:, :, 0:8],
                                        rden[:, :].unsqueeze(2).to_broadcast([P, 16, 8]), ALU.mult).then_inc(o_ready, 1)

            def step(late, b, n, t, p):
                if t is not None:
                    mask_rows(t, p)
                if late is not None:
                    normalise(late)
                if n is not None:
                    keep_max(n, 0)
                if t is not None:
                    normal_rows(t)
                    ctx_statistics(t, p)
                if n is not None:
                    keep_max(n, 1)
                if late is not None:
                    dve.wait_ge(y_done, late + 1)
                    nc.vector.tensor_tensor(T["x"][:, late, :], TURN[:, 384:512], T["x"][:, late, :], ALU.add).then_inc(x_ready, 1)
                if t is not None:
                    block_rows(t)
                if n is not None:
                    keep_max(n, 2)
                if late is not None:
                    dve.wait_ge(x_ready, late + 1)
                    nc.vector.bn_stats(T["x_stats"][:, late, :], T["x"][:, late, :])
                if n is not None:
                    keep_max(n, 3)
                if t is not None:
                    low_queries(t, p, b)
                    low_keys(t, p)
            mask_rows(0, 0)
            normal_rows(0)
            ctx_statistics(0, 0)
            block_rows(0)
            low_queries(0, 0, None)
            low_keys(0, 0)
            pipelined_deep(dve, NB, step)

        @block.scalar
        def _(act):
            nc.scalar.preload_act_table(ACT.Exp)
            act.wait_ge(zeroed, 3)

            def exponential(b, g):
                act.wait_ge(scores_done, 4 * b + g + 1)
                wait(act, av_done, 4 * b + g - 1)
                nc.scalar.activation(probs[:, g % 2, :], SCORES[g % 2][0:S, :], ACT.Exp, scale=SCALE).then_inc(exp_done, 1)

            def high_rows(t, b, p):
                act.wait_ge(blocked, 2 * t + 1)
                if b is not None:
                    act.wait_ge(scores_done, 4 * b + 4)
                nc.scalar.copy(q_hi[:, p, :, :], q_f[:, :, :]).then_inc(hi_ready, 1)
                act.wait_ge(blocked, 2 * t + 2)
                nc.scalar.copy(k_hi[:, p, :], k_f[:, :]).then_inc(hi_ready, 1)

            def step(late, b, n, t, p):
                if b is not None:
                    exponential(b, 0)
                    exponential(b, 1)
                if late is not None:
                    act.wait_ge(o_turned, late + 1)
                    wait(act, y_done, late)
                    nc.scalar.copy(oT[:, :], YT[:, 0:P]).then_inc(oT_ready, 1)
                if b is not None:
                    for g in range(2, 4):
                        exponential(b, g)
                if t is not None:
                    high_rows(t, b, p)
            high_rows(0, None, 0)
            pipelined_deep(act, NB, step)

        @block.tensor
        def _(pe):
            pe.wait_ge(zeroed, 3)
            def turn_rows(t, p):
                pe.wait_ge(xn_ready, t + 1)
                pe.wait_ge(ctx_in[p], t * 8 + 16 - 8 * p)
                wait(pe, x_ready, t - 2)
                pe.transpose(TURN[:, 0:P], xn[:, :], T["ident"][:, :])
                pe.transpose(TURN[:, P:P + S], ctx[:, p, :], T["ident"][0:S, 0:S]).then_inc(qk_turned, 1)

            def score(b, g, p):
                wait(pe, exp_done, 4 * b + g - 1 if g else 4 * b)
                if g == 0:
                    pe.wait_ge(lo_ready, 2 * b + 2)
                kg = slice(g * SP, g * SP + S)
                three_products(pe, SCORES[g % 2][0:S, :], (k_hi[:, p, kg], k_lo[:, p, kg]),
                               (q_hi[:, p, :, :], q_lo[:, p, :, :]), True, False)
                if g == 0:
                    pe.wait_ge(bias_ready, 4 * b + 4)
                for i in range(4):
                    mm = pe.matmul(SCORES[g % 2][0:S, i * P:(i + 1) * P], bias[:, p, 4 * i + g, 0:S],
                                   T["identb"][:, :], start=False, stop=(i == 3))
                mm.then_inc(scores_done, 1)

            def rough(n, i, q):
                if i == 0:
                    pe.wait_ge(hi_ready, 2 * n + 2)
                    pe.wait_ge(mask_ready, n + 1)
                wait(pe, max_done, 4 * n + i - 1 if i else 4 * n)
                pe.matmul(ROUGH[i % 2][:, 0:4 * SP], q_hi[:, q, i, :], k_hi[:, q, :], start=True, stop=False)
                pe.matmul(ROUGH[i % 2][:, 0:4 * SP].rearrange("p (g s) -> p g s", g=4)[:, :, 0:S], T["identb"][:, :],
                          maskb[:, q, :].unsqueeze(1).to_broadcast([P, 4, S]), start=False, stop=True).then_inc(rough_done, 1)

            def weigh(b, g, p):
                pe.wait_ge(exp_done, 4 * b + g + 1)
                if g == 0:
                    wait(pe, o_ready, b)
                    pe.wait_ge(v_ready, b + 1)
                for i in range(4):
                    h = 4 * g + i
                    mm = pe.matmul(AV[:, 9 * h:9 * h + 9], probs[:, g % 2, i * P:(i + 1) * P], v1[:, p, h, :], start=True, stop=True)
                mm.then_inc(av_done, 1)

            def step(late, b, n, t, p):
                q = 1 - p
                if b is not None:
                    score(b, 0, p)
                if late is not None:
                    weigh(late, 3, q)
                if n is not None:
                    rough(n, 0, q)
                if b is not None:
                    score(b, 1, p)
                if late is not None:
                    pe.wait_ge(o_ready, late + 1)
                    wait(pe, oT_ready, late)
                    pe.transpose(YT[:, 0:P], o[:, :], T["ident"][:, :]).then_inc(o_turned, 1)
                if n is not None:
                    rough(n, 1, q)
                if b is not None:
                    weigh(b, 0, p)
                if late is not None:
                    pe.wait_ge(oT_ready, late + 1)
                    if n is not None:
                        pe.wait_ge(blocked, 2 * n + 2)
                    pe.matmul(TURN[:, 384:512], T["onerow_f"][:, :], T["bout_row"][:, :], start=True, stop=False)
                    pe.matmul(TURN[:, 384:512], oT[:, :], T["w_out0"][:, :], start=False, stop=True).then_inc(y_done, 1)
                if b is not None:
                    score(b, 2, p)
                if t is not None:
                    turn_rows(t, p)
                if n is not None:
                    rough(n, 2, q)
                if b is not None:
                    weigh(b, 1, p)
                if n is not None:
                    rough(n, 3, q)
                if b is not None:
                    score(b, 3, p)
                    weigh(b, 2, p)
            turn_rows(0, 0)
            pipelined_deep(pe, NB, step)


def ffn0(nc, T, bank):
    NB = T["batches"]
    NG = NB // 4
    with ExitStack() as stack:
        core = Core(nc, stack)
        xT_all = core.sb("f0_xT_all", [P, NG, 512], F32)
        above = core.sb("f0_weight", [P, NB, 16], F32)
        share = core.sb("f0_share", [P, NB, 1], F32)
        with ExitStack() as s:
            route_all(nc, Core(nc, s), T, bank, xT_all, above, share)

        rows_r = core.sb("f0_expert_rows_r", [48, 4, P], F32R)
        xT_hi = core.sb("f0_xT_hi", [P, 2, 512], F32R)
        xT_lo = core.sb("f0_xT_lo", [P, 2, 512], F32R)
        combine = core.sb("f0_combine", [P, 4, 8, 16], F32)
        combT = core.sb("f0_combT", [48, 2, 512], F32R)
        gate = core.sb("f0_gate_sigmoid", [P, 2, 512], F32)
        silu = core.sb("f0_silu", [P, 2, 512], F32)
        hidden = core.sb("f0_hidden", [P, 2, 6, 512], F32)

        rows_ready = core.sem("f0_expert_rows_ready")
        zeroed = core.sem("f0_zeroed")
        hi_ready = core.sem("f0_hi_ready")
        lo_ready = core.sem("f0_lo_ready")
        comb_ready = core.sem("f0_comb_ready")
        comb_turned = core.sem("f0_comb_turned")
        comb_hi_ready = core.sem("f0_comb_hi_ready")
        comb_lo_ready = core.sem("f0_comb_lo_ready")
        gate_done = core.sem("f0_gate_done")
        up_done = core.sem("f0_up_done")
        spread_done = core.sem("f0_spread_done")
        sigmoid_done = core.sem("f0_sigmoid_done")
        silu_done = core.sem("f0_silu_done")
        hidden_done = core.sem("f0_hidden_done")
        weighed_done = core.sem("f0_weighed_done")
        y_done = core.sem("f0_y_done")
        x_ready = core.sem("f0_x_ready")

        COMB, GATE, UP, SPREAD, Y = bank[0], bank[2:4], bank[4:6], (bank[1], bank[6]), bank[7]
        block = stack.enter_context(nc.Block())

        @block.gpsimd
        def _(pool):
            nc.gpsimd.memset(combine[:, :, :, :], 0.0).then_inc(zeroed, 1)

        @block.vector
        def _(dve):
            dve.wait_ge(zeroed, 1)

            def add(b):
                dve.wait_ge(y_done, b + 1)
                for k in range(4):
                    nc.vector.tensor_tensor(T["x"][:, 4 * b + k, :], Y[:, k * P:(k + 1) * P], T["x"][:, 4 * b + k, :], ALU.add).then_inc(x_ready, 1)

            def statistics(b):
                dve.wait_ge(x_ready, 4 * b + 4)
                for k in range(4):
                    nc.vector.bn_stats(T["x_stats"][:, 4 * b + k, :], T["x"][:, 4 * b + k, :])

            def weigh(b, j, p):
                dve.wait_ge(hidden_done, 6 * b + j + 1)
                dve.wait_ge(spread_done, 4 * b + j - 1)
                nc.vector.tensor_tensor(hidden[:, p, j, :], SPREAD[j % 2][:, :], hidden[:, p, j, :], ALU.mult).then_inc(weighed_done, 1)

            def hide(b, j, p):
                dve.wait_ge(sigmoid_done, 6 * b + j + 1)
                wait(dve, hidden_done, 6 * b + j - 1)
                nc.vector.tensor_tensor(silu[:, j % 2, :], GATE[j % 2][:, :], gate[:, j % 2, :], ALU.mult).then_inc(silu_done, 1)
                if j >= 3:
                    weigh(b, j - 1, p)
                dve.wait_ge(silu_done, 6 * b + j + 1)
                dve.wait_ge(up_done, 6 * b + j + 1)
                if j == 0:
                    wait(dve, y_done, b - 1)
                nc.vector.tensor_tensor(hidden[:, p, j, :], UP[j % 2][:, :], silu[:, j % 2, :], ALU.mult).then_inc(hidden_done, 1)

            def step(late, b, n, t, p):
                q = 1 - p
                if b is not None:
                    hide(b, 0, p)
                if n is not None:
                    wait(dve, comb_turned, n)
                    nc.vector.tensor_tensor(combine[:, :, 0:3, :], above[:, bass.ds(4 * n, 4), :].unsqueeze(2).to_broadcast([P, 4, 3, 16]),
                                            share[:, bass.ds(4 * n, 4), :].unsqueeze(3).to_broadcast([P, 4, 3, 16]), ALU.mult).then_inc(comb_ready, 1)
                ended = late is not None and not (isinstance(late, int) and late < 1)
                if ended:
                    add(late - 1)
                if b is not None:
                    hide(b, 1, p)
                if n is not None:
                    dve.wait_ge(hi_ready, n + 1)
                    nc.vector.tensor_tensor(xT_lo[:, q, :], xT_all[:, n, :], xT_hi[:, q, :].bitcast(F32), ALU.subtract).then_inc(lo_ready, 1)
                if b is not None:
                    hide(b, 2, p)
                    hide(b, 3, p)
                if n is not None:
                    dve.wait_ge(comb_hi_ready, n + 1)
                    nc.vector.tensor_tensor(combT[32:48, q, :], COMB[32:48, :], combT[32:48, q, :].bitcast(F32), ALU.subtract).then_inc(comb_lo_ready, 1)
                if b is not None:
                    hide(b, 4, p)
                if ended:
                    statistics(late - 1)
                if b is not None:
                    hide(b, 5, p)
                    weigh(b, 5, p)
            pipelined_deep(dve, NG, step)
            add(NG - 1)
            statistics(NG - 1)

        @block.scalar
        def _(act):
            nc.scalar.preload_act_table(ACT.Sigmoid)
            nc.scalar.copy(rows_r[:, :, :], T["expert_rows"][:, :, :]).then_inc(rows_ready, 1)

            def sigmoid(b, j):
                act.wait_ge(gate_done, 6 * b + j + 1)
                wait(act, silu_done, 6 * b + j - 1 if j else 6 * b)
                nc.scalar.activation(gate[:, j % 2, :], GATE[j % 2][:, :], ACT.Sigmoid).then_inc(sigmoid_done, 1)

            def step(late, b, n, t, p):
                q = 1 - p
                if b is not None:
                    sigmoid(b, 0)
                    sigmoid(b, 1)
                if n is not None:
                    if b is not None:
                        wait(act, up_done, 6 * b)
                    nc.scalar.copy(xT_hi[:, q, :], xT_all[:, n, :]).then_inc(hi_ready, 1)
                if b is not None:
                    sigmoid(b, 2)
                if n is not None:
                    act.wait_ge(comb_turned, n + 1)
                    if b is not None:
                        wait(act, spread_done, 4 * b)
                    nc.scalar.copy(combT[:, q, :], COMB[0:48, :]).then_inc(comb_hi_ready, 1)
                if b is not None:
                    sigmoid(b, 3)
                    sigmoid(b, 4)
                    sigmoid(b, 5)
            pipelined_deep(act, NG, step)

        @block.tensor
        def _(pe):
            gu_hi, gu_lo = T["gate_up"]
            pe.wait_ge(rows_ready, 1)

            def expand(b, j, p):
                if j == 0:
                    pe.wait_ge(lo_ready, b + 1)
                x_parts = (xT_hi[:, p, :], xT_lo[:, p, :])
                wait(pe, silu_done, 6 * b + j - 1 if j else 6 * b)
                three_products(pe, GATE[j % 2][:, :], (gu_hi[:, 0, j, :], gu_lo[:, 0, j, :]), x_parts, True, True).then_inc(gate_done, 1)
                wait(pe, hidden_done, 6 * b + j - 1 if j else 6 * b)
                three_products(pe, UP[j % 2][:, :], (gu_hi[:, 1, j, :], gu_lo[:, 1, j, :]), x_parts, True, True).then_inc(up_done, 1)
                if j >= 2:
                    if j == 2:
                        pe.wait_ge(comb_lo_ready, b + 1)
                    wait(pe, weighed_done, 4 * b + j - 3)
                    pe.matmul(SPREAD[j % 2][:, :], rows_r[:, j - 2, :], combT[:, p, :], start=True, stop=True).then_inc(spread_done, 1)

            def down(b, k, p):
                if k == 0:
                    pe.wait_ge(hidden_done, 6 * b + 6)
                    pe.wait_ge(weighed_done, 4 * b + 4)
                    wait(pe, x_ready, 4 * b)
                for j in range(6):
                    mm = pe.matmul(Y[:, k * P:(k + 1) * P], hidden[:, p, j, k * P:(k + 1) * P], T["down"][:, j, :],
                                   start=(j == 0), stop=(j == 5))
                if k == 3:
                    mm.then_inc(y_done, 1)

            def step(late, b, n, t, p):
                for j in range(6):
                    if b is not None:
                        expand(b, j, p)
                    if late is not None and j >= 2:
                        down(late, j - 2, 1 - p)
                    if n is not None and j == 1:
                        pe.wait_ge(comb_ready, n + 1)
                        wait(pe, comb_lo_ready, n)
                        for k in range(4):
                            mm = pe.transpose(COMB[:, k * P:(k + 1) * P], combine[:, k, :, :].rearrange("p r e -> p (r e)"), T["ident"][:, :])
                        mm.then_inc(comb_turned, 1)
            pipelined_deep(pe, NG, step)


def route_all(nc, core, T, bank, xT_all, above, share):
    NB = T["batches"]
    NG = NB // 4
    BIG = 1e30
    xn = core.sb("fr_xn", [P, 2, 4, P], F32)
    xT = core.sb("fr_xT", [P, 2, 512], F32)
    score = core.sb("fr_score", [P, NB, 16], F32)
    biased = core.sb("fr_biased", [P, NB, 16], F32)
    hi2 = core.sb("fr_pair_max", [P, 4 * NB, 2], F32)
    lo2 = core.sb("fr_pair_min", [P, 4 * NB, 2], F32)
    best = core.sb("fr_best", [P, 4 * NB], F32)
    second = core.sb("fr_second", [P, 4 * NB], F32)
    third = core.sb("fr_third", [P, 4 * NB], F32)
    over = core.sb("fr_over", [P, NB, 4, 4], F32)
    tie = core.sb("fr_tie", [P, NB, 4, 4], F32)
    left = core.sb("fr_left", [P, NB, 16], F32)
    top8 = core.sb("fr_top8", [P, NB, 8], F32)
    xn_ready = core.sem("fr_xn_ready")
    turned = core.sem("fr_turned")
    xT_ready = core.sem("fr_xT_ready")
    xT_kept = core.sem("fr_xT_kept")
    logits_done = core.sem("fr_logits_done")
    score_ready = core.sem("fr_score_ready")
    route_step = core.sem("fr_route_step")
    TURN, LOGITS = bank[0:2], bank[2:4]
    with nc.Block() as block:

        @block.scalar
        def _(act):
            nc.scalar.preload_act_table(ACT.Sigmoid)

            def step(b, n, p):
                q = 1 - p
                if n is not None:
                    act.wait_ge(turned, n + 1)
                    wait(act, logits_done, n - 1)
                    nc.scalar.copy(xT[:, q, :], TURN[q][:, :]).then_inc(xT_ready, 1)
                    nc.scalar.copy(xT_all[:, n, :], TURN[q][:, :]).then_inc(xT_kept, 1)
                if b is not None:
                    act.wait_ge(logits_done, b + 1)
                    nc.scalar.activation(score[:, bass.ds(4 * b, 4), :].rearrange("p b e -> p (b e)"),
                                         LOGITS[p][:, 0:64], ACT.Sigmoid).then_inc(score_ready, 1)
            pipelined(act, NG, step)

        @block.tensor
        def _(pe):
            def step(b, n, p):
                q = 1 - p
                if n is not None:
                    pe.wait_ge(xn_ready, 2 * n + 2)
                    wait(pe, xT_kept, n - 1)
                    for k in range(4):
                        mm = pe.transpose(TURN[q][:, k * P:(k + 1) * P], xn[:, q, k, :], T["ident"][:, :])
                    mm.then_inc(turned, 1)
                if b is not None:
                    pe.wait_ge(xT_ready, b + 1)
                    wait(pe, score_ready, b - 1)
                    for k in range(4):
                        mm = pe.matmul(LOGITS[p][:, 16 * k:16 * k + 16], xT[:, p, k * P:(k + 1) * P], T["router"][:, :], start=True, stop=True)
                    mm.then_inc(logits_done, 1)
            pipelined(pe, NG, step)

        @block.gpsimd
        def _(pool):
            def step(b, n, p):
                if n is None:
                    return
                wait(pool, turned, n - 1)
                rows, wide = bass.ds(4 * n, 4), [P, 4, P]
                nc.gpsimd.tensor_tensor(xn[:, 1 - p, :, :], T["x"][:, rows, :], T["mean"][:, rows, :].to_broadcast(wide), ALU.subtract).then_inc(xn_ready, 1)
                pool.wait_ge(xn_ready, 2 * n + 1)
                nc.gpsimd.tensor_tensor(xn[:, 1 - p, :, :], xn[:, 1 - p, :, :], T["rstd"][:, rows, :].to_broadcast(wide), ALU.mult).then_inc(xn_ready, 1)
            pipelined(pool, NG, step)

        @block.vector
        def _(dve):
            steps = 0

            def then(instruction):
                nonlocal steps
                instruction.then_inc(route_step, 1)
                steps += 1

            def settled():
                dve.wait_ge(route_step, steps)

            V = nc.vector

            def route(H, score, biased, left, top8, over, tie, above, share, hi2, lo2, best, second, third):
                wide = [P, H, 16]
                then(V.tensor_tensor(biased[:, :, :], score[:, :, :], T["router_bias"][:, :].unsqueeze(1).to_broadcast(wide), ALU.add))
                settled()
                pairs = biased[:, :, :].rearrange("p b (g e t) -> p (b g) e t", g=4, e=2)
                then(V.tensor_tensor(hi2[:, :, :], pairs[:, :, :, 0], pairs[:, :, :, 1], ALU.max))
                then(V.tensor_tensor(lo2[:, :, :], pairs[:, :, :, 0], pairs[:, :, :, 1], ALU.min))
                settled()
                then(V.tensor_tensor(best[:, :], hi2[:, :, 0], hi2[:, :, 1], ALU.max))
                then(V.tensor_tensor(second[:, :], hi2[:, :, 0], hi2[:, :, 1], ALU.min))
                then(V.tensor_tensor(third[:, :], lo2[:, :, 0], lo2[:, :, 1], ALU.max))
                settled()
                then(V.tensor_tensor(second[:, :], second[:, :], third[:, :], ALU.max))
                settled()
                then(V.tensor_tensor(best[:, :], best[:, :], second[:, :], ALU.add))
                settled()
                sums = best[:, :].rearrange("p (b g) -> p b g", g=4)
                mine = sums.unsqueeze(3).to_broadcast([P, H, 4, 4])
                other = sums.unsqueeze(2).to_broadcast([P, H, 4, 4])
                tri = T["tri"][:, :, :].unsqueeze(1).to_broadcast([P, H, 4, 4])
                then(V.tensor_tensor(over[:, :, :, :], other, mine, ALU.is_gt))
                then(V.tensor_tensor(tie[:, :, :, :], other, mine, ALU.is_equal))
                settled()
                then(V.tensor_tensor(tie[:, :, :, :], tie[:, :, :, :], tri, ALU.mult))
                settled()
                then(V.tensor_tensor(over[:, :, :, :], over[:, :, :, :], tie[:, :, :, :], ALU.add))
                settled()
                rank, penalty = second, third
                then(V.tensor_reduce(rank[:, :], over[:, :, :, :], AX.X, ALU.add))
                settled()
                then(V.tensor_scalar(rank[:, :], rank[:, :], 2.0, None, ALU.is_lt))
                settled()
                then(V.tensor_scalar(penalty[:, :], rank[:, :], BIG, -BIG, ALU.mult, ALU.add))
                kept = rank[:, :].unsqueeze(2).to_broadcast([P, 4 * H, 4])
                left16 = left[:, :, :].rearrange("p b (g e) -> p (b g) e", g=4)
                then(V.tensor_tensor(left16, biased[:, :, :].rearrange("p b (g e) -> p (b g) e", g=4), kept, ALU.mult))
                settled()
                then(V.tensor_tensor(left16, left16, penalty[:, :].unsqueeze(2).to_broadcast([P, 4 * H, 4]), ALU.add))
                settled()
                V.memset(share[:, 0, :], 0.0)
                for b in range(H):
                    then(V.max(top8[:, b, :], left[:, b, :]))
                settled()
                equal = over[:, :, :, :].rearrange("p b i j -> p b (i j)")
                place = tie[:, :, :, :].rearrange("p b i j -> p b (i j)")
                fourth = top8[:, :, 3:4].to_broadcast(wide)
                then(V.tensor_tensor(above[:, :, :], left[:, :, :], fourth, ALU.is_gt))
                then(V.tensor_tensor(equal, left[:, :, :], fourth, ALU.is_equal))
                settled()
                then(V.tensor_reduce(share[:, :, 0], above[:, :, :], AX.X, ALU.add))
                then(V.tensor_tensor_scan(place.rearrange("p b e -> p (b e)"), T["blockstart"][:, 0:16 * H],
                                          equal.rearrange("p b e -> p (b e)"), 0.0, ALU.mult, ALU.add))
                settled()
                then(V.tensor_tensor(place, place, share[:, :, :].to_broadcast(wide), ALU.add))
                settled()
                then(V.scalar_tensor_tensor(equal, place, 4.0, equal, ALU.is_le, ALU.mult))
                settled()
                then(V.tensor_tensor(above[:, :, :], above[:, :, :], equal, ALU.add))
                settled()
                then(V.tensor_tensor(above[:, :, :], above[:, :, :], score[:, :, :], ALU.mult))
                settled()
                then(V.tensor_reduce(share[:, :, 0], above[:, :, :], AX.X, ALU.add))
                settled()
                then(V.tensor_scalar(share[:, :, 0], share[:, :, 0], 1e-20, None, ALU.add))
                settled()
                then(V.reciprocal(share[:, :, 0], share[:, :, 0]))

            for part in range(4):
                H = NB // 4
                b0, b1 = part * H, (part + 1) * H
                dve.wait_ge(score_ready, (part + 1) * NG // 4)
                route(H, *(t[:, b0:b1] for t in (score, biased, left, top8, over, tie, above, share)),
                      *(t[:, 4 * b0:4 * b1] for t in (hi2, lo2, best, second, third)))


def attention1(nc, dram, T, bank):
    NB = T["batches"]
    S = 77
    BLOCKS = ((0, P), (P, S))
    J = P + S
    SCALE = 64 ** -0.5
    with ExitStack() as stack:
        core = Core(nc, stack)
        ctx = core.sb("a1_ctx", [S, 2, P], F32)
        xn = core.sb("a1_xn", [P, P], F32)
        cn = core.sb("a1_cn", [S, P], F32)
        kv = core.sb("a1_kv", [P, 256], F32)
        kv_hi = core.sb("a1_kv_hi", [P, 2, 256], F32R)
        kv_lo = core.sb("a1_kv_lo", [P, 2, 256], F32R)
        g_hi = core.sb("a1_g_hi", [P, 2, 16 * P], F32R)
        g_lo = core.sb("a1_g_lo", [P, 2, 16 * P], F32R)
        v1 = core.sb("a1_v_and_one", [P, 2, 2, 16, 65], F32)
        negmax = core.sb("a1_negmax", [P, 16], F32)
        shift = core.sb("a1_shift", [P, 2, P], BF16)
        probs = core.sb("a1_probs", [P, 2, 2, 512], F32)
        rden = core.sb("a1_rden", [P, 4], F32)
        o = core.sb("a1_o", [P, 16, 64], F32)
        oT = core.sb("a1_oT", [P, 8, P], F32)

        ctx_in = [core.sem(f"a1_ctx_in{k}") for k in range(2)]
        zeroed = core.sem("a1_zeroed")
        cn_ready = core.sem("a1_cn_ready")
        xn_ready = core.sem("a1_xn_ready")
        turned = core.sem("a1_turned")
        kv_ready = core.sem("a1_kv_ready")
        kv_hi_ready = core.sem("a1_kv_hi_ready")
        kv_lo_ready = core.sem("a1_kv_lo_ready")
        v_done = core.sem("a1_v_done")
        v_kept = core.sem("a1_v_kept")
        g_done = core.sem("a1_g_done")
        g_hi_ready = core.sem("a1_g_hi_ready")
        g_lo_ready = core.sem("a1_g_lo_ready")
        rough_done = core.sem("a1_rough_done")
        max_done = core.sem("a1_max_done")
        max_turned = core.sem("a1_max_turned")
        shift_ready = core.sem("a1_shift_ready")
        scores_done = core.sem("a1_scores_done")
        exp_done = core.sem("a1_exp_done")
        av_done = core.sem("a1_av_done")
        rden_done = core.sem("a1_rden_done")
        o_ready = core.sem("a1_o_ready")
        o_turned = core.sem("a1_o_turned")
        oT_ready = core.sem("a1_oT_ready")
        y_done = core.sem("a1_y_done")
        x_ready = core.sem("a1_x_ready")
        parked = core.sem("a1_parked")

        TURN, GB, VB, ROUGH, SCORES, AV = bank[0], bank[1], bank[2], bank[3:5], bank[5:7], bank[7]
        block = stack.enter_context(nc.Block())

        @block.sync
        def _(sp):
            sp.dma_start(ctx[:, 0, :], dram["ctx"][0]).then_inc(ctx_in[0], 16)
            sp.dma_start(ctx[:, 1, :], dram["ctx"][1]).then_inc(ctx_in[1], 16)
            def park(b):
                sp.wait_ge(x_ready, b + 1)
                sp.dma_start(dram["x_parked"][b], T["x"][:, b, :]).then_inc(parked, 16)

            def load(b, k):
                sp.wait_ge(cn_ready, b - 1)
                sp.dma_start(ctx[:, k, :], dram["ctx"][b]).then_inc(ctx_in[k], 16)

            load(2, 0)
            load(3, 1)
            with sp.Fori(2, NB // 2) as pair:
                for k in range(2):
                    load(2 * pair + k, k)
                    park(2 * pair + k - 4)
            for b in range(NB - 4, NB):
                park(b)
            sp.wait_ge(parked, 16 * NB)

        @block.gpsimd
        def _(pool):
            nc.gpsimd.memset(v1[:, :, :, :, :], 1.0).then_inc(zeroed, 1)
            nc.gpsimd.memset(shift[:, :, :], 0.0).then_inc(zeroed, 1)
            nc.gpsimd.memset(kv[:, :], 0.0).then_inc(zeroed, 1)

        @block.vector
        def _(dve):
            dve.wait_ge(zeroed, 3)

            def keep_max(n, k):
                dve.wait_ge(rough_done, 8 * n + k + 1)
                if k == 0:
                    wait(dve, max_turned, n)
                nc.vector.tensor_reduce(negmax[:, 2 * k:2 * k + 2], ROUGH[k % 2][:, :].rearrange("p (h j) -> p h j", h=2)[:, :, 0:J],
                                        AX.X, ALU.max, negate=True).then_inc(max_done, 1)

            def normalise(b, c):
                dve.wait_ge(av_done, 4 * b + c + 1)
                av = AV[:, 0:260].rearrange("p (h d) -> p h d", h=4)
                nc.vector.reciprocal(rden[:, :], av[:, :, 64]).then_inc(rden_done, 1)
                dve.wait_ge(rden_done, 4 * b + c + 1)
                if c % 2 == 0:
                    wait(dve, o_turned, 2 * b - 1 + c // 2)
                nc.vector.tensor_tensor(o[:, 4 * c:4 * c + 4, :], av[:, :, 0:64],
                                        rden[:, :].unsqueeze(2).to_broadcast([P, 4, 64]), ALU.mult).then_inc(o_ready, 1)

            def turn_rows(t, p):
                wait(dve, turned, t)
                nc.vector.tensor_scalar(xn[:, :], T["x"][:, t, :], T["mean"][:, t, :], T["rstd"][:, t, :],
                                        ALU.subtract, ALU.mult).then_inc(xn_ready, 1)
                wait(dve, ctx_in[p], t * 8 + 16 - 8 * p)
                nc.vector.tensor_scalar(cn[:, :], ctx[:, p, :], T["ctx_mean"][0:S, t, :], T["ctx_rstd"][0:S, t, :],
                                        ALU.subtract, ALU.mult).then_inc(cn_ready, 1)

            def scale_rows(t):
                dve.wait_ge(turned, t + 1)
                wait(dve, g_done, 4 * t)
                wait(dve, kv_hi_ready, t)
                wait(dve, kv_lo_ready, t)
                for k, (at, length) in enumerate(BLOCKS):
                    nc.vector.tensor_scalar(kv[:, at:at + length], TURN[:, at:at + length], T["ln_cols"][:, 2 * k:2 * k + 1],
                                            T["ln_cols"][:, 2 * k + 1:2 * k + 2], ALU.mult, ALU.add).then_inc(kv_ready, 1)

            def low_rows(t, p):
                dve.wait_ge(kv_hi_ready, t + 1)
                nc.vector.tensor_tensor(kv_lo[:, p, :], kv[:, :], kv_hi[:, p, :].bitcast(F32), ALU.subtract).then_inc(kv_lo_ready, 1)

            def low_queries(n, c, q):
                dve.wait_ge(g_hi_ready, 4 * n + c + 1)
                nc.vector.tensor_tensor(g_lo[:, q, 512 * c:512 * c + 512], GB[:, :], g_hi[:, q, 512 * c:512 * c + 512].bitcast(F32),
                                        ALU.subtract).then_inc(g_lo_ready, 1)

            def step(late, b, n, t, p):
                q = 1 - p
                if t is not None:
                    turn_rows(t, p)
                if n is not None:
                    low_queries(n, 0, q)
                if late is not None:
                    dve.wait_ge(y_done, late + 1)
                    nc.vector.tensor_tensor(T["x"][:, late, :], TURN[:, 384:512], T["x"][:, late, :], ALU.add).then_inc(x_ready, 1)
                    dve.wait_ge(x_ready, late + 1)
                    nc.vector.bn_stats(T["x_stats"][:, late, :], T["x"][:, late, :])
                    nc.vector.tensor_reduce(T["row_max"][:, late, :], T["x"][:, late, :], AX.X, ALU.max)
                    nc.vector.tensor_reduce(T["row_min"][:, late, :], T["x"][:, late, :], AX.X, ALU.min)
                for c in range(1, 4):
                    if n is not None:
                        low_queries(n, c, q)
                        keep_max(n, 2 * c - 2)
                        keep_max(n, 2 * c - 1)
                    if b is not None:
                        normalise(b, c - 1)
                if n is not None:
                    keep_max(n, 6)
                    keep_max(n, 7)
                if t is not None:
                    scale_rows(t)
                if b is not None:
                    normalise(b, 3)
                if t is not None:
                    low_rows(t, p)
            turn_rows(0, 0)
            scale_rows(0)
            low_rows(0, 0)
            pipelined_deep(dve, NB, step)

        @block.scalar
        def _(act):
            nc.scalar.preload_act_table(ACT.Exp)
            act.wait_ge(zeroed, 3)

            def exponential(b, c, k):
                rows = BLOCKS[k][1]
                act.wait_ge(scores_done, 8 * b + 2 * c + k + 1)
                wait(act, av_done, 4 * b + c - 1 if c else 4 * b)
                nc.scalar.activation(probs[0:rows, c % 2, k, :], SCORES[k][0:rows, :], ACT.Exp, scale=SCALE).then_inc(exp_done, 1)

            def turn_o(b, half):
                act.wait_ge(o_turned, 2 * b + half + 1)
                if half == 0:
                    wait(act, y_done, b)
                nc.scalar.copy(oT[:, 4 * half:4 * half + 4, :], VB[:, :].rearrange("p (k t) -> p k t", k=4)).then_inc(oT_ready, 1)

            def keep_values(n, c, q):
                k, half = divmod(c, 2)
                rows = BLOCKS[k][1]
                act.wait_ge(v_done, 4 * n + c + 1)
                nc.scalar.copy(v1[0:rows, q, k, 8 * half:8 * half + 8, 0:64],
                               VB[0:rows, :].rearrange("p (h d) -> p h d", h=8)).then_inc(v_kept, 1)

            def high_queries(n, c, q):
                act.wait_ge(g_done, 4 * n + c + 1)
                nc.scalar.copy(g_hi[:, q, 512 * c:512 * c + 512], GB[:, :]).then_inc(g_hi_ready, 1)

            def high_rows(t, b, p):
                act.wait_ge(kv_ready, 2 * t + 2)
                if b is not None:
                    act.wait_ge(scores_done, 8 * b + 8)
                nc.scalar.copy(kv_hi[:, p, :], kv[:, :]).then_inc(kv_hi_ready, 1)

            def step(late, b, n, t, p):
                q = 1 - p
                for c in range(4):
                    if b is not None:
                        exponential(b, c, 0)
                        exponential(b, c, 1)
                    if late is not None and c == 0:
                        turn_o(late, 1)
                    if n is not None:
                        if c == 0:
                            high_queries(n, c, q)
                            if b is not None:
                                wait(act, av_done, 4 * b)
                            keep_values(n, c, q)
                        else:
                            keep_values(n, c, q)
                            high_queries(n, c, q)
                if b is not None:
                    turn_o(b, 0)
                if t is not None:
                    high_rows(t, b, p)
                if n is not None:
                    act.wait_ge(max_turned, n + 1)
                    nc.scalar.copy(shift[0:16, q, :], VB[0:16, 0:P]).then_inc(shift_ready, 1)
            high_rows(0, None, 0)
            pipelined_deep(act, NB, step)

        @block.tensor
        def _(pe):
            pe.wait_ge(zeroed, 3)

            def score(b, c, k, p):
                at, rows = BLOCKS[k]
                wait(pe, exp_done, 8 * b + 2 * c + k - 1 if c else 8 * b)
                out = SCORES[k][0:rows, :]
                three_products(pe, out, (kv_hi[:, p, at:at + rows], kv_lo[:, p, at:at + rows]),
                               (g_hi[:, p, 512 * c:512 * c + 512], g_lo[:, p, 512 * c:512 * c + 512]), True, False)
                if c == 0 and k == 0:
                    pe.wait_ge(shift_ready, b + 1)
                for i in range(4):
                    mm = pe.matmul(out[:, i * P:(i + 1) * P], T["onerow"][:, 4 * c + i, 0:rows], shift[:, p, :], start=False, stop=(i == 3))
                mm.then_inc(scores_done, 1)

            def values(n, c, q):
                k, half = divmod(c, 2)
                at, rows = BLOCKS[k]
                if c == 0:
                    pe.wait_ge(kv_lo_ready, n + 1)
                    wait(pe, oT_ready, 2 * (n - 1))
                else:
                    pe.wait_ge(v_kept, 4 * n + c)
                w = slice(512 * half, 512 * half + 512)
                three_products(pe, VB[0:rows, :], (kv_hi[:, q, at:at + rows], kv_lo[:, q, at:at + rows]),
                               (T["wv"][0][:, w], T["wv"][1][:, w]), True, True).then_inc(v_done, 1)

            def queries(n, c):
                if c == 0:
                    pe.wait_ge(kv_ready, 2 * n + 2)
                wait(pe, g_lo_ready, 4 * n + c)
                for i in range(4):
                    mm = pe.matmul(GB[:, i * P:(i + 1) * P], T["m"][:, 4 * c + i, :], kv[:, 0:P], start=True, stop=True)
                mm.then_inc(g_done, 1)

            def rough(n, k, q):
                pe.wait_ge(g_hi_ready, 4 * n + k // 2 + 1)
                wait(pe, max_done, 8 * n + max(k - 1, 0))
                for i in range(2):
                    h = 2 * k + i
                    mm = pe.matmul(ROUGH[k % 2][:, 256 * i:256 * i + 256], g_hi[:, q, h * P:(h + 1) * P], kv_hi[:, q, :], start=True, stop=True)
                mm.then_inc(rough_done, 1)

            def weigh(b, c, p):
                pe.wait_ge(exp_done, 8 * b + 2 * c + 2)
                wait(pe, o_ready, 4 * b + c)
                if c == 0:
                    pe.wait_ge(v_kept, 4 * b + 4)
                for i in range(4):
                    for k, (_, rows) in enumerate(BLOCKS):
                        mm = pe.matmul(AV[:, 65 * i:65 * i + 65], probs[0:rows, c % 2, k, i * P:(i + 1) * P],
                                       v1[0:rows, p, k, 4 * c + i, :], start=(k == 0), stop=(k == 1))
                mm.then_inc(av_done, 1)

            def turn_o(b, half, n):
                pe.wait_ge(o_ready, 4 * b + 2 * half + 2)
                if half:
                    pe.wait_ge(shift_ready, n)
                    pe.wait_ge(oT_ready, 2 * b + 1)
                elif n is not None:
                    pe.wait_ge(v_kept, 4 * n + 4)
                else:
                    pe.wait_ge(oT_ready, 2 * b)
                for i in range(4):
                    k = 4 * half + i
                    mm = pe.transpose(VB[:, i * P:(i + 1) * P], o[:, 2 * k:2 * k + 2, :].rearrange("p h d -> p (h d)"), T["ident"][:, :])
                mm.then_inc(o_turned, 1)

            def turn_rows(t):
                pe.wait_ge(xn_ready, t + 1)
                pe.wait_ge(cn_ready, t + 1)
                wait(pe, x_ready, t - 2)
                pe.transpose(TURN[:, 0:P], xn[:, :], T["ident"][:, :])
                pe.transpose(TURN[:, P:J], cn[:, :], T["ident"][0:S, 0:S]).then_inc(turned, 1)

            def step(late, b, n, t, p):
                q = 1 - p
                for c in range(4):
                    if b is not None:
                        score(b, c, 0, p)
                        score(b, c, 1, p)
                    if late is not None and c == 0:
                        turn_o(late, 1, late + 2 if b is not None else NB)
                    if n is not None and c == 0:
                        queries(n, c)
                        values(n, c, q)
                    elif n is not None:
                        values(n, c, q)
                        queries(n, c)
                    if late is not None and c == 0:
                        pe.wait_ge(oT_ready, 2 * late + 2)
                        if n is not None:
                            pe.wait_ge(kv_ready, 2 * n + 2)
                        for k in range(8):
                            mm = pe.matmul(TURN[:, 384:512], oT[:, k, :], T["w_out1"][:, k, :], start=(k == 0), stop=(k == 7))
                        mm.then_inc(y_done, 1)
                    if n is not None and c >= 1:
                        rough(n, 2 * c - 2, q)
                        rough(n, 2 * c - 1, q)
                    if b is not None and c >= 1:
                        weigh(b, c - 1, p)
                if b is not None:
                    turn_o(b, 0, n)
                if n is not None:
                    rough(n, 6, q)
                    rough(n, 7, q)
                if t is not None:
                    turn_rows(t)
                if b is not None:
                    weigh(b, 3, p)
                if n is not None:
                    pe.wait_ge(max_done, 8 * n + 8)
                    if b is not None:
                        pe.wait_ge(oT_ready, 2 * b + 1)
                    else:
                        pe.wait_ge(v_kept, 4 * n + 4)
                    pe.transpose(VB[0:16, 0:P], negmax[:, :], T["ident"][:, :]).then_inc(max_turned, 1)
            turn_rows(0)
            pipelined_deep(pe, NB, step)


def global_scale(nc, name, top, T, parts):
    with ExitStack() as stack:
        core = Core(nc, stack)
        row = core.sb(name + "_row_max", [P, len(parts)], F32)
        every = core.sb(name + "_all_max", [P, len(parts)], F32)
        reduced = core.sem(name + "_reduced")
        spread = core.sem(name + "_spread")
        clamped = core.sem(name + "_clamped")
        block = stack.enter_context(nc.Block())

        @block.vector
        def _(dve):
            for k, (maxima, _, _) in enumerate(parts):
                nc.vector.tensor_reduce(row[:, k:k + 1], maxima, AX.XY if len(maxima.shape) == 3 else AX.X, ALU.max).then_inc(reduced, 1)
            dve.wait_ge(spread, 1)
            for k, (_, step, inverse) in enumerate(parts):
                nc.vector.tensor_scalar(step, every[:, k:k + 1], 1.0 / 32767.0, 1e-12, ALU.mult, ALU.max).then_inc(clamped, 1)
            for k, (_, step, inverse) in enumerate(parts):
                dve.wait_ge(clamped, k + 1)
                nc.vector.reciprocal(inverse, step)

        @block.gpsimd
        def _(pool):
            pool.wait_ge(reduced, len(parts))
            nc.gpsimd.partition_all_reduce(every[:, :], row[:, :], P, RMAX).then_inc(spread, 1)


def quantise_weights(nc, dram, T, W, bank, x_in, weights, others_in):
    NB = T["batches"]
    with ExitStack() as stack:
        core = Core(nc, stack)
        raw = [core.sb(f"f1_{n}_raw", [P, 12, 32], F32) for n in ("gate", "up", "down")]
        step = core.sb("f1_weight_step", [P, 3, 12], F32)
        inverse = core.sb("f1_weight_inverse", [P, 3, 12], F32)
        turned = core.sb("f1_weight_turned", [P, 2, 3, P], F32)
        w_in = core.sem("f1_weights_in")
        zeroed = core.sem("zeroed")
        chain = core.sem("f1_weight_step_done")
        turn_done = core.sem("f1_weight_turn_done")
        kept = core.sem("f1_weight_kept")
        hi_ready = core.sem("f1_weight_hi_ready")
        block = stack.enter_context(nc.Block())

        @block.sync
        def _(sp):
            for k, name in enumerate(("w_gate", "w_up")):
                sp.dma_start(raw[k][:, :, :].rearrange("p (j r) i -> p j (r i)", j=3), dram[name].rearrange("(j p) c -> p j c", p=P)).then_inc(w_in, 16)
            sp.dma_start(raw[2][:, :, :].rearrange("p r i -> p (r i)"), dram["w_down"]).then_inc(w_in, 16)
            sp.dma_start(T["ident"][:, :], dram["ident"]).then_inc(w_in, 16)
            q = NB // 4
            for k in range(4):
                sp.dma_start(T["x"][:, k * q:(k + 1) * q, :],
                             dram["x"][k * q:(k + 1) * q].rearrange("b t c -> t b c")).then_inc(x_in[k], 16)

        @block.vector
        def _(dve):
            steps = 0

            def then(instruction):
                nonlocal steps
                instruction.then_inc(chain, 1)
                steps += 1
                dve.wait_ge(chain, steps)
            dve.wait_ge(w_in, 64)
            for k in range(3):
                w = raw[k][:, :, :]
                wide = lambda t: t[:, k, :].unsqueeze(2).to_broadcast([P, 12, 32])
                then(nc.vector.tensor_reduce(step[:, k, :], w, AX.X, ALU.max, apply_absolute_value=True))
                then(nc.vector.tensor_scalar(step[:, k, :], step[:, k, :], 1.0 / 7.0, 1e-12, ALU.mult, ALU.max))
                then(nc.vector.reciprocal(inverse[:, k, :], step[:, k, :]))
                then(nc.vector.tensor_tensor(w, w, wide(inverse), ALU.mult))
                then(nc.vector.tensor_scalar(w, w, ROUND, -ROUND, ALU.add, ALU.add))
                then(nc.vector.tensor_scalar(w, w, 7.0, -8.0, ALU.min, ALU.max))
                then(nc.vector.tensor_tensor(w, w, wide(step), ALU.mult))
            for k in range(2):
                dve.wait_ge(hi_ready, k + 1)
                nc.vector.tensor_tensor(W["gu"][1][:, k, :, :], turned[:, k, :, :], W["gu"][0][:, k, :, :].bitcast(F32), ALU.subtract)

        @block.tensor
        def _(pe):
            for k in range(3):
                pe.wait_ge(chain, 7 * k + 7)
                for j in range(3):
                    mm = pe.transpose(bank[k][:, j * P:(j + 1) * P], raw[k][:, 4 * j:4 * j + 4, :].rearrange("p r i -> p (r i)"), T["ident"][:, :])
                mm.then_inc(turn_done, 1)

        @block.gpsimd
        def _(pool):
            nc.gpsimd.memset(T["bout_row"][:, :], 0.0).then_inc(zeroed, 1)

        @block.scalar
        def _(act):
            act.wait_ge(zeroed, 1)
            for dst, src in weights:
                act.dma_start(dst[tuple(slice(None) for _ in dst.shape)], src).then_inc(others_in, 16)
            for k in range(2):
                act.wait_ge(turn_done, k + 1)
                nc.scalar.copy(turned[:, k, :, :], bank[k][:, 0:384].rearrange("p (j c) -> p j c", j=3)).then_inc(kept, 1)
                act.wait_ge(kept, k + 1)
                nc.scalar.copy(W["gu"][0][:, k, :, :], turned[:, k, :, :]).then_inc(hi_ready, 1)
            act.wait_ge(turn_done, 3)
            nc.scalar.copy(W["down"][:, :, :], bank[2][:, 0:384].rearrange("p (j c) -> p j c", j=3))


def ffn1(nc, dram, T, bank, out):
    NB = T["batches"]
    NG = NB // 4
    with ExitStack() as kept:
        core = Core(nc, kept)
        W = T["ffn1"]
        codes = T["x"][:, 0:NB // 2, :].bitcast(I16).rearrange("p (g b) c -> p g (b c)", b=2)
        spare = T["x"][:, 32:64, :].rearrange("p b c -> p (b c)").rearrange("p (n k c) -> p n k c", n=4, k=2)
        peaks = core.sb("f1_row_peaks", [P, NG, 6], F32)
        scales = {n: (core.sb(f"f1_{n}_step", [P, 1], F32), core.sb(f"f1_{n}_inverse", [P, 1], F32))
                  for n in ("x", "gate", "up", "gated", "o")}
        round_col = core.sb("f1_round", [P, 1], F32)
        row_peaks(nc, T, round_col)
        global_scale(nc, "f1_x", kept, T, [(T["row_max"][:, :, 0], scales["x"][0][:, :], scales["x"][1][:, :])])
        quantise_x(nc, T, W, bank, codes, peaks, scales)
        global_scale(nc, "f1_gu", kept, T, [(peaks[:, :, 0:3], scales["gate"][0][:, :], scales["gate"][1][:, :]),
                                            (peaks[:, :, 3:6], scales["up"][0][:, :], scales["up"][1][:, :])])
        gated = core.sb("f1_gated", [P, NG * 3, 512], F32)
        up = core.sb("f1_up_codes", [P, NG * 3, 512], I16)
        gate_and_up(nc, T, W, bank, codes, spare, peaks, scales, gated, up, round_col)
        global_scale(nc, "f1_gd", kept, T, [(peaks[:, :, 0:3], scales["gated"][0][:, :], scales["gated"][1][:, :])])
        scales["both"] = core.sb("f1_gated_and_up_step", [P, 1], F32)
        with nc.Block() as block:
            @block.vector
            def _(dve):
                nc.vector.tensor_tensor(scales["both"][:, :], scales["gated"][0][:, :], scales["up"][0][:, :], ALU.mult)
        multiply_up(nc, peaks, scales, gated, up, round_col)
        global_scale(nc, "f1_o", kept, T, [(peaks[:, :, 0:3], scales["o"][0][:, :], scales["o"][1][:, :])])
        project(nc, dram, W, bank, scales, gated, spare, round_col, out)


def row_peaks(nc, T, round_col):
    with ExitStack() as stack:
        core = Core(nc, stack)
        step = core.sem("fp_peak_step")
        block = stack.enter_context(nc.Block())

        @block.gpsimd
        def _(pool):
            nc.gpsimd.memset(round_col[:, :], ROUND)

        @block.vector
        def _(dve):
            top, low, mean, rstd = (T[n][:, :, 0] for n in ("row_max", "row_min", "mean", "rstd"))
            nc.vector.tensor_tensor(top, top, mean, ALU.subtract).then_inc(step, 1)
            nc.vector.tensor_tensor(low, mean, low, ALU.subtract).then_inc(step, 1)
            dve.wait_ge(step, 2)
            nc.vector.tensor_tensor(top, top, low, ALU.max).then_inc(step, 1)
            dve.wait_ge(step, 3)
            nc.vector.tensor_tensor(top, top, rstd, ALU.mult).then_inc(step, 1)
            dve.wait_ge(step, 4)


def quantise_x(nc, T, W, bank, codes, peaks, scales):
    NG = codes.shape[1]
    with ExitStack() as stack:
        core = Core(nc, stack)
        xn = core.sb("fq_xn", [P, 2, 4, P], F32)
        c = core.sb("fq_codes", [P, 2, 4, P], F32)
        centred = core.sem("fq_centred")
        normal = core.sem("fq_normal")
        xq = core.sb("fq_x", [P, 2, 512], F32)
        hi = core.sb("fq_x_hi", [P, 2, 512], F32R)
        lo = core.sb("fq_x_lo", [P, 2, 512], F32R)
        scaled = core.sem("fq_scaled")
        rounded = core.sem("fq_rounded")
        turned = core.sem("fq_turned")
        kept = core.sem("fq_codes_kept")
        xq_ready = core.sem("fq_x_ready")
        hi_ready = core.sem("fq_hi_ready")
        lo_ready = core.sem("fq_lo_ready")
        product_done = core.sem("fq_product_done")
        peak_done = core.sem("fq_peak_done")
        TURN, OUT = bank[0:2], bank[2:8]
        step_x, inverse_x = scales["x"]
        block = stack.enter_context(nc.Block())

        @block.vector
        def _(dve):
            def scale_rows(t, p):
                dve.wait_ge(normal, t + 1)
                wait(dve, turned, t - 1)
                nc.vector.tensor_scalar(c[:, p, :, :], xn[:, p, :, :], inverse_x[:, :], ROUND, ALU.mult, ALU.add).then_inc(scaled, 1)

            def round_rows(t, p):
                dve.wait_ge(scaled, t + 1)
                nc.vector.tensor_scalar(c[:, p, :, :], c[:, p, :, :], -ROUND, None, ALU.add).then_inc(rounded, 1)

            def peak(b, j):
                dve.wait_ge(product_done, 6 * b + j + 1)
                nc.vector.tensor_reduce(peaks[:, b, j:j + 1], OUT[j][:, :], AX.X, ALU.max, apply_absolute_value=True).then_inc(peak_done, 1)

            def step(late, b, n, t, p):
                if t is not None:
                    scale_rows(t, p)
                if b is not None:
                    peak(b, 0)
                if t is not None:
                    round_rows(t, p)
                if n is not None:
                    dve.wait_ge(hi_ready, n + 1)
                    if late is not None:
                        wait(dve, product_done, 6 * late + 6)
                    nc.vector.tensor_tensor(lo[:, 1 - p, :], xq[:, 1 - p, :], hi[:, 1 - p, :].bitcast(F32), ALU.subtract).then_inc(lo_ready, 1)
                if b is not None:
                    for j in range(1, 6):
                        peak(b, j)
            scale_rows(0, 0)
            round_rows(0, 0)
            pipelined_deep(dve, NG, step)

        @block.gpsimd
        def _(pool):
            def step(b, n, p):
                if n is None:
                    return
                wait(pool, scaled, n - 1)
                rows, wide = bass.ds(4 * n, 4), [P, 4, P]
                nc.gpsimd.tensor_tensor(xn[:, 1 - p, :, :], T["x"][:, rows, :], T["mean"][:, rows, :].to_broadcast(wide), ALU.subtract).then_inc(centred, 1)
                pool.wait_ge(centred, n + 1)
                nc.gpsimd.tensor_tensor(xn[:, 1 - p, :, :], xn[:, 1 - p, :, :], T["rstd"][:, rows, :].to_broadcast(wide), ALU.mult).then_inc(normal, 1)
            pipelined(pool, NG, step)

        @block.scalar
        def _(act):
            nc.scalar.preload_act_table(ACT.Identity)

            def keep(t, p):
                act.wait_ge(turned, t + 1)
                nc.scalar.copy(codes[:, t, :], TURN[p][:, :]).then_inc(kept, 1)
                wait(act, lo_ready, t - 1)
                nc.scalar.activation(xq[:, p, :], TURN[p][:, :], ACT.Identity, scale=step_x[:, :]).then_inc(xq_ready, 1)

            def step(late, b, n, t, p):
                if n is not None:
                    if late is not None:
                        wait(act, product_done, 6 * late + 6)
                    act.wait_ge(xq_ready, n + 1)
                    nc.scalar.copy(hi[:, 1 - p, :], xq[:, 1 - p, :]).then_inc(hi_ready, 1)
                if t is not None:
                    keep(t, p)
            keep(0, 0)
            pipelined_deep(act, NG, step)

        @block.tensor
        def _(pe):
            def turn(t, p):
                pe.wait_ge(rounded, t + 1)
                wait(pe, xq_ready, t - 1)
                for k in range(4):
                    mm = pe.transpose(TURN[p][:, k * P:(k + 1) * P], c[:, p, k, :], T["ident"][:, :])
                mm.then_inc(turned, 1)

            def product(b, j, p):
                wait(pe, peak_done, 6 * b - 5 + j)
                k, m = divmod(j, 3)
                three_products(pe, OUT[j][:, :], (W["gu"][0][:, k, m, :], W["gu"][1][:, k, m, :]),
                               (hi[:, p, :], lo[:, p, :]), True, True).then_inc(product_done, 1)

            def step(late, b, n, t, p):
                if b is not None:
                    pe.wait_ge(lo_ready, b + 1)
                    for j in range(3):
                        product(b, j, p)
                if t is not None:
                    turn(t, p)
                if b is not None:
                    for j in range(3, 6):
                        product(b, j, p)
            turn(0, 0)
            pipelined_deep(pe, NG, step)


def gate_and_up(nc, T, W, bank, codes, spare, peaks, scales, gated, up, round_col):
    NG = codes.shape[1]
    with ExitStack() as stack:
        core = Core(nc, stack)
        xq = core.sb("fg_x", [P, 512], F32)
        hi = core.sb("fg_x_hi", [P, 2, 512], F32R)
        lo = core.sb("fg_x_lo", [P, 2, 512], F32R)
        spares = spare.rearrange("p n k c -> p (n k) c")
        tg, tu, gate = spares[:, 0:2, :], spares[:, 2:4, :], spares[:, 4:7, :]
        sig = core.sb("fg_sigmoid", [P, 3, 512], F32)
        part = core.sb("fg_gate_step_part", [P, 1], F32)
        part_ready = core.sem("fg_part_ready")
        xq_ready = core.sem("fg_x_ready")
        hi_ready = core.sem("fg_hi_ready")
        lo_ready = core.sem("fg_lo_ready")
        gate_done = core.sem("fg_gate_done")
        up_done = core.sem("fg_up_done")
        tg_ready = core.sem("fg_gate_scaled_ready")
        tu_ready = core.sem("fg_up_scaled_ready")
        gate_ready = core.sem("fg_gate_ready")
        up_ready = core.sem("fg_up_ready")
        sig_ready = core.sem("fg_sigmoid_ready")
        scaled_ready = core.sem("fg_sigmoid_scaled")
        rounded_ready = core.sem("fg_sigmoid_rounded")
        gated_ready = core.sem("fg_gated_ready")
        GATE, UP = bank[0:3], bank[3:6]
        block = stack.enter_context(nc.Block())

        def has_second_next(g):
            return not (isinstance(g, int) and g + 2 >= NG)

        @block.vector
        def _(dve):
            def restore(n):
                wait(dve, lo_ready, n)
                nc.vector.tensor_scalar(xq[:, :], codes[:, n, :], scales["x"][0][:, :], None, ALU.mult).then_inc(xq_ready, 1)

            def gate_of(k, g, m):
                dve.wait_ge(tg_ready, k + 1)
                wait(dve, gated_ready, k - 2)
                nc.vector.tensor_scalar(gate[:, m % 3, :], tg[:, m % 2, :], -ROUND, part[:, :], ALU.add, ALU.mult).then_inc(gate_ready, 1)
                if m % 3 == 1 and has_second_next(g):
                    restore(g + 2)

            def up_codes(k, g, m):
                dve.wait_ge(tu_ready, k + 1)
                nc.vector.tensor_scalar(up[:, k, :], tu[:, m % 2, :], -ROUND, None, ALU.add).then_inc(up_ready, 1)

            def scale(k, g, m):
                dve.wait_ge(sig_ready, k + 1)
                nc.vector.tensor_scalar(sig[:, m % 3, :], sig[:, m % 3, :], 65536.0, ROUND, ALU.mult, ALU.add).then_inc(scaled_ready, 1)

            def rounding(k, g, m):
                dve.wait_ge(scaled_ready, k + 1)
                nc.vector.tensor_scalar(sig[:, m % 3, :], sig[:, m % 3, :], -ROUND, 65535.0, ALU.add, ALU.min).then_inc(rounded_ready, 1)

            def peak(k, g, m):
                dve.wait_ge(gated_ready, k + 1)
                nc.vector.tensor_reduce(peaks[:, g, m % 3:m % 3 + 1], gated[:, k, :], AX.X, ALU.max, apply_absolute_value=True)

            nc.vector.tensor_scalar(part[:, :], scales["gate"][0][:, :], 1.0 / 65536.0, None, ALU.mult).then_inc(part_ready, 1)
            restore(0)
            restore(1)
            dve.wait_ge(part_ready, 1)
            staggered(dve, 3 * NG, [(1, up_codes), (0, gate_of), (1, scale), (3, peak), (1, rounding)])

        @block.gpsimd
        def _(pool):
            def split(n, p):
                pool.wait_ge(hi_ready, n + 1)
                nc.gpsimd.tensor_tensor(lo[:, p, :], xq[:, :], hi[:, p, :].bitcast(F32), ALU.subtract).then_inc(lo_ready, 1)

            def multiply(k, g, m):
                if m % 3 == 2 and has_second_next(g):
                    split(g + 2, m // 3)
                pool.wait_ge(rounded_ready, k + 1)
                nc.gpsimd.tensor_tensor(gated[:, k, :], sig[:, m % 3, :], gate[:, m % 3, :], ALU.mult).then_inc(gated_ready, 1)
            split(0, 0)
            split(1, 1)
            staggered(pool, 3 * NG, [(0, multiply)])

        @block.scalar
        def _(act):
            nc.scalar.preload_act_table(ACT.Sigmoid)

            def split(n, p):
                act.wait_ge(xq_ready, n + 1)
                wait(act, up_done, 3 * (n - 1))
                nc.scalar.copy(hi[:, p, :], xq[:, :]).then_inc(hi_ready, 1)

            def scaled_gate(k, g, m):
                act.wait_ge(gate_done, k + 1)
                wait(act, gate_ready, k - 1)
                nc.scalar.activation(tg[:, m % 2, :], GATE[m % 3][:, :], ACT.Identity, bias=round_col[:, :], scale=scales["gate"][1][:, :]).then_inc(tg_ready, 1)

            def scaled_up(k, g, m):
                act.wait_ge(up_done, k + 1)
                wait(act, up_ready, k - 1)
                nc.scalar.activation(tu[:, m % 2, :], UP[m % 3][:, :], ACT.Identity, bias=round_col[:, :], scale=scales["up"][1][:, :]).then_inc(tu_ready, 1)
                if m % 3 == 2 and has_second_next(g):
                    split(g + 2, m // 3)

            def sigmoid(k, g, m):
                act.wait_ge(gate_ready, k + 1)
                wait(act, gated_ready, k - 2)
                nc.scalar.activation(sig[:, m % 3, :], gate[:, m % 3, :], ACT.Sigmoid, scale=65536.0).then_inc(sig_ready, 1)

            split(0, 0)
            split(1, 1)
            staggered(act, 3 * NG, [(0, scaled_gate), (1, sigmoid), (0, scaled_up)])

        @block.tensor
        def _(pe):
            def products(k, g, m):
                if m % 3 == 0:
                    pe.wait_ge(lo_ready, g + 1)
                j = m % 3
                x_parts = (hi[:, m // 3, :], lo[:, m // 3, :])
                wait(pe, tg_ready, k - 2)
                three_products(pe, GATE[j][:, :], (W["gu"][0][:, 0, j, :], W["gu"][1][:, 0, j, :]), x_parts, True, True).then_inc(gate_done, 1)
                wait(pe, tu_ready, k - 2)
                three_products(pe, UP[j][:, :], (W["gu"][0][:, 1, j, :], W["gu"][1][:, 1, j, :]), x_parts, True, True).then_inc(up_done, 1)
            staggered(pe, 3 * NG, [(0, products)])


def multiply_up(nc, peaks, scales, gated, up, round_col):
    NK = gated.shape[1]
    with ExitStack() as stack:
        core = Core(nc, stack)
        t = core.sb("fm_scaled", [P, 3, 512], F32)
        q = core.sb("fm_gated_codes", [P, 2, 512], F32)
        minus = core.sb("fm_minus_round", [P, 1], F32)
        minus_ready = core.sem("fm_minus_round_ready")
        t_ready = core.sem("fm_scaled_ready")
        q_ready = core.sem("fm_codes_ready")
        o_ready = core.sem("fm_o_ready")
        block = stack.enter_context(nc.Block())

        @block.scalar
        def _(act):
            nc.scalar.preload_act_table(ACT.Identity)
            def scaled(k, g, m):
                wait(act, q_ready, k - 2)
                nc.scalar.activation(t[:, m % 3, :], gated[:, k, :], ACT.Identity, bias=round_col[:, :], scale=scales["gated"][1][:, :]).then_inc(t_ready, 1)

            def rounded(k, g, m):
                act.wait_ge(t_ready, k + 1)
                wait(act, o_ready, k - 1)
                nc.scalar.activation(q[:, m % 2, :], t[:, m % 3, :], ACT.Identity, bias=minus[:, :]).then_inc(q_ready, 1)

            act.wait_ge(minus_ready, 1)
            staggered(act, NK, [(0, scaled), (1, rounded)])

        @block.gpsimd
        def _(pool):
            nc.gpsimd.memset(minus[:, :], -ROUND).then_inc(minus_ready, 1)

        @block.vector
        def _(dve):
            def multiply(k, g, m):
                dve.wait_ge(q_ready, k + 1)
                nc.vector.scalar_tensor_tensor(gated[:, k, :], up[:, k, :], scales["both"][:, :], q[:, m % 2, :], ALU.mult, ALU.mult).then_inc(o_ready, 1)

            def peak(k, g, m):
                dve.wait_ge(o_ready, k + 1)
                nc.vector.tensor_reduce(peaks[:, g, m % 3:m % 3 + 1], gated[:, k, :], AX.X, ALU.max, apply_absolute_value=True)

            staggered(dve, NK, [(0, multiply), (1, peak)])


def project(nc, dram, W, bank, scales, o, spare, round_col, out):
    NG = o.shape[1] // 3
    with ExitStack() as stack:
        core = Core(nc, stack)
        t = core.sb("fp_scaled", [P, 3, 512], F32)
        q = core.sb("fp_o", [P, 2, 3, 512], F32)
        y, x = (spare[:, k, :, :].rearrange("p k (b c) -> p k b c", b=4) for k in range(2))
        t_ready = core.sem("fp_scaled_ready")
        q_ready = core.sem("fp_o_ready")
        y_done = core.sem("fp_y_done")
        sum_ready = core.sem("fp_sum_ready")
        stored = [core.sem(f"fp_stored{k}") for k in range(2)]
        x_in = [core.sem(f"fp_x_in{k}") for k in range(2)]
        Y = bank[0:2]
        block = stack.enter_context(nc.Block())

        @block.scalar
        def _(act):
            nc.scalar.preload_act_table(ACT.Identity)
            def scaled(k, g, m):
                wait(act, q_ready, k - 2)
                nc.scalar.activation(t[:, m % 3, :], o[:, k, :], ACT.Identity, bias=round_col[:, :], scale=scales["o"][1][:, :]).then_inc(t_ready, 1)
            staggered(act, 3 * NG, [(0, scaled)])

        @block.vector
        def _(dve):
            def quantised(n, p):
                wait(dve, y_done, n - 1)
                for j in range(3):
                    dve.wait_ge(t_ready, 3 * n + j + 1)
                    nc.vector.tensor_scalar(q[:, p, j, :], t[:, j, :], -ROUND, scales["o"][0][:, :], ALU.add, ALU.mult).then_inc(q_ready, 1)

            def add(b, p):
                turn = 8 * (b - p)
                dve.wait_ge(y_done, b + 1)
                wait(dve, stored[p], turn)
                dve.wait_ge(x_in[p], turn + 16)
                nc.vector.tensor_tensor(y[:, p, :, :], Y[p][:, :].rearrange("p (k c) -> p k c", k=4), x[:, p, :, :], ALU.add).then_inc(sum_ready, 1)

            def step(b, n, p):
                if n is not None:
                    quantised(n, 1 - p)
                if b is not None:
                    add(b, p)
            pipelined(dve, NG, step)

        @block.tensor
        def _(pe):
            def step(b, n, p):
                if b is None:
                    return
                pe.wait_ge(q_ready, 3 * b + 3)
                wait(pe, sum_ready, b - 1)
                for k in range(4):
                    for j in range(3):
                        mm = pe.matmul(Y[p][:, k * P:(k + 1) * P], q[:, p, j, k * P:(k + 1) * P], W["down"][:, j, :],
                                       start=(j == 0), stop=(j == 2))
                mm.then_inc(y_done, 1)
            pipelined(pe, NG, step)

        @block.sync
        def _(sp):
            rows = lambda t, g: t[bass.ds(4 * g, 4)].rearrange("b t c -> t b c")

            def load(g, p):
                sp.dma_start(x[:, p, :, :], rows(dram["x_parked"], g)).then_inc(x_in[p], 16)

            def store(g, p):
                sp.wait_ge(sum_ready, g + 1)
                sp.dma_start(rows(out, g), y[:, p, :, :]).then_inc(stored[p], 16)

            load(0, 0)
            load(1, 1)
            if NG > 2:
                with sp.Fori(0, NG // 2 - 1) as i:
                    for p in range(2):
                        store(2 * i + p, p)
                        load(2 * i + 2 + p, p)
            store(NG - 2, 0)
            store(NG - 1, 1)
            for p in range(2):
                sp.wait_ge(stored[p], 16 * (NG // 2))


def build(nc, dram, out, stop_after=9):
    NB = dram["x"].shape[0]
    with ExitStack() as top:
        core = Core(nc, top)
        bank = [top.enter_context(nc.psum_tensor(f"bank{k}", [P, 512], F32)) for k in range(8)]
        T = {
            "batches": NB,
            "x": core.sb("x", [P, max(NB, 64), P], F32),
            "ident": core.sb("ident", [P, P], F32),
            "identb": core.sb("identb", [P, P], BF16),
            "x_stats": core.sb("x_stats", [P, NB, 6], F32),
            "ctx_stats": core.sb("ctx_stats", [P, NB, 6], F32),
            "mean": core.sb("x_mean", [P, NB, 1], F32),
            "ctx_mean": core.sb("ctx_mean", [P, NB, 1], F32),
            "rstd": core.sb("x_rstd", [P, NB, 1], F32),
            "ctx_rstd": core.sb("ctx_rstd", [P, NB, 1], F32),
            "row_max": core.sb("x_row_max", [P, NB, 1], F32),
            "row_min": core.sb("x_row_min", [P, NB, 1], F32),
            "ffn1": {"gu": (core.sb("f1_gate_up_hi", [P, 2, 3, P], F32R), core.sb("f1_gate_up_lo", [P, 2, 3, P], F32R)),
                     "down": core.sb("f1_down", [P, 3, P], F32)},
        }
        with ExitStack() as mid:
            core = Core(nc, mid)
            T.update({
                "headmask": core.sb("headmask", [P, 4], F32),
                "groupmask": core.sb("groupmask", [P, 4], F32),
                "tri": core.sb("tri", [P, 4, 4], F32),
                "blockstart": core.sb("blockstart", [P, 1024], F32),
                "expert_rows": core.sb("expert_rows", [48, 4, P], F32),
                "onerow": core.sb("onerow", [P, 16, P], BF16),
                "onerow_f": core.sb("onerow_f", [P, P], F32),
                "wv": (core.sb("wv_hi", [P, 1024], F32R), core.sb("wv_lo", [P, 1024], F32R)),
                "gate_up": (core.sb("gate_up_hi", [P, 2, 6, P], F32R), core.sb("gate_up_lo", [P, 2, 6, P], F32R)),
                "down": core.sb("down", [P, 6, P], F32),
                "router": core.sb("router", [P, 16], F32),
                "router_bias": core.sb("router_bias", [P, 16], F32),
                "w_out0": core.sb("w_out0", [P, P], F32),
                "bout_row": core.sb("bout_row", [P, P], F32),
                "w_out1": core.sb("w_out1", [P, 8, P], F32),
                "ln_cols": core.sb("ln_cols", [P, 4], F32),
                "m": core.sb("wq_wk", [P, 16, P], F32),
            })
            load_and_prepare(nc, dram, T, bank)
            x_rows = (T["x_stats"], T["mean"], T["rstd"], P)
            ctx_rows = (T["ctx_stats"], T["ctx_mean"], T["ctx_rstd"], 77)
            row_scales(nc, "rows0", [x_rows + (False,)])
            if stop_after >= 1:
                attention0(nc, dram, T, bank)
            if stop_after >= 2:
                row_scales(nc, "rows1", [x_rows + (False,)])
                ffn0(nc, T, bank)
            if stop_after >= 3:
                row_scales(nc, "rows2", [x_rows + (True,), ctx_rows + (False,)])
                attention1(nc, dram, T, bank)
        if stop_after >= 4:
            row_scales(nc, "rows3", [x_rows + (False,)])
            ffn1(nc, dram, T, bank, out)
            return
        with ExitStack() as s:
            done = s.enter_context(nc.semaphore("dump"))
            blk = s.enter_context(nc.Block())

            @blk.sync
            def _(sp):
                sp.dma_start(out.rearrange("b t c -> t b c"), T["x"][:, 0:NB, :]).then_inc(done, 16)
                sp.wait_ge(done, 16)


def kernel(**inputs):
    import numpy as _np
    import concourse.bacc as _bacc
    from concourse import mybir as _mybir
    from concourse.bass_utils import run_bass_kernel_spmd as _run

    a = {k: _np.asarray(v) for k, v in inputs.items()}
    nb = a["x"].shape[0]
    rows = _np.arange(128)
    tri = _np.tril(_np.ones((4, 4), _np.float32), -1)
    start = (_np.arange(1024) % 16 != 0).astype(_np.float32)
    by_c = lambda w: w.transpose(1, 0, 2).reshape(128, 512)
    arrays = {
        "x": a["x"], "ctx": a["ctx_1024"], "mask": a["mask_Bx1xSxS2_ik1"].reshape(nb, 128, 77),
        "w_out0": a["L0_xattn_w_out"].T, "b_out0": a["L0_xattn_b_out"],
        "router": a["L0_ffn_router_w"].T, "router_bias": a["L0_ffn_correction_bias"],
        "gate_up": _np.concatenate([a["L0_ffn_shared_gate_w"].T, by_c(a["L0_ffn_gate_w"]),
                                    a["L0_ffn_shared_up_w"].T, by_c(a["L0_ffn_up_w"])], axis=1),
        "down": _np.concatenate([a["L0_ffn_shared_down_w"].T, a["L0_ffn_down_w"].reshape(512, 128)], axis=0),
        "ln_cols": _np.stack([a["L1_xattn_ln_l_g"], a["L1_xattn_ln_l_b"], a["L1_xattn_ln_m_g"], a["L1_xattn_ln_m_b"]], axis=1),
        "wq": a["L1_xattn_Wq"].T, "wk": a["L1_xattn_Wkv"][:, :1024].T, "wv": a["L1_xattn_Wkv"][:, 1024:],
        "w_out1": a["L1_xattn_Wout"],
        "w_gate": a["L1_ffn_w_gate"], "w_up": a["L1_ffn_w_up"], "w_down": a["L1_ffn_w_down"],
        "ident": _np.eye(128, dtype=_np.float32),
        "headmask": (rows[:, None] // 8 % 4 == _np.arange(4)[None, :]).astype(_np.float32),
        "groupmask": (rows[:, None] // 32 == _np.arange(4)[None, :]).astype(_np.float32),
        "tri": _np.ascontiguousarray(_np.broadcast_to(tri, (128, 4, 4))),
        "blockstart": _np.ascontiguousarray(_np.broadcast_to(start, (128, 1024))),
        "expert_rows": _np.stack([(_np.arange(48)[:, None] % 32 == 4 * j + rows[None, :] // 32) for j in range(4)], axis=1).astype(_np.float32),
    }
    arrays = {k: _np.ascontiguousarray(v) for k, v in arrays.items()}
    nc = _bacc.Bacc("TRN2", target_bir_lowering=False, num_devices=1)
    dram = {k: nc.dram_tensor(f"in_{k}", v.shape, _mybir.dt.from_np(v.dtype), kind="ExternalInput").ap() for k, v in arrays.items()}
    out = nc.dram_tensor("out_x", (nb, 128, 128), _mybir.dt.from_np(_np.dtype("float32")), kind="ExternalOutput").ap()
    dram["x_parked"] = nc.dram_tensor("x_parked", (nb, 128, 128), _mybir.dt.float32, kind="Internal").ap()
    build(nc, dram, out)
    r = _run(nc, [{f"in_{k}": v for k, v in arrays.items()}], core_ids=[0])
    return r.results[0]["out_x"]
```
